# Optimizing a Trainium2 kernel written in Bass

```python
import numpy as np
import jax
import jax.numpy as jnp

def _softmax(x, axis=-1):
    return jax.nn.softmax(x, axis=axis)

def _gelu(x):
    return jax.nn.gelu(x, approximate=True)

def _silu(x):
    return jax.nn.silu(x)

def _sigmoid(x):
    return jax.nn.sigmoid(x)

def _layernorm(x, axis=-1, eps=1e-05):
    m = jnp.mean(x, axis=axis, keepdims=True)
    v = jnp.var(x, axis=axis, keepdims=True)
    return (x - m) / jnp.sqrt(v + eps)

def _scatter_add(tgt, idx, src, axis=0):
    return tgt.at[idx].add(src)

def _segment_sum(src, seg, n):
    return jax.ops.segment_sum(src, seg, n)
kernel_name = 'mk_gps_d4_gnn_r32_4ba3d9'

def setup_inputs(seed: int=0):
    np.random.seed(seed)
    _w = jnp.asarray

    def _rec_inputs():
        import jax
        import jax.numpy as jnp
        _gk = jax.random.key(seed)
        x = -0.0003713 + 1 * jax.random.normal(jax.random.fold_in(_gk, 1), (3125, 256), jnp.float32)
        src = jax.random.randint(jax.random.fold_in(_gk, 2), (50000,), 0, 3125, jnp.int32)
        dst = jnp.minimum((3125 * jax.random.uniform(jax.random.fold_in(_gk, 3), (50000,)) ** 2.0).astype(jnp.int32), 99999)
        _o = jnp.argsort(dst, stable=True)
        src = src[_o]
        dst = dst[_o]
        edge_attr_128 = -5.16925e-05 + 1.00005 * jax.random.normal(jax.random.fold_in(_gk, 12), (50000, 128), jnp.float32)
        edge_type_2 = jax.random.randint(jax.random.fold_in(_gk, 14), (50000,), 0, 2, jnp.int32)
        return (x, src, dst, edge_attr_128, edge_type_2)
    x, src, dst, edge_attr_128, edge_type_2 = _rec_inputs()

    def _L0_gnn_setup():
        import jax, jax.numpy as jnp
        import numpy as np
        N = 50000
        E = 25000
        IN_C = 256
        HID = 64
        HEADS = 4
        NEG_SLOPE = 0.2

        def _gat_conv(x, W, att_src, att_dst, b, src, dst):
            n = x.shape[0]
            h = (x @ W).reshape(n, HEADS, HID)
            a_s = jnp.einsum('nhc,hc->nh', h, att_src)
            a_d = jnp.einsum('nhc,hc->nh', h, att_dst)
            e = jax.nn.leaky_relu(a_s[src] + a_d[dst], NEG_SLOPE)
            m = jax.ops.segment_max(e, dst, num_segments=n)
            ex = jnp.exp(e - m[dst])
            denom = jax.ops.segment_sum(ex, dst, num_segments=n)
            alpha = ex / denom[dst]
            msg = h[src] * alpha[:, :, None]
            out = jax.ops.segment_sum(msg, dst, num_segments=n)
            return out.reshape(n, HEADS * HID) + b
        key = jax.random.key(seed)
        ks = jax.random.split(key, 12)
        x = jax.random.normal(ks[0], (N, IN_C), dtype=jnp.float32)
        edge_index = jax.random.randint(ks[1], (2, E), 0, N, dtype=jnp.int64)
        s1 = 1.0 / np.sqrt(IN_C)
        W1 = jax.random.normal(ks[2], (IN_C, HEADS * HID), dtype=jnp.float32) * s1
        att_src1 = jax.random.normal(ks[3], (HEADS, HID), dtype=jnp.float32) * 0.1
        att_dst1 = jax.random.normal(ks[4], (HEADS, HID), dtype=jnp.float32) * 0.1
        b1 = jnp.zeros((HEADS * HID,), dtype=jnp.float32)
        s2 = 1.0 / np.sqrt(HEADS * HID)
        W2 = jax.random.normal(ks[5], (HEADS * HID, HEADS * HID), dtype=jnp.float32) * s2
        att_src2 = jax.random.normal(ks[6], (HEADS, HID), dtype=jnp.float32) * 0.1
        att_dst2 = jax.random.normal(ks[7], (HEADS, HID), dtype=jnp.float32) * 0.1
        b2 = jnp.zeros((HEADS * HID,), dtype=jnp.float32)
        return {'x': x, 'edge_index': edge_index, 'W1': W1, 'att_src1': att_src1, 'att_dst1': att_dst1, 'b1': b1, 'W2': W2, 'att_src2': att_src2, 'att_dst2': att_dst2, 'b2': b2}
    _L0_gnn_all = _L0_gnn_setup()
    _L0_gnn_in = {k: v for k, v in _L0_gnn_all.items() if k in ('W1', 'att_src1', 'att_dst1', 'b1', 'W2', 'att_src2', 'att_dst2', 'b2')}
    del _L0_gnn_all

    def _L0_mix_setup():
        import jax, jax.numpy as jnp
        import numpy as np
        B, L, D, H = (4, 512, 256, 8)
        DK = D // H

        def _heads(t):
            b, l, d = t.shape
            return t.reshape(b, l, H, DK).transpose(0, 2, 1, 3)
        key = jax.random.key(seed)
        ks = jax.random.split(key, 9)
        s = 0.02
        return {'x': jax.random.normal(ks[0], (B, L, D), dtype=jnp.float32), 'Wq': jax.random.normal(ks[1], (D, D), dtype=jnp.float32) * s, 'bq': jnp.zeros((D,), dtype=jnp.float32), 'Wk': jax.random.normal(ks[2], (D, D), dtype=jnp.float32) * s, 'bk': jnp.zeros((D,), dtype=jnp.float32), 'Wv': jax.random.normal(ks[3], (D, D), dtype=jnp.float32) * s, 'bv': jnp.zeros((D,), dtype=jnp.float32), 'Wfc': jax.random.normal(ks[4], (D, D), dtype=jnp.float32) * s, 'bfc': jnp.zeros((D,), dtype=jnp.float32)}
    _L0_mix_all = _L0_mix_setup()
    _L0_mix_in = {k: v for k, v in _L0_mix_all.items() if k in ('Wq', 'bq', 'Wk', 'bk', 'Wv', 'bv', 'Wfc', 'bfc')}
    del _L0_mix_all

    def _L0_ffn_setup():
        import jax, jax.numpy as jnp
        import numpy as np
        B, T, D, H, E = (16, 128, 256, 512, 8)
        key = jax.random.key(seed)
        ks = jax.random.split(key, 5)
        x = jax.random.normal(ks[0], (B, T, D), dtype=jnp.float32)
        gate_w = jax.random.normal(ks[1], (D, E), dtype=jnp.float32) * 0.02
        gate_b = jnp.zeros((E,), dtype=jnp.float32)
        W1 = jax.random.normal(ks[2], (E, D, H), dtype=jnp.float32) * 0.02
        b1 = jnp.zeros((E, H), dtype=jnp.float32)
        W2 = jax.random.normal(ks[3], (E, H, D), dtype=jnp.float32) * 0.02
        b2 = jnp.zeros((E, D), dtype=jnp.float32)
        return {'x': x, 'gate_w': gate_w, 'gate_b': gate_b, 'W1': W1, 'b1': b1, 'W2': W2, 'b2': b2}
    _L0_ffn_all = _L0_ffn_setup()
    _L0_ffn_in = {k: v for k, v in _L0_ffn_all.items() if k in ('gate_w', 'gate_b', 'W1', 'b1', 'W2', 'b2')}
    del _L0_ffn_all

    def _L1_gnn_setup():
        import jax, jax.numpy as jnp
        import numpy as np
        N_NODES = 50000
        N_EDGES = 25000
        DIM = 256
        key = jax.random.key(seed)
        k1, k2, k3, k4, k5 = jax.random.split(key, 5)
        x = jax.random.normal(k1, (N_NODES, DIM), dtype=jnp.float32)
        edge_index = jax.random.randint(k2, (2, N_EDGES), 0, N_NODES, dtype=jnp.int64)
        W1 = jax.random.normal(k3, (DIM, DIM), dtype=jnp.float32) / np.sqrt(DIM)
        W2 = jax.random.normal(k4, (DIM, DIM), dtype=jnp.float32) / np.sqrt(DIM)
        return {'x': x, 'edge_index': edge_index, 'W1': W1, 'W2': W2}
    _L1_gnn_all = _L1_gnn_setup()
    _L1_gnn_in = {k: v for k, v in _L1_gnn_all.items() if k in ('W1', 'W2')}
    del _L1_gnn_all

    def _L1_mix_setup():
        import jax, jax.numpy as jnp
        import numpy as np
        MIDC = 256
        HEADS = 8
        HEADC = MIDC // HEADS
        EPS = 1e-05

        def _ln(x, gamma, beta):
            mu = jnp.mean(x, axis=-1, keepdims=True)
            var = jnp.var(x, axis=-1, keepdims=True)
            return (x - mu) * jax.lax.rsqrt(var + EPS) * gamma + beta
        key = jax.random.key(seed)
        ks = jax.random.split(key, 8)
        B, HW, C = (8, 128, MIDC)
        s = 1.0 / np.sqrt(C)
        return {'x': jax.random.normal(ks[0], (B, HW, C), jnp.float32), 'w_qkv': jax.random.normal(ks[1], (C, 3 * C), jnp.float32) * s, 'b_qkv': jnp.zeros((3 * C,), jnp.float32), 'kln_g': jnp.ones((HEADC,), jnp.float32), 'kln_b': jnp.zeros((HEADC,), jnp.float32), 'vln_g': jnp.ones((HEADC,), jnp.float32), 'vln_b': jnp.zeros((HEADC,), jnp.float32), 'w1': jax.random.normal(ks[2], (C, C), jnp.float32) * s, 'b1': jnp.zeros((C,), jnp.float32), 'w2': jax.random.normal(ks[3], (C, C), jnp.float32) * s, 'b2': jnp.zeros((C,), jnp.float32)}
    _L1_mix_all = _L1_mix_setup()
    _L1_mix_in = {k: v for k, v in _L1_mix_all.items() if k in ('w_qkv', 'b_qkv', 'kln_g', 'kln_b', 'vln_g', 'vln_b', 'w1', 'b1', 'w2', 'b2')}
    del _L1_mix_all

    def _L1_ffn_setup():
        import math
        import jax, jax.numpy as jnp
        import numpy as np
        CAPACITY_FACTOR = 1.25
        key = jax.random.key(seed)
        ks = jax.random.split(key, 5)
        B, L, D, F, E = (8, 256, 256, 1024, 8)
        h = jax.random.normal(ks[0], (B, L, D), dtype=jnp.float32)
        gate_w = jax.random.normal(ks[1], (D, E), dtype=jnp.float32) * 0.02
        gate_b = jnp.zeros((E,), dtype=jnp.float32)
        w1 = jax.random.normal(ks[2], (E, D, F), dtype=jnp.float32) * (1.0 / math.sqrt(D))
        b1 = jnp.zeros((E, F), dtype=jnp.float32)
        w2 = jax.random.normal(ks[3], (E, F, D), dtype=jnp.float32) * (1.0 / math.sqrt(F))
        b2 = jnp.zeros((E, D), dtype=jnp.float32)
        return {'h': h, 'gate_w': gate_w, 'gate_b': gate_b, 'w1': w1, 'b1': b1, 'w2': w2, 'b2': b2}
    _L1_ffn_all = _L1_ffn_setup()
    _L1_ffn_in = {k: v for k, v in _L1_ffn_all.items() if k in ('gate_w', 'gate_b', 'w1', 'b1', 'w2', 'b2')}
    del _L1_ffn_all

    def _L2_gnn_setup():
        import jax, jax.numpy as jnp
        import numpy as np
        N_NODES = 50000
        N_EDGES = 25000
        IN_DIM = 256
        OUT_DIM = 256
        HEADS = 1
        EDGE_DIM = 128
        NEG_SLOPE = 0.01
        key = jax.random.key(seed)
        ks = jax.random.split(key, 8)
        x = jax.random.normal(ks[0], (N_NODES, IN_DIM), dtype=jnp.float32)
        edge_index = jax.random.randint(ks[1], (2, N_EDGES), 0, N_NODES, dtype=jnp.int64)
        edge_attr = jax.random.normal(ks[2], (N_EDGES, EDGE_DIM), dtype=jnp.float32)
        hc = HEADS * OUT_DIM
        Wn = jax.random.normal(ks[3], (hc, IN_DIM), dtype=jnp.float32) / np.sqrt(IN_DIM)
        bn = jnp.zeros((hc,), dtype=jnp.float32)
        We = jax.random.normal(ks[4], (hc, EDGE_DIM), dtype=jnp.float32) / np.sqrt(EDGE_DIM)
        be = jnp.zeros((hc,), dtype=jnp.float32)
        attn = jax.random.normal(ks[5], (1, HEADS, OUT_DIM), dtype=jnp.float32) * np.sqrt(2.0 / (HEADS * OUT_DIM + 1))
        return {'x': x, 'edge_index': edge_index, 'edge_attr': edge_attr, 'Wn': Wn, 'bn': bn, 'We': We, 'be': be, 'attn': attn}
    _L2_gnn_all = _L2_gnn_setup()
    _L2_gnn_in = {k: v for k, v in _L2_gnn_all.items() if k in ('Wn', 'bn', 'We', 'be', 'attn')}
    del _L2_gnn_all

    def _L2_mix_setup():
        import jax, jax.numpy as jnp
        import numpy as np
        HEADS = 4
        DIM_HEAD = 32
        key = jax.random.key(seed)
        k1, k2, k3 = jax.random.split(key, 3)
        B, L, D = (16, 256, 256)
        hidden = HEADS * DIM_HEAD
        x = jax.random.normal(k1, (B, L, D), dtype=jnp.float32)
        W_qkv = jax.random.normal(k2, (D, 3 * hidden), dtype=jnp.float32) * D ** (-0.5)
        W_out = jax.random.normal(k3, (hidden, D), dtype=jnp.float32) * hidden ** (-0.5)
        b_out = jnp.zeros((D,), dtype=jnp.float32)
        return {'x': x, 'W_qkv': W_qkv, 'W_out': W_out, 'b_out': b_out}
    _L2_mix_all = _L2_mix_setup()
    _L2_mix_in = {k: v for k, v in _L2_mix_all.items() if k in ('W_qkv', 'W_out', 'b_out')}
    del _L2_mix_all

    def _L2_ffn_setup():
        import jax, jax.numpy as jnp
        import numpy as np
        B, S, H, F, E, K = (8, 128, 256, 512, 16, 2)
        EPS = 1e-05
        key = jax.random.key(seed)
        ks = jax.random.split(key, 9)
        sc = 0.02
        return {'x': jax.random.normal(ks[0], (B, S, H), dtype=jnp.float32), 'gate_w': jax.random.normal(ks[1], (H, E), dtype=jnp.float32) * sc, 'gate_b': jnp.zeros((E,), dtype=jnp.float32), 'w1': jax.random.normal(ks[2], (E, H, F), dtype=jnp.float32) * sc, 'b1': jnp.zeros((E, F), dtype=jnp.float32), 'w2': jax.random.normal(ks[3], (E, F, H), dtype=jnp.float32) * sc, 'b2': jnp.zeros((E, H), dtype=jnp.float32), 'gamma': jnp.ones((H,), dtype=jnp.float32), 'beta': jnp.zeros((H,), dtype=jnp.float32)}
    _L2_ffn_all = _L2_ffn_setup()
    _L2_ffn_in = {k: v for k, v in _L2_ffn_all.items() if k in ('gate_w', 'gate_b', 'w1', 'b1', 'w2', 'b2', 'gamma', 'beta')}
    del _L2_ffn_all

    def _L3_gnn_setup():
        import jax, jax.numpy as jnp
        import numpy as np
        N, E = (625, 10000)
        IN_DIM, H, D = (256, 32, 8)
        NUM_ETYPES, L = (2, 2)

        def _hgt_layer(x, Wk, Wq, Wv, Wa, Watt, Wmsg, pri, skip, src, dst, etype):
            n = x.shape[0]
            k = (x @ Wk).reshape(n, H, D)
            q = (x @ Wq).reshape(n, H, D)
            v = (x @ Wv).reshape(n, H, D)
            k_e, q_e, v_e = (k[src], q[dst], v[src])
            is0 = (etype == 0)[:, None, None]
            kw = jnp.where(is0, jnp.einsum('ehd,hdf->ehf', k_e, Watt[:, 0]), jnp.einsum('ehd,hdf->ehf', k_e, Watt[:, 1]))
            m = jnp.where(is0, jnp.einsum('ehd,hdf->ehf', v_e, Wmsg[:, 0]), jnp.einsum('ehd,hdf->ehf', v_e, Wmsg[:, 1]))
            a = (kw * q_e).sum(-1) * pri[:, etype].T / np.float32(np.sqrt(D))
            amax = jax.ops.segment_max(a, dst, num_segments=n)
            ea = jnp.exp(a - amax[dst])
            att = ea / jax.ops.segment_sum(ea, dst, num_segments=n)[dst]
            h = jax.ops.segment_sum(m * att[:, :, None], dst, num_segments=n).reshape(n, H * D)
            h = h @ Wa
            alpha = jax.nn.sigmoid(skip)
            return h * alpha + x * (1.0 - alpha)
        key = jax.random.key(seed)
        ks = jax.random.split(key, 12)
        HD = H * D
        s = 0.02
        return {'x': jax.random.normal(ks[0], (N, IN_DIM), jnp.float32), 'Wk': jax.random.normal(ks[1], (L, IN_DIM, HD), jnp.float32) * s, 'Wq': jax.random.normal(ks[2], (L, IN_DIM, HD), jnp.float32) * s, 'Wv': jax.random.normal(ks[3], (L, IN_DIM, HD), jnp.float32) * s, 'Wa': jax.random.normal(ks[4], (L, HD, HD), jnp.float32) * s, 'Watt': jax.random.normal(ks[5], (L, H, NUM_ETYPES, D, D), jnp.float32) * s, 'Wmsg': jax.random.normal(ks[6], (L, H, NUM_ETYPES, D, D), jnp.float32) * s, 'pri': jnp.ones((L, H, NUM_ETYPES), jnp.float32), 'skip': jnp.ones((L,), jnp.float32), 'src': jax.random.randint(ks[7], (E,), 0, N), 'dst': jax.random.randint(ks[8], (E,), 0, N), 'etype': jax.random.randint(ks[9], (E,), 0, NUM_ETYPES)}
    _L3_gnn_all = _L3_gnn_setup()
    _L3_gnn_in = {k: v for k, v in _L3_gnn_all.items() if k in ('Wk', 'Wq', 'Wv', 'Wa', 'Watt', 'Wmsg', 'pri', 'skip')}
    del _L3_gnn_all

    def _L3_mix_setup():
        import jax, jax.numpy as jnp
        import numpy as np
        HEADS, DIM_HEAD = (8, 64)
        EPS = 1e-05

        def instance_norm(t):
            mu = jnp.mean(t, axis=-1, keepdims=True)
            var = jnp.mean((t - mu) ** 2, axis=-1, keepdims=True)
            return (t - mu) * jax.lax.rsqrt(var + EPS)
        key = jax.random.key(seed)
        k1, k2, k3, k4 = jax.random.split(key, 4)
        B, N, D = (8, 256, 256)
        inner = HEADS * DIM_HEAD
        x = jax.random.normal(k1, (B, N, D), jnp.float32)
        w_qkv = jax.random.normal(k2, (3 * inner, D), jnp.float32) / np.sqrt(D).astype(np.float32)
        w_out = jax.random.normal(k3, (D, inner), jnp.float32) / np.sqrt(inner).astype(np.float32)
        b_out = 0.01 * jax.random.normal(k4, (D,), jnp.float32)
        return {'x': x, 'w_qkv': w_qkv, 'w_out': w_out, 'b_out': b_out}
    _L3_mix_all = _L3_mix_setup()
    _L3_mix_in = {k: v for k, v in _L3_mix_all.items() if k in ('w_qkv', 'w_out', 'b_out')}
    del _L3_mix_all

    def _L3_ffn_setup():
        import jax, jax.numpy as jnp
        import numpy as np
        NUM_EXPERTS = 8
        TOP_K = 2
        B, S, D = (8, 256, 256)

        def _moe(tokens, router_w, w1, b1, w2, b2):
            N = tokens.shape[0]
            E = router_w.shape[0]
            logits = tokens.astype(jnp.float32) @ router_w.astype(jnp.float32).T
            probs = jax.nn.softmax(logits, axis=-1)
            rw, re = jax.lax.top_k(probs, TOP_K)
            if TOP_K > 1:
                rw = rw / jnp.maximum(rw.sum(-1, keepdims=True), 1e-12)
            rw = rw.astype(tokens.dtype)
            combine = jnp.zeros((N, E), tokens.dtype).at[jnp.arange(N)[:, None], re].set(rw)
            out = tokens
            for e in range(E):
                h = jax.nn.gelu(tokens @ w1[e] + b1[e], approximate=False)
                y = h @ w2[e] + b2[e]
                out = out + combine[:, e:e + 1] * y
            return out
        key = jax.random.key(seed)
        ks = jax.random.split(key, 4)
        scale = 1.0 / np.sqrt(D).astype(np.float32)
        return {'input_embeddings': jax.random.normal(ks[0], (B, S, D), jnp.float32), 'router_w': jax.random.normal(ks[1], (NUM_EXPERTS, D), jnp.float32) * scale, 'w1': jax.random.normal(ks[2], (NUM_EXPERTS, D, D), jnp.float32) * scale, 'b1': jnp.zeros((NUM_EXPERTS, D), jnp.float32), 'w2': jax.random.normal(ks[3], (NUM_EXPERTS, D, D), jnp.float32) * scale, 'b2': jnp.zeros((NUM_EXPERTS, D), jnp.float32)}
    _L3_ffn_all = _L3_ffn_setup()
    _L3_ffn_in = {k: v for k, v in _L3_ffn_all.items() if k in ('router_w', 'w1', 'b1', 'w2', 'b2')}
    del _L3_ffn_all
    return {'x': x, 'src': src, 'dst': dst, 'edge_attr_128': edge_attr_128, 'edge_type_2': edge_type_2, 'L0_gnn_W1': _L0_gnn_in['W1'], 'L0_gnn_att_src1': _L0_gnn_in['att_src1'], 'L0_gnn_att_dst1': _L0_gnn_in['att_dst1'], 'L0_gnn_b1': _L0_gnn_in['b1'], 'L0_gnn_W2': _L0_gnn_in['W2'], 'L0_gnn_att_src2': _L0_gnn_in['att_src2'], 'L0_gnn_att_dst2': _L0_gnn_in['att_dst2'], 'L0_gnn_b2': _L0_gnn_in['b2'], 'L0_mix_Wq': _L0_mix_in['Wq'], 'L0_mix_bq': _L0_mix_in['bq'], 'L0_mix_Wk': _L0_mix_in['Wk'], 'L0_mix_bk': _L0_mix_in['bk'], 'L0_mix_Wv': _L0_mix_in['Wv'], 'L0_mix_bv': _L0_mix_in['bv'], 'L0_mix_Wfc': _L0_mix_in['Wfc'], 'L0_mix_bfc': _L0_mix_in['bfc'], 'L0_ffn_gate_w': _L0_ffn_in['gate_w'], 'L0_ffn_gate_b': _L0_ffn_in['gate_b'], 'L0_ffn_W1': _L0_ffn_in['W1'], 'L0_ffn_b1': _L0_ffn_in['b1'], 'L0_ffn_W2': _L0_ffn_in['W2'], 'L0_ffn_b2': _L0_ffn_in['b2'], 'L1_gnn_W1': _L1_gnn_in['W1'], 'L1_gnn_W2': _L1_gnn_in['W2'], 'L1_mix_w_qkv': _L1_mix_in['w_qkv'], 'L1_mix_b_qkv': _L1_mix_in['b_qkv'], 'L1_mix_kln_g': _L1_mix_in['kln_g'], 'L1_mix_kln_b': _L1_mix_in['kln_b'], 'L1_mix_vln_g': _L1_mix_in['vln_g'], 'L1_mix_vln_b': _L1_mix_in['vln_b'], 'L1_mix_w1': _L1_mix_in['w1'], 'L1_mix_b1': _L1_mix_in['b1'], 'L1_mix_w2': _L1_mix_in['w2'], 'L1_mix_b2': _L1_mix_in['b2'], 'L1_ffn_gate_w': _L1_ffn_in['gate_w'], 'L1_ffn_gate_b': _L1_ffn_in['gate_b'], 'L1_ffn_w1': _L1_ffn_in['w1'], 'L1_ffn_b1': _L1_ffn_in['b1'], 'L1_ffn_w2': _L1_ffn_in['w2'], 'L1_ffn_b2': _L1_ffn_in['b2'], 'L2_gnn_Wn': _L2_gnn_in['Wn'], 'L2_gnn_bn': _L2_gnn_in['bn'], 'L2_gnn_We': _L2_gnn_in['We'], 'L2_gnn_be': _L2_gnn_in['be'], 'L2_gnn_attn': _L2_gnn_in['attn'], 'L2_mix_W_qkv': _L2_mix_in['W_qkv'], 'L2_mix_W_out': _L2_mix_in['W_out'], 'L2_mix_b_out': _L2_mix_in['b_out'], 'L2_ffn_gate_w': _L2_ffn_in['gate_w'], 'L2_ffn_gate_b': _L2_ffn_in['gate_b'], 'L2_ffn_w1': _L2_ffn_in['w1'], 'L2_ffn_b1': _L2_ffn_in['b1'], 'L2_ffn_w2': _L2_ffn_in['w2'], 'L2_ffn_b2': _L2_ffn_in['b2'], 'L2_ffn_gamma': _L2_ffn_in['gamma'], 'L2_ffn_beta': _L2_ffn_in['beta'], 'L3_gnn_Wk': _L3_gnn_in['Wk'], 'L3_gnn_Wq': _L3_gnn_in['Wq'], 'L3_gnn_Wv': _L3_gnn_in['Wv'], 'L3_gnn_Wa': _L3_gnn_in['Wa'], 'L3_gnn_Watt': _L3_gnn_in['Watt'], 'L3_gnn_Wmsg': _L3_gnn_in['Wmsg'], 'L3_gnn_pri': _L3_gnn_in['pri'], 'L3_gnn_skip': _L3_gnn_in['skip'], 'L3_mix_w_qkv': _L3_mix_in['w_qkv'], 'L3_mix_w_out': _L3_mix_in['w_out'], 'L3_mix_b_out': _L3_mix_in['b_out'], 'L3_ffn_router_w': _L3_ffn_in['router_w'], 'L3_ffn_w1': _L3_ffn_in['w1'], 'L3_ffn_b1': _L3_ffn_in['b1'], 'L3_ffn_w2': _L3_ffn_in['w2'], 'L3_ffn_b2': _L3_ffn_in['b2']}

def reference(x, src, dst, edge_attr_128, edge_type_2, L0_gnn_W1, L0_gnn_att_src1, L0_gnn_att_dst1, L0_gnn_b1, L0_gnn_W2, L0_gnn_att_src2, L0_gnn_att_dst2, L0_gnn_b2, L0_mix_Wq, L0_mix_bq, L0_mix_Wk, L0_mix_bk, L0_mix_Wv, L0_mix_bv, L0_mix_Wfc, L0_mix_bfc, L0_ffn_gate_w, L0_ffn_gate_b, L0_ffn_W1, L0_ffn_b1, L0_ffn_W2, L0_ffn_b2, L1_gnn_W1, L1_gnn_W2, L1_mix_w_qkv, L1_mix_b_qkv, L1_mix_kln_g, L1_mix_kln_b, L1_mix_vln_g, L1_mix_vln_b, L1_mix_w1, L1_mix_b1, L1_mix_w2, L1_mix_b2, L1_ffn_gate_w, L1_ffn_gate_b, L1_ffn_w1, L1_ffn_b1, L1_ffn_w2, L1_ffn_b2, L2_gnn_Wn, L2_gnn_bn, L2_gnn_We, L2_gnn_be, L2_gnn_attn, L2_mix_W_qkv, L2_mix_W_out, L2_mix_b_out, L2_ffn_gate_w, L2_ffn_gate_b, L2_ffn_w1, L2_ffn_b1, L2_ffn_w2, L2_ffn_b2, L2_ffn_gamma, L2_ffn_beta, L3_gnn_Wk, L3_gnn_Wq, L3_gnn_Wv, L3_gnn_Wa, L3_gnn_Watt, L3_gnn_Wmsg, L3_gnn_pri, L3_gnn_skip, L3_mix_w_qkv, L3_mix_w_out, L3_mix_b_out, L3_ffn_router_w, L3_ffn_w1, L3_ffn_b1, L3_ffn_w2, L3_ffn_b2):
    import jax
    import jax.numpy as jnp

    def _L0_gnn_ref(x, edge_index, W1, att_src1, att_dst1, b1, W2, att_src2, att_dst2, b2):
        import jax, jax.numpy as jnp
        import numpy as np
        N = 50000
        E = 25000
        IN_C = 256
        HID = 64
        HEADS = 4
        NEG_SLOPE = 0.2

        def _gat_conv(x, W, att_src, att_dst, b, src, dst):
            n = x.shape[0]
            h = (x @ W).reshape(n, HEADS, HID)
            a_s = jnp.einsum('nhc,hc->nh', h, att_src)
            a_d = jnp.einsum('nhc,hc->nh', h, att_dst)
            e = jax.nn.leaky_relu(a_s[src] + a_d[dst], NEG_SLOPE)
            m = jax.ops.segment_max(e, dst, num_segments=n)
            ex = jnp.exp(e - m[dst])
            denom = jax.ops.segment_sum(ex, dst, num_segments=n)
            alpha = ex / denom[dst]
            msg = h[src] * alpha[:, :, None]
            out = jax.ops.segment_sum(msg, dst, num_segments=n)
            return out.reshape(n, HEADS * HID) + b
        loop = jnp.arange(N, dtype=edge_index.dtype)
        src = jnp.concatenate([edge_index[0], loop])
        dst = jnp.concatenate([edge_index[1], loop])
        h = _gat_conv(x, W1, att_src1, att_dst1, b1, src, dst)
        h = jax.nn.elu(h)
        h = _gat_conv(h, W2, att_src2, att_dst2, b2, src, dst)
        h = jax.nn.elu(h)
        return h

    def _L0_mix_ref(x, Wq, bq, Wk, bk, Wv, bv, Wfc, bfc):
        import jax, jax.numpy as jnp
        import numpy as np
        B, L, D, H = (4, 512, 256, 8)
        DK = D // H

        def _heads(t):
            b, l, d = t.shape
            return t.reshape(b, l, H, DK).transpose(0, 2, 1, 3)
        q = _heads(x @ Wq.T + bq)
        k = _heads(x @ Wk.T + bk)
        v = _heads(x @ Wv.T + bv)
        seq_len = q.shape[-2]
        p_attn = jnp.einsum('bhnd,bhne->bhde', k, v) / seq_len
        out = jnp.einsum('bhnd,bhde->bhne', q, p_attn)
        out = out.transpose(0, 2, 1, 3).reshape(x.shape[0], seq_len, H * DK)
        return out @ Wfc.T + bfc

    def _L0_ffn_ref(x, gate_w, gate_b, W1, b1, W2, b2):
        import jax, jax.numpy as jnp
        import numpy as np
        B, T, D, H, E = (16, 128, 256, 512, 8)
        Bb, Tt, Dd = x.shape
        Ee = gate_w.shape[1]
        xf = x.reshape(-1, Dd)
        N = xf.shape[0]
        logits = xf @ gate_w + gate_b
        probs = jax.nn.softmax(logits, axis=-1)
        top2_vals, top2_idx = jax.lax.top_k(probs, 2)
        cw = jnp.zeros((N, Ee), dtype=xf.dtype).at[jnp.arange(N)[:, None], top2_idx].add(top2_vals)

        def step(acc, params):
            w1, bb1, w2, bb2, we = params
            h = jax.nn.gelu(xf @ w1 + bb1, approximate=False)
            y = h @ w2 + bb2
            return (acc + we[:, None] * y, None)
        out, _ = jax.lax.scan(step, jnp.zeros_like(xf), (W1, b1, W2, b2, cw.T))
        return out.reshape(Bb, Tt, Dd)

    def _L1_gnn_ref(x, edge_index, W1, W2):
        import jax, jax.numpy as jnp
        import numpy as np
        N_NODES = 50000
        N_EDGES = 25000
        DIM = 256
        self_part = x @ W1.T
        proj = x @ W2.T
        src, dst = (edge_index[0], edge_index[1])
        source_feats = proj[src]
        neighbor_part = jax.ops.segment_sum(source_feats, dst, num_segments=x.shape[0])
        return jax.nn.relu(self_part + neighbor_part)

    def _L1_mix_ref(x, w_qkv, b_qkv, kln_g, kln_b, vln_g, vln_b, w1, b1, w2, b2):
        import jax, jax.numpy as jnp
        import numpy as np
        MIDC = 256
        HEADS = 8
        HEADC = MIDC // HEADS
        EPS = 1e-05

        def _ln(x, gamma, beta):
            mu = jnp.mean(x, axis=-1, keepdims=True)
            var = jnp.var(x, axis=-1, keepdims=True)
            return (x - mu) * jax.lax.rsqrt(var + EPS) * gamma + beta
        B, HW, C = x.shape
        bias = x
        qkv = (x @ w_qkv + b_qkv).reshape(B, HW, HEADS, 3 * HEADC)
        qkv = qkv.transpose(0, 2, 1, 3)
        q, k, v = jnp.split(qkv, 3, axis=-1)
        k = _ln(k, kln_g, kln_b)
        v = _ln(v, vln_g, vln_b)
        kv = jnp.einsum('bhnd,bhne->bhde', k, v) / HW
        out = jnp.einsum('bhnd,bhde->bhne', q, kv)
        out = out.transpose(0, 2, 1, 3).reshape(B, HW, C)
        ret = out + bias
        h = jax.nn.gelu(ret @ w1 + b1, approximate=False)
        return h @ w2 + b2 + bias

    def _L1_ffn_ref(h, gate_w, gate_b, w1, b1, w2, b2):
        import math
        import jax, jax.numpy as jnp
        import numpy as np
        CAPACITY_FACTOR = 1.25
        B, L, D = h.shape
        E = gate_w.shape[1]
        T = B * L
        C = max(1, math.ceil(CAPACITY_FACTOR * T / E))
        x = h.reshape(T, D)
        logits = x @ gate_w + gate_b
        probs = jax.nn.softmax(logits, axis=-1)
        idx = jnp.argmax(probs, axis=-1)
        prb = jnp.take_along_axis(probs, idx[:, None], axis=1)[:, 0]
        one_hot = jax.nn.one_hot(idx, E, dtype=jnp.float32)
        pos = (jnp.cumsum(one_hot, axis=0) * one_hot).sum(-1).astype(jnp.int32) - 1
        kept = pos < C
        pos_safe = jnp.where(kept, pos, C)
        buf = jnp.zeros((E, C, D), dtype=h.dtype).at[idx, pos_safe].set(x, mode='drop')
        hmid = jax.nn.relu(jnp.einsum('ecd,edf->ecf', buf, w1) + b1[:, None, :])
        ybuf = jnp.einsum('ecf,efd->ecd', hmid, w2) + b2[:, None, :]
        pos_g = jnp.minimum(pos, C - 1)
        y_tok = ybuf[idx, pos_g] * (prb * kept)[:, None]
        y = y_tok.reshape(B, L, D)
        y = jnp.nan_to_num(y, nan=0.0, posinf=10000.0, neginf=-10000.0)
        return y

    def _L2_gnn_ref(x, edge_index, edge_attr, Wn, bn, We, be, attn):
        import jax, jax.numpy as jnp
        import numpy as np
        N_NODES = 50000
        N_EDGES = 25000
        IN_DIM = 256
        OUT_DIM = 256
        HEADS = 1
        EDGE_DIM = 128
        NEG_SLOPE = 0.01
        N = x.shape[0]
        H, C = (attn.shape[1], attn.shape[2])
        src, dst = (edge_index[0], edge_index[1])
        h = x @ Wn.T + bn
        e = edge_attr @ We.T + be
        xj = h[src].reshape(-1, H, C)
        ee = e.reshape(-1, H, C)
        a = jax.nn.leaky_relu(jnp.sum((xj + ee) * attn, axis=-1), NEG_SLOPE)
        m = jax.ops.segment_max(a, dst, num_segments=N)
        a = jnp.exp(a - m[dst])
        denom = jax.ops.segment_sum(a, dst, num_segments=N)
        a = a / (denom[dst] + 1e-16)
        msg = (xj * a[..., None]).reshape(-1, H * C)
        out = jax.ops.segment_sum(msg, dst, num_segments=N)
        return jax.nn.relu(out)

    def _L2_mix_ref(x, W_qkv, W_out, b_out):
        import jax, jax.numpy as jnp
        import numpy as np
        HEADS = 4
        DIM_HEAD = 32
        B, L, D = x.shape
        scale = DIM_HEAD ** (-0.5)
        qkv = jnp.einsum('bld,df->blf', x, W_qkv)
        qkv = qkv.reshape(B, L, 3, HEADS, DIM_HEAD)
        q = jnp.transpose(qkv[:, :, 0], (0, 2, 1, 3)) * scale
        k = jax.nn.softmax(jnp.transpose(qkv[:, :, 1], (0, 2, 1, 3)), axis=2)
        v = jnp.transpose(qkv[:, :, 2], (0, 2, 1, 3))
        context = jnp.einsum('bhld,bhle->bhde', k, v)
        out = jnp.einsum('bhde,bhld->bhle', context, q)
        out = jnp.transpose(out, (0, 2, 1, 3)).reshape(B, L, HEADS * DIM_HEAD)
        return jnp.einsum('blf,fd->bld', out, W_out) + b_out

    def _L2_ffn_ref(x, gate_w, gate_b, w1, b1, w2, b2, gamma, beta):
        import jax, jax.numpy as jnp
        import numpy as np
        B, S, H, F, E, K = (8, 128, 256, 512, 16, 2)
        EPS = 1e-05
        gate_logits = x @ gate_w + gate_b
        topk_vals, topk_idx = jax.lax.top_k(gate_logits, K)
        topk_w = jax.nn.softmax(topk_vals, axis=-1)
        h = jax.nn.relu(jnp.einsum('bsh,ehf->bsef', x, w1) + b1)
        expert_out = jnp.einsum('bsef,efh->bseh', h, w2) + b2
        sel = jnp.take_along_axis(expert_out, topk_idx[:, :, :, None], axis=2)
        moe = jnp.sum(topk_w[..., None] * sel, axis=2)
        y = x + moe
        mu = jnp.mean(y, axis=-1, keepdims=True)
        var = jnp.var(y, axis=-1, keepdims=True)
        return (y - mu) / jnp.sqrt(var + EPS) * gamma + beta

    def _L3_gnn_ref(x, Wk, Wq, Wv, Wa, Watt, Wmsg, pri, skip, src, dst, etype):
        import jax, jax.numpy as jnp
        import numpy as np
        N, E = (625, 10000)
        IN_DIM, H, D = (256, 32, 8)
        NUM_ETYPES, L = (2, 2)

        def _hgt_layer(x, Wk, Wq, Wv, Wa, Watt, Wmsg, pri, skip, src, dst, etype):
            n = x.shape[0]
            k = (x @ Wk).reshape(n, H, D)
            q = (x @ Wq).reshape(n, H, D)
            v = (x @ Wv).reshape(n, H, D)
            k_e, q_e, v_e = (k[src], q[dst], v[src])
            is0 = (etype == 0)[:, None, None]
            kw = jnp.where(is0, jnp.einsum('ehd,hdf->ehf', k_e, Watt[:, 0]), jnp.einsum('ehd,hdf->ehf', k_e, Watt[:, 1]))
            m = jnp.where(is0, jnp.einsum('ehd,hdf->ehf', v_e, Wmsg[:, 0]), jnp.einsum('ehd,hdf->ehf', v_e, Wmsg[:, 1]))
            a = (kw * q_e).sum(-1) * pri[:, etype].T / np.float32(np.sqrt(D))
            amax = jax.ops.segment_max(a, dst, num_segments=n)
            ea = jnp.exp(a - amax[dst])
            att = ea / jax.ops.segment_sum(ea, dst, num_segments=n)[dst]
            h = jax.ops.segment_sum(m * att[:, :, None], dst, num_segments=n).reshape(n, H * D)
            h = h @ Wa
            alpha = jax.nn.sigmoid(skip)
            return h * alpha + x * (1.0 - alpha)
        h = x
        for l in range(L):
            h = _hgt_layer(h, Wk[l], Wq[l], Wv[l], Wa[l], Watt[l], Wmsg[l], pri[l], skip[l], src, dst, etype)
        return h

    def _L3_mix_ref(x, w_qkv, w_out, b_out):
        import jax, jax.numpy as jnp
        import numpy as np
        HEADS, DIM_HEAD = (8, 64)
        EPS = 1e-05

        def instance_norm(t):
            mu = jnp.mean(t, axis=-1, keepdims=True)
            var = jnp.mean((t - mu) ** 2, axis=-1, keepdims=True)
            return (t - mu) * jax.lax.rsqrt(var + EPS)
        B, N, _ = x.shape
        H, Dh = (HEADS, DIM_HEAD)
        qkv = jnp.einsum('bnd,ed->bne', x, w_qkv)
        q, k, v = jnp.split(qkv, 3, axis=-1)

        def to_heads(t):
            return t.reshape(B, N, H, Dh).transpose(0, 2, 1, 3)
        q, k, v = (to_heads(q), to_heads(k), to_heads(v))
        k = instance_norm(k)
        v = instance_norm(v)
        dots = jnp.einsum('bhnd,bhne->bhde', k, v)
        out = jnp.einsum('bhnd,bhde->bhne', q, dots) / N
        out = out.transpose(0, 2, 1, 3).reshape(B, N, H * Dh)
        return jnp.einsum('bne,de->bnd', out, w_out) + b_out

    def _L3_ffn_ref(input_embeddings, router_w, w1, b1, w2, b2):
        import jax, jax.numpy as jnp
        import numpy as np
        NUM_EXPERTS = 8
        TOP_K = 2
        B, S, D = (8, 256, 256)

        def _moe(tokens, router_w, w1, b1, w2, b2):
            N = tokens.shape[0]
            E = router_w.shape[0]
            logits = tokens.astype(jnp.float32) @ router_w.astype(jnp.float32).T
            probs = jax.nn.softmax(logits, axis=-1)
            rw, re = jax.lax.top_k(probs, TOP_K)
            if TOP_K > 1:
                rw = rw / jnp.maximum(rw.sum(-1, keepdims=True), 1e-12)
            rw = rw.astype(tokens.dtype)
            combine = jnp.zeros((N, E), tokens.dtype).at[jnp.arange(N)[:, None], re].set(rw)
            out = tokens
            for e in range(E):
                h = jax.nn.gelu(tokens @ w1[e] + b1[e], approximate=False)
                y = h @ w2[e] + b2[e]
                out = out + combine[:, e:e + 1] * y
            return out
        b, s, d = input_embeddings.shape
        tokens = input_embeddings.reshape(b * s, d)
        return _moe(tokens, router_w, w1, b1, w2, b2).reshape(b, s, d)
    edge_index = jnp.stack([src, dst])
    xn = _layernorm(x, axis=-1)
    x = x + _L0_gnn_ref(xn, edge_index, L0_gnn_W1, L0_gnn_att_src1, L0_gnn_att_dst1, L0_gnn_b1, L0_gnn_W2, L0_gnn_att_src2, L0_gnn_att_dst2, L0_gnn_b2) + _L0_mix_ref(xn[None], L0_mix_Wq, L0_mix_bq, L0_mix_Wk, L0_mix_bk, L0_mix_Wv, L0_mix_bv, L0_mix_Wfc, L0_mix_bfc)[0]
    x = x + _L0_ffn_ref(_layernorm(x, axis=-1)[None], L0_ffn_gate_w, L0_ffn_gate_b, L0_ffn_W1, L0_ffn_b1, L0_ffn_W2, L0_ffn_b2)[0]
    xn = _layernorm(x, axis=-1)
    x = x + _L1_gnn_ref(xn, edge_index, L1_gnn_W1, L1_gnn_W2) + _L1_mix_ref(xn[None], L1_mix_w_qkv, L1_mix_b_qkv, L1_mix_kln_g, L1_mix_kln_b, L1_mix_vln_g, L1_mix_vln_b, L1_mix_w1, L1_mix_b1, L1_mix_w2, L1_mix_b2)[0]
    x = x + _L1_ffn_ref(_layernorm(x, axis=-1)[None], L1_ffn_gate_w, L1_ffn_gate_b, L1_ffn_w1, L1_ffn_b1, L1_ffn_w2, L1_ffn_b2)[0]
    xn = _layernorm(x, axis=-1)
    x = x + _L2_gnn_ref(xn, edge_index, edge_attr_128, L2_gnn_Wn, L2_gnn_bn, L2_gnn_We, L2_gnn_be, L2_gnn_attn) + _L2_mix_ref(xn[None], L2_mix_W_qkv, L2_mix_W_out, L2_mix_b_out)[0]
    x = x + _L2_ffn_ref(_layernorm(x, axis=-1)[None], L2_ffn_gate_w, L2_ffn_gate_b, L2_ffn_w1, L2_ffn_b1, L2_ffn_w2, L2_ffn_b2, L2_ffn_gamma, L2_ffn_beta)[0]
    xn = _layernorm(x, axis=-1)
    x = x + _L3_gnn_ref(xn, L3_gnn_Wk, L3_gnn_Wq, L3_gnn_Wv, L3_gnn_Wa, L3_gnn_Watt, L3_gnn_Wmsg, L3_gnn_pri, L3_gnn_skip, src, dst, edge_type_2) + _L3_mix_ref(xn[None], L3_mix_w_qkv, L3_mix_w_out, L3_mix_b_out)[0]
    x = x + _L3_ffn_ref(_layernorm(x, axis=-1)[None], L3_ffn_router_w, L3_ffn_w1, L3_ffn_b1, L3_ffn_w2, L3_ffn_b2)[0]
    return x

_drawn_inputs = setup_inputs


def setup_inputs(seed=0):
    import zlib

    import numpy as np

    out = dict(_drawn_inputs(seed))
    spreads = {'L0_gnn_b1': (0.0, 0.426),
     'L0_gnn_b2': (0.0, 0.432),
     'L0_mix_bq': (0.0, 0.771),
     'L0_mix_bk': (0.0, 0.771),
     'L0_mix_bv': (0.0, 0.773),
     'L0_mix_bfc': (0.0, 0.453),
     'L0_ffn_gate_b': (0.0, 0.8),
     'L0_ffn_b1': (0.0, 2.0),
     'L0_ffn_b2': (0.0, 0.8),
     'L1_mix_b_qkv': (0.0, 0.1),
     'L1_mix_kln_g': (1.0, 0.6),
     'L1_mix_kln_b': (0.0, 0.374),
     'L1_mix_vln_g': (1.0, 0.6),
     'L1_mix_vln_b': (0.0, 0.314),
     'L1_mix_b1': (0.0, 0.879),
     'L1_mix_b2': (0.0, 0.623),
     'L1_ffn_gate_b': (0.0, 1.279),
     'L1_ffn_b1': (0.0, 2.0),
     'L1_ffn_b2': (0.0, 2.0),
     'L2_gnn_bn': (0.0, 0.957),
     'L2_gnn_be': (0.0, 2.0),
     'L2_mix_b_out': (0.0, 0.627),
     'L2_ffn_gate_b': (0.0, 0.484),
     'L2_ffn_b1': (0.0, 0.8),
     'L2_ffn_b2': (0.0, 1.652),
     'L2_ffn_gamma': (1.0, 0.6),
     'L2_ffn_beta': (0.0, 0.85),
     'L3_gnn_pri': (1.0, 0.6),
     'L3_gnn_skip': (1.0, 0.6),
     'L3_ffn_b1': (0.0, 2.0),
     'L3_ffn_b2': (0.0, 2.0)}
    factors = {'L0_gnn_att_dst1': 29.512,
     'L0_gnn_att_dst2': 51.632,
     'L0_mix_Wq': 7.03,
     'L0_mix_Wk': 7.615,
     'L0_mix_Wv': 7.45,
     'L0_mix_Wfc': 4.671,
     'L0_ffn_W1': 15.839,
     'L2_ffn_gate_w': 2.818,
     'L2_ffn_w1': 4.411,
     'L2_ffn_w2': 3.497,
     'L3_gnn_Wk': 8.0,
     'L3_gnn_Wq': 8.0,
     'L3_gnn_Wv': 8.0,
     'L3_gnn_Wa': 8.0,
     'L3_gnn_Watt': 8.0,
     'L3_gnn_Wmsg': 8.0,
     'L3_mix_b_out': 64.0,
     'L0_gnn_W1': 3.874,
     'L0_gnn_att_src1': 5.401,
     'L0_gnn_att_src2': 8.0,
     'L0_ffn_gate_w': 5.493,
     'L0_ffn_W2': 4.783,
     'L1_ffn_gate_w': 2.833,
     'L1_ffn_w1': 4.974,
     'L1_ffn_w2': 3.531}
    for name, (base, spread) in spreads.items():
        noise = np.random.default_rng([zlib.crc32(name.encode()), seed]).standard_normal(out[name].shape)
        drawn = base * np.exp(spread * noise) if base else spread * noise
        out[name] = jnp.asarray(drawn.astype(out[name].dtype))
    for name, factor in factors.items():
        out[name] = (out[name] * factor).astype(out[name].dtype)
    return out
```

```python
from contextlib import ExitStack

import concourse.bass as bass
from concourse import mybir

F32 = mybir.dt.float32
BF16 = mybir.dt.bfloat16
I32 = mybir.dt.int32
U32 = mybir.dt.uint32
ALU = mybir.AluOpType
ACT = mybir.ActivationFunctionType
AX = mybir.AxisListType

N, D, E = 3125, 256, 50000
P = 125
NT = N // P
ER = E // P
EG = 4
TE = 416
assert E // 128 + NT <= TE and TE % EG == 0
NG = TE // EG
GE = EG * 128
BIG = 1.0e30
ROUND = 12582912.0


def each(eng, count, body, unroll=2, peel=False):
    for i in range(unroll if peel else 0):
        body(i, i)
    with eng.Fori(int(peel), count // unroll) as k:
        for u in range(unroll):
            body(unroll * k + u, u)
    for i in range(count - count % unroll, count):
        body(i, i % unroll)


def later(i, n=2):
    return not isinstance(i, int) or i >= n


def piped(eng, count, stages, unroll=4):
    first = -(-(max(lag for lag, _ in stages) + unroll) // unroll) * unroll

    def step(i, u):
        for lag, body in stages:
            if not isinstance(i, int) or 0 <= i - lag < count:
                body(i - lag, (u - lag) % unroll)
    for i in range(first):
        step(i, i % unroll)
    last = count // unroll * unroll
    with eng.Fori(first // unroll, last // unroll) as k:
        for u in range(unroll):
            step(unroll * k + u, u)
    for i in range(last, count + max(lag for lag, _ in stages)):
        step(i, i % unroll)


class Core:

    def __init__(self, nc, ins, out):
        self.nc, self.ins, self.out = nc, ins, out
        self.spent = []

    def dram(self, name, shape, dt=F32):
        return self.nc.dram_tensor(name, shape, dt, kind="Internal").ap()


class Phase:

    def __init__(self, core, name):
        self.core, self.nc, self.name = core, core.nc, name

    def __enter__(self):
        self.ctx = ExitStack()
        self.sems = []
        if len(self.core.spent) > 90:
            self.nc.all_engine_barrier()
            self.nc.clear_and_free_semaphores(self.core.spent)
            self.nc.all_engine_barrier()
            self.core.spent = []
        return self

    def __exit__(self, *a):
        self.ctx.close()
        self.core.spent += self.sems

    def sb(self, name, shape, dt=F32):
        return self.ctx.enter_context(self.nc.sbuf_tensor(f"{self.name}_{name}", shape, dt))

    def psum(self, name, shape, dt=F32):
        return self.ctx.enter_context(self.nc.psum_tensor(f"{self.name}_{name}", shape, dt))

    def sem(self, name):
        self.sems.append(self.nc.alloc_semaphore(f"{self.name}_{name}"))
        return self.sems[-1]

    def block(self):
        return self.ctx.enter_context(self.nc.Block())


def constants(core, keep):
    core.ident = keep.sb("ident", [128, 128])
    core.ones = keep.sb("ones", [128, 128])
    core.tri = keep.sb("tri", [128, 128])
    core.low = keep.sb("low", [128, 128])
    core.iota = keep.sb("iota", [128, 128])
    core.iotap = keep.sb("iotap", [128, 1])
    with Phase(core, "const") as ph:
        made = ph.sem("made")
        block = ph.block()

        @block.gpsimd
        def _(gp):
            gp.memset(core.ones[:, :], 1.0).then_inc(made, 1)
            gp.iota(core.iota[:, :], [[1, 128]], 0, 0, allow_small_or_imprecise_dtypes=True).then_inc(made, 1)
            gp.iota(core.iotap[:, :], [[0, 1]], 0, 1, allow_small_or_imprecise_dtypes=True).then_inc(made, 1)
            gp.wait_ge(made, 3)
            gp.affine_select(out=core.ident[:, :], in_=core.ones[:, :], compare_op=ALU.is_equal, fill=0.0,
                             base=0, pattern=[[1, 128]], channel_multiplier=-1)
            gp.affine_select(out=core.tri[:, :], in_=core.ones[:, :], compare_op=ALU.is_gt, fill=0.0,
                             base=0, pattern=[[1, 128]], channel_multiplier=-1)
            gp.affine_select(out=core.low[:, :], in_=core.ones[:, :], compare_op=ALU.is_gt, fill=0.0,
                             base=0, pattern=[[-1, 128]], channel_multiplier=1)


def sort_edges(core, keep):
    ins = core.ins
    core.e_src = keep.sb("e_src", [128, TE], I32)
    core.e_srct = keep.sb("e_srct", [128, TE], I32)
    core.e_loc = keep.sb("e_loc", [128, TE])
    core.e_last = keep.sb("e_last", [128, TE])
    core.e_ee = keep.sb("e_ee", [128, TE])
    core.e_blk = keep.sb("e_blk", [1, TE], I32)
    core.locrow = core.dram("locrow", (TE * 128,))
    core.rstrow = core.dram("rstrow", (TE * 128,))
    dstrows = core.dram("dstrows", (ER, P))
    lorows = core.dram("lorows", (ER, P))
    recs = core.dram("recs", (TE * 128, 4), I32)
    dsts = core.dram("dsts", (TE * 128 + 2,))
    G = 8
    NGU = ER // G

    with Phase(core, "prep") as keep2:
        dstc = keep2.sb("dst", [P, ER])
        hic = keep2.sb("hi", [P, ER])
        loc = keep2.sb("lo", [P, ER])
        rec = keep2.sb("rec", [P, ER, 4], I32)
        start = keep2.sb("start", [P, NT])

        with Phase(core, "digits") as ph:
            si = ph.sb("si", [P, ER], I32)
            di = ph.sb("di", [P, ER], I32)
            ti = ph.sb("ti", [P, ER], I32)
            tmp = ph.sb("tmp", [P, ER])
            sf = ph.sb("sf", [P, ER])
            tf = ph.sb("tf", [P, ER])
            att = ph.sb("att", [128, 2])
            attb = ph.sb("attb", [128, 2, P])
            web = ph.sb("web", [128, 2, 129])
            wea = ph.sb("wea", [P, 129])
            ea = ph.sb("ea", [P, 2, G, 128])
            prod = ph.sb("prod", [P, G, 128])
            ee = ph.sb("ee", [P, ER])
            rowsb = ph.sb("rowsb", [100, 2, 4, P])
            pad = ph.sb("pad", [128, TE, 4], I32)
            pw = ph.psum("pw", [P, 129])
            pt = ph.psum("pt", [100, 4, P])
            loaded, attr_in = ph.sem("loaded"), [ph.sem(f"attr_in{b}") for b in range(2)]
            attr_used = ph.sem("attr_used")
            bc, wea_ready, wea_here = ph.sem("bc"), ph.sem("wea_ready"), ph.sem("wea_here")
            digits, turned, rows_out, stored, padded = (ph.sem("digits"), ph.sem("turned"), ph.sem("rows_out"),
                                                        ph.sem("stored"), ph.sem("padded"))
            block = ph.block()
            attr = ins["edge_attr_128"].rearrange("(p t) c -> p t c", p=P)

            @block.sync
            def _(sp):
                for dst, src in ((si, "src"), (di, "dst"), (ti, "edge_type_2")):
                    sp.dma_start(dst[:, :], ins[src].rearrange("(p t) -> p t", p=P)).then_inc(loaded, 16)
                sp.dma_start(web[:, :, 0:128], ins["L2_gnn_We"].rearrange("(k p) c -> p k c", p=128)).then_inc(loaded, 16)
                with core.nc.allow_non_contiguous_dma(reason="two short columns"):
                    sp.dma_start(web[:, :, 128:129], ins["L2_gnn_be"].rearrange("(k p o) -> p k o", p=128, o=1)).then_inc(loaded, 16)
                    sp.dma_start(att[:, :], ins["L2_gnn_attn"].rearrange("a b (k p) -> p (a b k)", p=128)).then_inc(loaded, 16)

                def load(g, b):
                    sp.wait_ge(attr_used, g + 1)
                    sp.dma_start(ea[:, b, :, :], attr[:, bass.ds(g * G, G), :]).then_inc(attr_in[b], 16)
                each(sp, NGU, load)
                sp.wait_ge(rows_out, 2)
                for i, rows in enumerate((dstrows, lorows)):
                    sp.dma_start(rows.rearrange("(j r) p -> r j p", r=100), rowsb[:, i, :, :]).then_inc(stored, 16)
                sp.wait_ge(padded, 1)
                sp.dma_start(recs.rearrange("(p t) w -> p t w", p=128), pad[:, :, :]).then_inc(stored, 16)
                sp.wait_ge(stored, 48)

            @block.gpsimd
            def _(gp):
                gp.memset(pad[:, :, :], 0)
                gp.drain()
                gp.memset(pad[:, :, 1:2], -1).then_inc(padded, 1)

            @block.tensor
            def _(pe):
                pe.wait_ge(bc, 2)
                for k in range(2):
                    mm = pe.matmul(pw[:, :], attb[:, k, :], web[:, k, :], start=(k == 0), stop=(k == 1))
                mm.then_inc(wea_ready, 1)
                pe.wait_ge(digits, 1)
                for i, m in enumerate((dstc, loc)):
                    if i:
                        pe.wait_ge(rows_out, i)
                    for j in range(4):
                        mm = pe.transpose(pt[:, j, :], m[:, 100 * j:100 * j + 100], core.ident[0:P, 0:P])
                    mm.then_inc(turned, 1)

            @block.scalar
            def _(act):
                for i in range(2):
                    act.wait_ge(turned, i + 1)
                    act.copy(rowsb[:, i, :, :], pt[:, :, :]).then_inc(rows_out, 1)

            @block.vector
            def _(v):
                v.sem_inc(attr_used, 2)
                v.wait_ge(loaded, 96)
                for k in range(2):
                    v.tensor_scalar(attb[:, k, :], core.ones[:, 0:P], att[:, k:k + 1], None, ALU.mult).then_inc(bc, 1)
                v.tensor_copy(dstc[:, :], di[:, :])
                v.tensor_copy(sf[:, :], si[:, :])
                v.tensor_copy(tf[:, :], ti[:, :])
                v.drain()
                v.tensor_scalar(tmp[:, :], dstc[:, :], -62.0, 1.0 / P, ALU.add, ALU.mult)
                v.drain()
                v.tensor_scalar(hic[:, :], tmp[:, :], ROUND, -ROUND, ALU.add, ALU.add)
                v.drain()
                v.scalar_tensor_tensor(out=loc[:, :], in0=hic[:, :], scalar=-float(P), in1=dstc[:, :],
                                       op0=ALU.mult, op1=ALU.add).then_inc(digits, 1)
                v.tensor_copy(rec[:, :, 0], si[:, :])
                v.tensor_copy(rec[:, :, 1], di[:, :])
                v.scalar_tensor_tensor(out=rec[:, :, 2], in0=sf[:, :], scalar=2.0, in1=tf[:, :],
                                       op0=ALU.mult, op1=ALU.add)
                v.wait_ge(wea_ready, 1)
                v.tensor_copy(wea[:, :], pw[:, :])
                v.drain()

                def score(g, b):
                    v.wait_ge(attr_in[b], 16 * (g // 2 + 1) if isinstance(g, int) else 8 * (g - b) + 16)
                    v.tensor_tensor(prod[:, :, :], ea[:, b, :, :], wea[:, 0:128].unsqueeze(1).to_broadcast([P, G, 128]),
                                    ALU.mult).then_inc(attr_used, 1)
                    v.drain()
                    v.tensor_reduce(ee[:, bass.ds(g * G, G)], prod[:, :, :], AX.X, ALU.add)
                    v.drain()
                each(v, NGU, score)
                v.tensor_scalar(rec[:, :, 3].bitcast(F32), ee[:, :], wea[:, 128:129], None, ALU.add)

        with Phase(core, "count") as ph:
            ohl = ph.sb("ohl", [P, 2, G, P], BF16)
            ohh = ph.sb("ohh", [P, 2, G, NT], BF16)
            zero = ph.sb("zero", [P, P], BF16)
            total = ph.sb("total", [P, NT])
            tiles = ph.sb("tiles", [P, 3, NT])
            tstart = ph.sb("tstart", [P, NT])
            ct = ph.sb("ct", [1, TE, NT])
            io = ph.sb("io", [1, TE])
            bf = ph.sb("bf", [1, TE])
            ph_t = ph.psum("t", [P, NT])
            ph_c = ph.psum("c", [P, NT])
            ph_b = ph.psum("b", [P, NT])
            zeroed, hot, used, summed, copied, ranked = (ph.sem("zeroed"), ph.sem("hot"), ph.sem("used"),
                                                         ph.sem("summed"), ph.sem("copied"), ph.sem("ranked"))
            counted = ph.sem("counted")
            block = ph.block()

            @block.gpsimd
            def _(gp):
                gp.iota(io[:, :], [[1, TE]], 0, 0, allow_small_or_imprecise_dtypes=True).then_inc(counted, 1)

            @block.tensor
            def _(pe):
                pe.sem_inc(used, 2)
                pe.wait_ge(zeroed, 1)
                pe.matmul(ph_t[:, :], zero[:, :], zero[:, 0:NT], start=True, stop=False)

                def count(g, b):
                    pe.wait_ge(hot, g + 1)
                    for j in range(G):
                        mm = pe.matmul(ph_t[:, :], ohl[:, b, j, :], ohh[:, b, j, :], start=False, stop=False)
                    mm.then_inc(used, 1)
                each(pe, NGU, count)
                pe.matmul(ph_t[:, :], zero[:, :], zero[:, 0:NT], start=False, stop=True).then_inc(summed, 1)
                pe.wait_ge(copied, 1)
                pe.matmul(ph_b[:, :], core.tri[0:P, 0:P], total[:, :], start=True, stop=True)
                pe.matmul(ph_c[:, :], core.ones[0:P, 0:P], total[:, :], start=True, stop=True).then_inc(ranked, 1)

            @block.vector
            def _(v):
                v.memset(zero[:, :], 0.0).then_inc(zeroed, 1)

                def hots(g, b):
                    v.wait_ge(used, g + 1)
                    v.tensor_tensor(ohl[:, b, :, :], core.iota[0:P, 0:P].unsqueeze(1).to_broadcast([P, G, P]),
                                    loc[:, bass.ds(g * G, G)].unsqueeze(2).to_broadcast([P, G, P]), ALU.is_equal)
                    v.tensor_tensor(ohh[:, b, :, :], core.iota[0:P, 0:NT].unsqueeze(1).to_broadcast([P, G, NT]),
                                    hic[:, bass.ds(g * G, G)].unsqueeze(2).to_broadcast([P, G, NT]), ALU.is_equal)
                    v.drain()
                    v.sem_inc(hot, 1)
                each(v, NGU, hots)
                v.wait_ge(summed, 1)
                v.tensor_copy(total[:, :], ph_t[:, :]).then_inc(copied, 1)
                v.wait_ge(ranked, 1)
                v.tensor_scalar(tiles[:, 0, :], ph_c[:, :], 1.0 / 128, 63.75 / 128, ALU.mult, ALU.add)
                v.drain()
                v.tensor_scalar(tiles[:, 1, :], tiles[:, 0, :], ROUND, -ROUND, ALU.add, ALU.add)
                v.memset(tiles[:, 2, :], 0.0)
                v.drain()
                v.memset(tstart[:, 0:1], 0.0)
                v.tensor_tensor_scan(tstart[:, 1:NT], tiles[:, 1, 0:NT - 1], tiles[:, 2, 0:NT - 1], 0.0, ALU.add, ALU.add)
                v.drain()
                v.scalar_tensor_tensor(out=start[:, :], in0=tstart[:, :], scalar=128.0, in1=ph_b[:, :],
                                       op0=ALU.mult, op1=ALU.add)
                v.wait_ge(counted, 1)
                v.tensor_tensor(ct[:, :, :], io[:, :].unsqueeze(2).to_broadcast([1, TE, NT]),
                                tstart[0:1, :].unsqueeze(1).to_broadcast([1, TE, NT]), ALU.is_ge)
                v.drain()
                v.tensor_reduce(bf[:, :], ct[:, :, :], AX.X, ALU.add)
                v.drain()
                v.tensor_scalar(core.e_blk[:, :], bf[:, :], -1.0, None, ALU.add)

        with Phase(core, "place") as ph:
            ohl = ph.sb("ohl", [P, 2, G, P])
            ohh = ph.sb("ohh", [P, 2, G, NT])
            oht = ph.sb("oht", [P, 2, G, P])
            eq = ph.sb("eq", [P, G, P])
            eqt = ph.sb("eqt", [P, G, P])
            rank = ph.sb("rank", [P, G])
            lk = ph.sb("lk", [P, G, NT])
            posf = ph.sb("posf", [P, G])
            posf2 = ph.sb("posf2", [P, G])
            pos = ph.sb("pos", [P, 2, G], I32)
            stage = ph.sb("stage", [P, 2, G, 4], I32)
            run = ph.sb("run", [P, 2, G + 1, NT])
            drow = ph.sb("drow", [P, 2, G * P])
            lrow = ph.sb("lrow", [P, 2, G * P])
            p_delta = ph.psum("delta", [P, 2, 512])
            p_look = ph.psum("look", [P, 2, 512])
            rows_in, rows_used = [ph.sem(f"rows_in{b}") for b in range(2)], ph.sem("rows_used")
            hot, delta, runs, looked, placed = ph.sem("hot"), ph.sem("delta"), ph.sem("runs"), ph.sem("looked"), ph.sem("placed")
            scat = [ph.sem(f"scat{b}") for b in range(2)]
            block = ph.block()

            @block.sync
            def _(sp):
                def load(g, b):
                    sp.wait_ge(rows_used, g + 1)
                    for sbt, rows in ((drow, dstrows), (lrow, lorows)):
                        sp.dma_start(sbt[:, b, :], rows[bass.ds(g * G, G), :].rearrange("t p -> (t p)").partition_broadcast(P)
                                     ).then_inc(rows_in[b], 16)
                each(sp, NGU, load)

            @block.tensor
            def _(pe):
                def count(g, b):
                    pe.wait_ge(hot, g + 1)
                    for j in range(G):
                        mm = pe.matmul(p_delta[:, b, j * NT:(j + 1) * NT], ohl[:, b, j, :], ohh[:, b, j, :], start=True, stop=True)
                    mm.then_inc(delta, 1)
                    pe.wait_ge(runs, g + 1)
                    for j in range(G):
                        mm = pe.matmul(p_look[:, b, j * NT:(j + 1) * NT], oht[:, b, j, :], run[:, b, j, :], start=True, stop=True)
                    mm.then_inc(looked, 1)
                each(pe, NGU, count)

            @block.vector
            def _(v):
                v.sem_inc(rows_used, 2)
                v.tensor_copy(run[:, 1, G, :], start[:, :])
                v.drain()

                def place(g, b):
                    v.wait_ge(rows_in[b], 16 * (g - b) + 32)
                    v.tensor_tensor(ohl[:, b, :, :], core.iota[0:P, 0:P].unsqueeze(1).to_broadcast([P, G, P]),
                                    loc[:, bass.ds(g * G, G)].unsqueeze(2).to_broadcast([P, G, P]), ALU.is_equal)
                    v.tensor_tensor(ohh[:, b, :, :], core.iota[0:P, 0:NT].unsqueeze(1).to_broadcast([P, G, NT]),
                                    hic[:, bass.ds(g * G, G)].unsqueeze(2).to_broadcast([P, G, NT]), ALU.is_equal)
                    v.tensor_scalar(oht[:, b, :, :].rearrange("p g e -> p (g e)"), lrow[:, b, :], core.iotap[0:P, :], None, ALU.is_equal)
                    v.tensor_tensor(eq[:, :, :], drow[:, b, :].rearrange("p (g e) -> p g e", g=G),
                                    dstc[:, bass.ds(g * G, G)].unsqueeze(2).to_broadcast([P, G, P]), ALU.is_equal)
                    v.drain()
                    v.sem_inc(hot, 1)
                    v.sem_inc(rows_used, 1)
                    v.tensor_tensor(eqt[:, :, :], eq[:, :, :], core.low[0:P, 0:P].unsqueeze(1).to_broadcast([P, G, P]), ALU.mult)
                    v.drain()
                    v.tensor_reduce(rank[:, :], eqt[:, :, :], AX.X, ALU.add)
                    v.tensor_copy(run[:, b, 0, :], run[:, 1 - b, G, :])
                    v.drain()
                    v.wait_ge(delta, g + 1)
                    for j in range(G):
                        v.tensor_tensor(run[:, b, j + 1, :], run[:, b, j, :], p_delta[:, b, j * NT:(j + 1) * NT], ALU.add)
                        v.drain()
                    v.sem_inc(runs, 1)
                    v.wait_ge(looked, g + 1)
                    v.tensor_tensor(lk[:, :, :], p_look[:, b, 0:G * NT].rearrange("p (g h) -> p g h", g=G), ohh[:, b, :, :], ALU.mult)
                    v.drain()
                    v.tensor_reduce(posf[:, :], lk[:, :, :], AX.X, ALU.add)
                    v.drain()
                    v.tensor_tensor(posf2[:, :], posf[:, :], rank[:, :], ALU.add)
                    v.drain()
                    if later(g):
                        v.wait_ge(scat[b], G * 8 * (g - b))
                    v.tensor_copy(pos[:, b, :], posf2[:, :])
                    v.tensor_copy(stage[:, b, :, :], rec[:, bass.ds(g * G, G), :])
                    v.drain()
                    v.sem_inc(placed, 1)
                each(v, NGU, place, peel=True)

            @block.gpsimd
            def _(gp):
                def scatter(g, b):
                    gp.wait_ge(placed, g + 1)
                    gp.nop(nofuse=True)
                    for j in range(G):
                        gp.indirect_dma_start(recs, bass.IndirectOffsetOnAxis(ap=pos[:, b, j:j + 1].bitcast(U32), axis=0),
                                              stage[:, b, j, :], None).then_inc(scat[b], 16)
                each(gp, NGU, scatter)
                for b in range(2):
                    gp.wait_ge(scat[b], G * 16 * (NGU // 2))

    with Phase(core, "cols") as ph:
        R, J = 104, 4
        rc = ph.sb("rc", [128, TE, 4], I32)
        dcol = ph.sb("dcol", [128, TE])
        drow = ph.sb("drow", [R, J, 128])
        win = ph.sb("win", [R, 3, J, 128])
        tmp = ph.sb("tmp", [R, 4, J * 128])
        ends = ph.sb("ends", [1, 2])
        pt = ph.psum("pt", [R, J, 128])
        pc = ph.psum("pc", [128, 2, 512])
        loaded, cols, turned, rows, stored, windows = (ph.sem("loaded"), ph.sem("cols"), ph.sem("turned"), ph.sem("rows"),
                                                       ph.sem("stored"), ph.sem("windows"))
        made, back = ph.sem("made"), ph.sem("back")
        block = ph.block()

        @block.sync
        def _(sp):
            sp.dma_start(rc[:, :, :], recs.rearrange("(t p) w -> p t w", p=128)).then_inc(loaded, 16)
            sp.wait_ge(rows, 1)
            sp.dma_start(dsts[1:1 + TE * 128].rearrange("(j r e) -> r j e", r=R, e=128), drow[:, :, :]).then_inc(stored, 16)
            sp.dma_start(dsts[0:1].rearrange("(a b) -> a b", a=1), ends[:, 0:1]).then_inc(stored, 16)
            sp.dma_start(dsts[TE * 128 + 1:TE * 128 + 2].rearrange("(a b) -> a b", a=1), ends[:, 1:2]).then_inc(stored, 16)
            sp.wait_ge(stored, 48)
            for i, o in enumerate((1, 0, 2)):
                sp.dma_start(win[:, i, :, :], dsts[o:o + TE * 128].rearrange("(j r e) -> r j e", r=R, e=128)).then_inc(windows, 16)
            sp.wait_ge(made, 1)
            sp.dma_start(core.locrow.rearrange("(j r e) -> r j e", r=R, e=128), tmp[:, 1, :].rearrange("r (j e) -> r j e", j=J)).then_inc(stored, 16)
            sp.dma_start(core.rstrow.rearrange("(j r e) -> r j e", r=R, e=128), tmp[:, 2, :].rearrange("r (j e) -> r j e", j=J)).then_inc(stored, 16)
            sp.wait_ge(stored, 80)

        @block.tensor
        def _(pe):
            pe.wait_ge(cols, 1)
            for j in range(J):
                mm = pe.transpose(pt[:, j, :], dcol[:, R * j:R * j + R], core.ident[:, :])
            mm.then_inc(turned, 1)
            pe.wait_ge(made, 1)
            for i, k in enumerate((1, 3)):
                for j in range(J):
                    mm = pe.transpose(pc[:, i, R * j:R * j + R], tmp[:, k, 128 * j:128 * j + 128], core.ident[0:R, 0:R])
            mm.then_inc(back, 1)

        @block.vector
        def _(v):
            v.memset(ends[:, :], -2.0)
            v.wait_ge(loaded, 16)
            v.tensor_copy(dcol[:, :], rc[:, :, 1]).then_inc(cols, 1)
            v.tensor_copy(core.e_src[:, :], rc[:, :, 0])
            v.tensor_copy(core.e_srct[:, :], rc[:, :, 2])
            v.tensor_copy(core.e_ee[:, :], rc[:, :, 3].bitcast(F32))
            v.wait_ge(turned, 1)
            v.tensor_copy(drow[:, :, :], pt[:, :, :])
            v.drain()
            v.sem_inc(rows, 1)
            v.wait_ge(windows, 48)
            here, before, after = (win[:, i, :, :].rearrange("r j e -> r (j e)") for i in range(3))
            t = [tmp[:, i, :] for i in range(4)]
            v.tensor_scalar(t[0], here, -62.0, 1.0 / P, ALU.add, ALU.mult)
            v.drain()
            v.tensor_scalar(t[1], t[0], ROUND, -ROUND, ALU.add, ALU.add)
            v.drain()
            v.scalar_tensor_tensor(out=t[0], in0=t[1], scalar=-float(P), in1=here, op0=ALU.mult, op1=ALU.add)
            v.tensor_scalar(t[2], here, 0.0, None, ALU.is_ge)
            v.drain()
            v.scalar_tensor_tensor(out=t[3], in0=t[0], scalar=1.0, in1=t[2], op0=ALU.add, op1=ALU.mult)
            v.drain()
            v.tensor_scalar(t[1], t[3], -1.0, None, ALU.add)
            v.tensor_tensor(t[0], here, after, ALU.not_equal)
            v.tensor_tensor(t[2], here, before, ALU.not_equal)
            v.drain()
            v.tensor_tensor(here, t[0], t[3], ALU.mult)
            v.tensor_scalar(before, t[2], -BIG, None, ALU.mult)
            v.drain()
            v.tensor_scalar(t[3], here, -1.0, None, ALU.add)
            v.tensor_copy(t[2], before)
            v.drain()
            v.sem_inc(made, 1)
            v.wait_ge(back, 1)
            v.tensor_copy(core.e_loc[:, :], pc[:, 0, 0:TE])
            v.tensor_copy(core.e_last[:, :], pc[:, 1, 0:TE])


def edge_scores(core, name, H, sc, best, table, idx, q=None, ee=False):
    nc = core.nc
    W = table.shape[1]
    with Phase(core, name) as ph:
        ix = ph.sb("ix", [128, 4, EG], I32)
        g = ph.sb("g", [128, 4, EG, W])
        rst = ph.sb("rst", [H, 4, GE])
        run = ph.sb("run", [H, 2, GE])
        raw = ph.sb("raw", [128, 4, EG, H])
        last = ph.sb("last", [128, 4, EG, P])
        bk = ph.sb("bk", [128, 2, EG, H + 1])
        back = ph.psum("back", [128, 512])[:, 0:EG * H].rearrange("p (g h) -> p g h", h=H)
        rows = ph.psum("rows", [H, GE])
        tops = ph.psum("tops", [P, 2, 512])
        if q is not None:
            lrow = ph.sb("lrow", [P, 4, GE])
            hot = ph.sb("hot", [P, 2, GE])
            prod = ph.sb("prod", [128, EG, D])
            qe = ph.psum("qe", [128, 2, EG, D])
        s_ix, s_used = ph.sem("ix_ready"), ph.sem("g_used")
        s_g = [ph.sem(f"g_in{b}") for b in range(4)]
        s_rst = [ph.sem(f"rst_in{b}") for b in range(4)]
        s_run, s_raw, s_kept, s_rows, s_back, s_bk = (ph.sem("run"), ph.sem("raw"), ph.sem("kept"), ph.sem("rows"),
                                                      ph.sem("back"), ph.sem("bk"))
        s_last, s_tops, s_added, s_hot, s_qe = ph.sem("last"), ph.sem("tops"), ph.sem("added"), ph.sem("hot"), ph.sem("qe")
        s_zero = ph.sem("zero")
        block = ph.block()

        @block.sync
        def _(sp):
            def load(i, b):
                sp.wait_ge(s_run, i + 1)
                sp.dma_start(rst[:, b, :], core.rstrow[bass.ds(i * GE, GE)].partition_broadcast(H)).then_inc(s_rst[b], 16)
                if q is not None:
                    sp.dma_start(lrow[:, b, :], core.locrow[bass.ds(i * GE, GE)].partition_broadcast(P)).then_inc(s_rst[b], 16)
            each(sp, NG, load, 4)

        def rows_in(eng, i, b):
            eng.wait_ge(s_rst[b], (16 if q is None else 32) * (1 if isinstance(i, int) else 0)
                        + ((16 if q is None else 32) * (i // 4) if isinstance(i, int) else (4 if q is None else 8) * (i - b + 4)))

        @block.gpsimd
        def _(gp):
            def gather(i, b):
                if later(i, 4):
                    gp.wait_ge(s_used, i - 3)
                gp.tensor_copy(ix[:, b, :], idx[:, bass.ds(i * EG, EG)]).then_inc(s_ix, 1)
                gp.wait_ge(s_ix, i + 1)
                gp.nop(nofuse=True)
                for j in range(EG):
                    gp.indirect_dma_start(g[:, b, j, :], None, table,
                                          bass.IndirectOffsetOnAxis(ap=ix[:, b, j:j + 1].bitcast(U32), axis=0)).then_inc(s_g[b], 16)
            each(gp, NG, gather, 4, peel=True)

        @block.tensor
        def _(pe):
            def queries(i, b):
                pe.wait_ge(s_hot, i + 1)
                if later(i):
                    pe.wait_ge(s_used, i - 1)
                for j in range(EG):
                    blk = pe.value_load(core.e_blk[0:1, bass.ds(i * EG + j, 1)], min_val=0, max_val=NT - 1)
                    mm = pe.matmul(qe[:, b % 2, j, :], hot[:, b % 2, 128 * j:128 * j + 128], q[:, bass.ds(blk, 1), :].rearrange("p o c -> p (o c)"),
                                   start=True, stop=True)
                mm.then_inc(s_qe, 1)

            def turn(i, b):
                pe.wait_ge(s_raw, i + 1)
                if later(i, 1):
                    pe.wait_ge(s_run, i + 4)
                for j in range(EG):
                    mm = pe.transpose(rows[:, 128 * j:128 * j + 128], raw[:, b, j, :], core.ident[:, :])
                mm.then_inc(s_rows, 1)

            def turn_back(i, b):
                pe.wait_ge(s_run, i + 5)
                if later(i, 1):
                    pe.wait_ge(s_bk, i)
                pe.nop(nofuse=True)
                for j in range(EG):
                    mm = pe.transpose(back[:, j, :], run[:, b % 2, 128 * j:128 * j + 128], core.ident[0:H, 0:H])
                mm.then_inc(s_back, 1)

            def pick(i, b):
                pe.wait_ge(s_bk, i + 1)
                pe.wait_ge(s_last, i + 1)
                if later(i):
                    pe.wait_ge(s_added, i - 1)
                for j in range(EG):
                    mm = pe.matmul(tops[:, b % 2, j * (H + 1):(j + 1) * (H + 1)], last[:, b, j, :], bk[:, b % 2, j, :],
                                   start=True, stop=True)
                mm.then_inc(s_tops, 1)
            piped(pe, NG, ([(0, queries)] if q is not None else []) + [(1, turn), (2, turn_back), (3, pick)])

        @block.scalar
        def _(act):
            act.wait_ge(s_zero, 1)

            def keep(i, b):
                act.wait_ge(s_raw, i + 1)
                act.copy(sc[:, bass.ds(i * EG, EG), :], raw[:, b, :, :]).then_inc(s_kept, 1)

            def copy_back(i, b):
                act.wait_ge(s_back, i + 1)
                if later(i):
                    act.wait_ge(s_tops, i - 1)
                act.copy(bk[:, b % 2, :, 0:H], back[:, :, :]).then_inc(s_bk, 1)
            piped(act, NG, [(1, keep), (2, copy_back)])

        @block.vector
        def _(v):
            v.memset(best[:, :, :], 0.0)
            v.memset(bk[:, :, :, H:H + 1], 1.0)
            v.memset(run[:, 1, GE - 1:GE], -BIG)
            v.drain()
            v.sem_inc(s_run, 4)
            v.sem_inc(s_zero, 1)

            def one_hot(i, b):
                rows_in(v, i, b)
                if later(i):
                    v.wait_ge(s_qe, i - 1)
                v.tensor_scalar(hot[:, b % 2, :], lrow[:, b, :], core.iotap[0:P, :], None, ALU.is_equal).then_inc(s_hot, 1)

            def score(i, b):
                v.wait_ge(s_g[b], 16 * EG * (i // 4 + 1) if isinstance(i, int) else 4 * EG * (i - b + 4))
                if later(i, 4):
                    v.wait_ge(s_kept, i - 3)
                    v.wait_ge(s_rows, i - 3)
                if q is not None:
                    v.wait_ge(s_qe, i + 1)
                    if later(i, 1):
                        v.wait_ge(s_raw, i)
                    v.tensor_tensor(prod[:, :, :], g[:, b, :, :], qe[:, b % 2, :, :], ALU.mult).then_inc(s_used, 1)
                    v.drain()
                    v.tensor_reduce(raw[:, b, :, :], prod[:, :, :].rearrange("p g (h d) -> p g h d", h=H), AX.X, ALU.add).then_inc(s_raw, 1)
                elif ee:
                    ex = core.e_ee[:, bass.ds(i * EG, EG)].unsqueeze(2)
                    v.tensor_tensor(g[:, b, :, :], g[:, b, :, :], ex, ALU.add)
                    v.drain()
                    v.scalar_tensor_tensor(out=raw[:, b, :, :], in0=g[:, b, :, :], scalar=0.01, in1=g[:, b, :, :],
                                           op0=ALU.mult, op1=ALU.max)
                    v.drain()
                    v.sem_inc(s_raw, 1)
                    v.sem_inc(s_used, 1)
                else:
                    v.tensor_copy(raw[:, b, :, :], g[:, b, :, :])
                    v.drain()
                    v.sem_inc(s_raw, 1)
                    v.sem_inc(s_used, 1)

            def scan(i, b):
                rows_in(v, i, b)
                v.wait_ge(s_rows, i + 1)
                if later(i):
                    v.wait_ge(s_back, i - 1)
                if later(i, 1):
                    v.wait_ge(s_run, i + 4)
                v.tensor_tensor_scan(run[:, b % 2, :], rst[:, b, :], rows[:, :], run[:, 1 - b % 2, GE - 1:GE], ALU.add, ALU.max
                                     ).then_inc(s_run, 1)

            def last_edges(i, b):
                if later(i, 4):
                    v.wait_ge(s_tops, i - 3)
                v.tensor_tensor(last[:, b, :, :], core.iota[:, 0:P].unsqueeze(1).to_broadcast([128, EG, P]),
                                core.e_last[:, bass.ds(i * EG, EG)].unsqueeze(2).to_broadcast([128, EG, P]), ALU.is_equal
                                ).then_inc(s_last, 1)

            def add(i, b):
                v.wait_ge(s_tops, i + 1)
                for j in range(EG):
                    blk = v.value_load(core.e_blk[0:1, bass.ds(i * EG + j, 1)], min_val=0, max_val=NT - 1)
                    slot = best[:, bass.ds(blk, 1), :].rearrange("p o c -> p (o c)")
                    ins = v.tensor_tensor(slot, slot, tops[:, b % 2, j * (H + 1):(j + 1) * (H + 1)], ALU.add)
                    if j < EG - 1:
                        v.drain()
                ins.then_inc(s_added, 1)
                v.drain()
            piped(v, NG, ([(0, one_hot)] if q is not None else []) + [(1, score), (2, last_edges), (2, scan), (4, add)])


def edge_sums(core, name, H, acc, table, idx, sc=None, dtab=None, leaky=False):
    nc = core.nc
    WO = D + H
    with Phase(core, name) as ph:
        ix = ph.sb("ix", [128, 4, EG], I32)
        g = ph.sb("g", [128, 4, EG, D])
        here = ph.sb("here", [128, 2, EG, P])
        out = ph.psum("out", [P, EG, 512])
        if H:
            WD = dtab.shape[2]
            lrow = ph.sb("lrow", [P, 4, GE])
            hot = ph.sb("hot", [P, 2, GE])
            x = ph.sb("x", [128, 3, EG, H])
            msg = ph.sb("msg", [128, 2, EG, WO])
            de = ph.psum("de", [128, 2, 512])
        s_ix, s_used = ph.sem("ix_ready"), ph.sem("g_used")
        s_g = [ph.sem(f"g_in{b}") for b in range(4)]
        s_row = [ph.sem(f"row_in{b}") for b in range(4)]
        s_hot, s_de, s_x, s_ex, s_msg, s_here, s_out, s_added = (
            ph.sem("hot"), ph.sem("de"), ph.sem("x"), ph.sem("ex"), ph.sem("msg"), ph.sem("here"), ph.sem("out"), ph.sem("added"))
        block = ph.block()

        @block.sync
        def _(sp):
            def load(i, b):
                sp.wait_ge(s_hot, i + 1)
                sp.dma_start(lrow[:, b, :], core.locrow[bass.ds(i * GE, GE)].partition_broadcast(P)).then_inc(s_row[b], 16)
            if H:
                each(sp, NG, load, 4)

        @block.gpsimd
        def _(gp):
            def gather(i, b):
                if later(i, 4):
                    gp.wait_ge(s_used if H else s_out, i - 3)
                gp.tensor_copy(ix[:, b, :], idx[:, bass.ds(i * EG, EG)]).then_inc(s_ix, 1)
                gp.wait_ge(s_ix, i + 1)
                gp.nop(nofuse=True)
                for j in range(EG):
                    gp.indirect_dma_start(g[:, b, j, :], None, table,
                                          bass.IndirectOffsetOnAxis(ap=ix[:, b, j:j + 1].bitcast(U32), axis=0)).then_inc(s_g[b], 16)
            each(gp, NG, gather, 4, peel=True)

        def g_in(eng, i, b):
            eng.wait_ge(s_g[b], 16 * EG * (i // 4 + 1) if isinstance(i, int) else 4 * EG * (i - b + 4))

        @block.tensor
        def _(pe):
            def of_dst(i, b):
                pe.wait_ge(s_hot, i + 5)
                if later(i):
                    pe.wait_ge(s_x, i - 1)
                for j in range(EG):
                    blk = pe.value_load(core.e_blk[0:1, bass.ds(i * EG + j, 1)], min_val=0, max_val=NT - 1)
                    mm = pe.matmul(de[:, b % 2, j * WD:(j + 1) * WD], hot[:, b % 2, 128 * j:128 * j + 128],
                                   dtab[:, bass.ds(blk, 1), :].rearrange("p o c -> p (o c)"), start=True, stop=True)
                mm.then_inc(s_de, 1)

            def total(i, b):
                pe.wait_ge(s_here, i + 1)
                if H:
                    pe.wait_ge(s_msg, i + 1)
                else:
                    g_in(pe, i, b)
                if later(i, 1):
                    pe.wait_ge(s_added, i)
                for j in range(EG):
                    mm = pe.matmul(out[:, j, 0:WO], here[:, b % 2, j, :], msg[:, b % 2, j, :] if H else g[:, b, j, :], start=True, stop=True)
                mm.then_inc(s_out, 1)
            piped(pe, NG, [(0, of_dst), (2, total)] if H else [(1, total)])

        if H:
            @block.scalar
            def _(act):
                def weigh(i, b):
                    act.wait_ge(s_x, i + 1)
                    if later(i):
                        act.wait_ge(s_out, i - 1)
                    act.activation(msg[:, b % 2, :, D:WO], x[:, 2, :, :], ACT.Exp).then_inc(s_ex, 1)
                piped(act, NG, [(1, weigh)])

        @block.vector
        def _(v):
            v.memset(acc[:, :, :], 0.0)
            v.drain()
            if H:
                v.sem_inc(s_hot, 4)

            def one_hot(i, b):
                v.wait_ge(s_row[b], 16 * (i // 4 + 1) if isinstance(i, int) else 4 * (i - b + 4))
                if later(i):
                    v.wait_ge(s_de, i - 1)
                v.tensor_scalar(hot[:, b % 2, :], lrow[:, b, :], core.iotap[0:P, :], None, ALU.is_equal).then_inc(s_hot, 1)

            def score(i, b):
                v.wait_ge(s_de, i + 1)
                if later(i, 1):
                    v.wait_ge(s_ex, i)
                d = de[:, b % 2, 0:EG * WD].rearrange("p (g w) -> p g w", g=EG)
                e = sc[:, bass.ds(i * EG, EG), :]
                if leaky:
                    v.tensor_tensor(x[:, 0, :, :], e, d[:, :, H:2 * H], ALU.add)
                    v.drain()
                    v.scalar_tensor_tensor(out=x[:, 1, :, :], in0=x[:, 0, :, :], scalar=0.2, in1=x[:, 0, :, :], op0=ALU.mult, op1=ALU.max)
                    v.drain()
                    v.tensor_tensor(x[:, 0, :, :], x[:, 1, :, :], d[:, :, 0:H], ALU.subtract)
                else:
                    v.tensor_tensor(x[:, 0, :, :], e, d[:, :, 0:H], ALU.subtract)
                v.drain()
                v.tensor_scalar(x[:, 2, :, :], x[:, 0, :, :], 0.0, None, ALU.min).then_inc(s_x, 1)

            def weigh(i, b):
                g_in(v, i, b)
                v.wait_ge(s_ex, i + 1)
                if later(i):
                    v.wait_ge(s_out, i - 1)
                v.tensor_tensor(msg[:, b % 2, :, 0:D].rearrange("p g (h d) -> p g h d", h=H),
                                g[:, b, :, :].rearrange("p g (h d) -> p g h d", h=H),
                                msg[:, b % 2, :, D:WO].unsqueeze(3).to_broadcast([128, EG, H, D // H]), ALU.mult)
                v.drain()
                v.sem_inc(s_msg, 1)
                v.sem_inc(s_used, 1)

            def edges_here(i, b):
                if later(i):
                    v.wait_ge(s_out, i - 1)
                v.tensor_tensor(here[:, b % 2, :, :], core.iota[:, 0:P].unsqueeze(1).to_broadcast([128, EG, P]),
                                core.e_loc[:, bass.ds(i * EG, EG)].unsqueeze(2).to_broadcast([128, EG, P]), ALU.is_equal
                                ).then_inc(s_here, 1)

            def add(i, b):
                v.wait_ge(s_out, i + 1)
                for j in range(EG):
                    blk = v.value_load(core.e_blk[0:1, bass.ds(i * EG + j, 1)], min_val=0, max_val=NT - 1)
                    slot = acc[:, bass.ds(blk, 1), :].rearrange("p o c -> p (o c)")
                    v.tensor_tensor(slot, slot, out[:, j, 0:WO], ALU.add)
                    v.drain()
                v.sem_inc(s_added, 1)
            if H:
                piped(v, NG, [(0, one_hot), (1, score), (2, edges_here), (2, weigh), (3, add)])
            else:
                piped(v, NG, [(1, edges_here), (2, add)])


def move(core, name, pairs):
    with Phase(core, name) as ph:
        moved = ph.sem("moved")
        block = ph.block()

        @block.sync
        def _(sp):
            with core.nc.allow_non_contiguous_dma(reason="short rows"):
                for dst, src in pairs:
                    sp.dma_start(dst, src).then_inc(moved, 16)
            sp.wait_ge(moved, 16 * len(pairs))


def on_vector(core, name, body):
    with Phase(core, name) as ph:
        block = ph.block()

        @block.vector
        def _(v):
            body(v)
            v.drain()


def on_scalar(core, name, body):
    with Phase(core, name) as ph:
        block = ph.block()

        @block.scalar
        def _(act):
            body(act)
            act.drain()


def nodes(a):
    return a.rearrange("(t p) c -> p t c", p=P)


def flat(a):
    return a.rearrange("p t c -> p (t c)")


def normalize(core, name, src, dst, G=1, gain=None):
    C = src.shape[2]
    W = C // G
    with Phase(core, name) as ph:
        st = ph.sb("st", [P, NT * G, 6])
        mv = ph.sb("mv", [P, NT * G, 2])
        ve = ph.sb("ve", [P, NT * G])
        sd = ph.sb("sd", [P, NT * G])
        rs = ph.sb("rs", [P, NT * G])
        sq = ph.sb("sq", [P, C])
        var, root = ph.sem("var"), ph.sem("root")
        s3 = src[:, :, :].rearrange("p t (g c) -> p (t g) c", g=G)
        d3 = dst[:, :, :].rearrange("p t (g c) -> p (t g) c", g=G)
        block = ph.block()

        @block.vector
        def _(v):
            if G == 1:
                with v.Fori(0, NT) as t:
                    v.bn_stats(st[:, bass.ds(t, 1), :].rearrange("p o c -> p (o c)"), s3[:, bass.ds(t, 1), :].rearrange("p o c -> p (o c)"))
                v.drain()
                for t in range(NT):
                    v.bn_aggr(mv[:, t, :], st[:, t, :])
                v.drain()
                v.tensor_tensor(d3, s3, mv[:, :, 0:1].to_broadcast([P, NT * G, W]), ALU.subtract)
            else:
                v.tensor_reduce(ve[:, :], s3, AX.X, ALU.add)
                v.drain()
                v.tensor_scalar(mv[:, :, 0], ve[:, :], 1.0 / W, None, ALU.mult)
                v.drain()
                v.tensor_tensor(d3, s3, mv[:, :, 0:1].to_broadcast([P, NT * G, W]), ALU.subtract)
                v.drain()
                with v.Fori(0, NT) as t:
                    d = dst[:, bass.ds(t, 1), :].rearrange("p o c -> p (o c)")
                    v.tensor_tensor(sq[:, :], d, d, ALU.mult)
                    v.drain()
                    v.tensor_reduce(ve[:, bass.ds(t * G, G)], sq[:, :].rearrange("p (g c) -> p g c", g=G), AX.X, ALU.add)
                    v.drain()
                v.tensor_scalar(mv[:, :, 1], ve[:, :], 1.0 / W, None, ALU.mult)
            v.drain()
            v.tensor_scalar(ve[:, :], mv[:, :, 1], 1e-5, None, ALU.add)
            v.drain()
            v.sem_inc(var, 1)
            v.wait_ge(root, 1)
            v.reciprocal(rs[:, :], sd[:, :])
            v.drain()
            v.tensor_tensor(d3, d3, rs[:, :].unsqueeze(2).to_broadcast([P, NT * G, W]), ALU.mult)
            v.drain()
            if gain is not None:
                v.tensor_tensor(dst[:, :, :], dst[:, :, :], gain[:, 0:1, :].to_broadcast([P, NT, C]), ALU.mult)
                v.drain()
                v.tensor_tensor(dst[:, :, :], dst[:, :, :], gain[:, 1:2, :].to_broadcast([P, NT, C]), ALU.add)
                v.drain()

        @block.scalar
        def _(act):
            act.wait_ge(var, 1)
            act.activation(sd[:, :], ve[:, :], ACT.Sqrt).then_inc(root, 1)


def project(core, name, src, w, M, use, bias=None, func=None):
    mode, dst = use
    cuts = [(c, min(c + 512, M)) for c in range(0, M, 512)]
    with Phase(core, name) as ph:
        rows = ph.sb("rows", [P, 2, D])
        xt = ph.sb("xt", [128, 2, 2, P])
        pt = ph.psum("pt", [128, 512])
        out = ph.psum("out", [P, 2, len(cuts), 512])
        s_rows, s_turn, s_xt, s_mm, s_used = ph.sem("rows"), ph.sem("turned"), ph.sem("xt"), ph.sem("mm"), ph.sem("used")
        ptv = pt[:, 0:2 * P].rearrange("c (k p) -> c k p", k=2)
        block = ph.block()

        @block.gpsimd
        def _(gp):
            def take(t, b):
                if later(t):
                    gp.wait_ge(s_turn, t - 1)
                gp.tensor_copy(rows[:, b, :], src[:, bass.ds(t, 1), 0:D].rearrange("p o c -> p (o c)"))
                gp.drain()
                gp.sem_inc(s_rows, 1)
            each(gp, NT, take, peel=True)

        @block.tensor
        def _(pe):
            def turn(t, b):
                pe.wait_ge(s_rows, t + 1)
                if later(t, 1):
                    pe.wait_ge(s_xt, t)
                for k in range(2):
                    mm = pe.transpose(ptv[:, k, :], rows[:, b, 128 * k:128 * k + 128], core.ident[0:P, 0:P])
                mm.then_inc(s_turn, 1)

            def multiply(t, b):
                pe.wait_ge(s_xt, t + 1)
                if later(t):
                    pe.wait_ge(s_used, t - 1)
                for i, (c, d) in enumerate(cuts):
                    o = out[:, b, i, 0:d - c]
                    for k in range(2):
                        mm = pe.matmul(o, xt[:, b, k, :], w[:, k, c:d], start=(k == 0), stop=(k == 1 and bias is None))
                    if bias is not None:
                        mm = pe.matmul(o, core.ones[0:1, 0:P], bias[0:1, c:d], start=False, stop=True)
                mm.then_inc(s_mm, 1)
            piped(pe, NT, [(0, turn), (1, multiply)], 2)

        @block.scalar
        def _(act):
            def lay(t, b):
                act.wait_ge(s_turn, t + 1)
                if later(t):
                    act.wait_ge(s_mm, t - 1)
                act.copy(xt[:, b, :, :], ptv).then_inc(s_xt, 1)
            each(act, NT, lay, peel=True)

        @block.vector
        def _(v):
            def take(t, b):
                v.wait_ge(s_mm, t + 1)
                for i, (c, d) in enumerate(cuts):
                    to = dst[:, bass.ds(t, 1), c:d].rearrange("p o c -> p (o c)")
                    if mode == "add":
                        v.tensor_tensor(to, to, out[:, b, i, 0:d - c], ALU.add)
                    else:
                        v.tensor_copy(to, out[:, b, i, 0:d - c])
                v.drain()
                v.sem_inc(s_used, 1)
            each(v, NT, take)


def weights(core, ph, name, M, *srcs):
    w = ph.sb(name, [128, 2, M])
    pairs, c = [], 0
    for src in srcs:
        m = src.shape[1]
        pairs.append((w[:, :, c:c + m], src.rearrange("(k p) m -> p k m", p=128)))
        c += m
    move(core, f"{ph.name}_{name}_in", pairs)
    return w


def rowvec(core, ph, name, M, *srcs, parts=1):
    r = ph.sb(name, [parts, M])
    pairs, c = [], 0
    for src in srcs:
        m = src.shape[0]
        pairs.append((r[:, c:c + m], src.partition_broadcast(parts)))
        c += m
    move(core, f"{ph.name}_{name}_in", pairs)
    return r


def elu(core, name, a, tmp):
    on_vector(core, f"{name}_lo", lambda v: v.tensor_scalar(flat(tmp[:, :, :]), flat(a[:, :, :]), 0.0, None, ALU.min))
    on_scalar(core, f"{name}_ex", lambda act: act.activation(flat(tmp[:, :, :]), flat(tmp[:, :, :]), ACT.Exp))

    def hi(v):
        v.tensor_scalar(flat(a[:, :, :]), flat(a[:, :, :]), 0.0, -1.0, ALU.max, ALU.add)
        v.drain()
        v.tensor_tensor(a[:, :, :], a[:, :, :], tmp[:, :, :], ALU.add)
    on_vector(core, f"{name}_hi", hi)


def gat(core, name, src, dst, W, att_src, att_dst, b):
    H = 4
    ins = core.ins
    th, tas = core.dram(f"{name}_th", (N, D)), core.dram(f"{name}_tas", (N, H))
    with Phase(core, name) as ph:
        h = ph.sb("h", [P, NT, D])
        a_s = ph.sb("a_s", [P, NT, H])
        dtab = ph.sb("dtab", [P, NT, 2 * H])
        sc = ph.sb("sc", [128, TE, H])
        best = ph.sb("best", [P, NT, H + 1])
        acc = ph.sb("acc", [P, NT, D + H])
        sw = ph.sb("sw", [P, NT, H])
        den = ph.sb("den", [P, NT, H])
        t = ph.sb("t", [P, NT, H])
        brow = rowvec(core, ph, "b", D, ins[b], parts=P)
        arow = rowvec(core, ph, "a", 2 * D, ins[att_src].rearrange("h c -> (h c)"), ins[att_dst].rearrange("h c -> (h c)"), parts=P)
        with Phase(core, f"{name}_w") as pw:
            w = weights(core, pw, "w", D, ins[W])
            project(core, f"{name}_h", src, w, D, ("copy", h))
        with Phase(core, f"{name}_x") as px:
            tmp = px.sb("tmp", [P, NT, D])

            def terms(v):
                for k, to in ((0, a_s[:, :, :]), (1, dtab[:, :, H:2 * H])):
                    v.tensor_tensor(tmp[:, :, :], h[:, :, :], arow[:, D * k:D * k + D].unsqueeze(1).to_broadcast([P, NT, D]), ALU.mult)
                    v.drain()
                    v.tensor_reduce(to, tmp[:, :, :].rearrange("p t (h c) -> p t h c", h=H), AX.X, ALU.add)
                    v.drain()
            on_vector(core, f"{name}_terms", terms)
        move(core, f"{name}_tabs", [(nodes(th), h[:, :, :]), (nodes(tas), a_s[:, :, :])])
        edge_scores(core, f"{name}_sc", H, sc, best, tas, core.e_src)

        def greatest(v):
            v.tensor_scalar(t[:, :, 0:1], best[:, :, H:H + 1], -1.0, BIG, ALU.add, ALU.mult)
            v.drain()
            v.tensor_tensor(den[:, :, :], best[:, :, 0:H], t[:, :, 0:1].to_broadcast([P, NT, H]), ALU.add)
            v.drain()
            v.tensor_tensor(sw[:, :, :], den[:, :, :], a_s[:, :, :], ALU.max)
            v.drain()
            v.tensor_tensor(t[:, :, :], sw[:, :, :], dtab[:, :, H:2 * H], ALU.add)
            v.tensor_tensor(den[:, :, :], a_s[:, :, :], dtab[:, :, H:2 * H], ALU.add)
            v.drain()
            v.scalar_tensor_tensor(out=dtab[:, :, 0:H], in0=t[:, :, :], scalar=0.2, in1=t[:, :, :], op0=ALU.mult, op1=ALU.max)
            v.scalar_tensor_tensor(out=sw[:, :, :], in0=den[:, :, :], scalar=0.2, in1=den[:, :, :], op0=ALU.mult, op1=ALU.max)
            v.drain()
            v.tensor_tensor(t[:, :, :], sw[:, :, :], dtab[:, :, 0:H], ALU.subtract)
        on_vector(core, f"{name}_greatest", greatest)
        on_scalar(core, f"{name}_self", lambda act: act.activation(sw[:, :, :], t[:, :, :], ACT.Exp))
        edge_sums(core, f"{name}_sum", H, acc, th, core.e_src, sc, dtab, leaky=True)

        def finish(v):
            v.tensor_tensor(den[:, :, :], acc[:, :, D:D + H], sw[:, :, :], ALU.add)
            for hh in range(H):
                c = slice(64 * hh, 64 * hh + 64)
                v.tensor_tensor(h[:, :, c], h[:, :, c], sw[:, :, hh:hh + 1].to_broadcast([P, NT, 64]), ALU.mult)
            v.drain()
            v.tensor_tensor(h[:, :, :], h[:, :, :], acc[:, :, 0:D], ALU.add)
            v.reciprocal(t[:, :, :], den[:, :, :])
            v.drain()
            for hh in range(H):
                c = slice(64 * hh, 64 * hh + 64)
                v.tensor_tensor(h[:, :, c], h[:, :, c], t[:, :, hh:hh + 1].to_broadcast([P, NT, 64]), ALU.mult)
            v.drain()
            v.tensor_tensor(dst[:, :, :], h[:, :, :], brow[:, :].unsqueeze(1).to_broadcast([P, NT, D]), ALU.add)
        on_vector(core, f"{name}_finish", finish)
        elu(core, f"{name}_elu", dst, h)


def gram(core, name, kv, K, left, right, out, sums=None):
    C = K // 128
    W = kv.shape[2]
    with Phase(core, name) as ph:
        st = ph.sb("st", [P, 2, W])
        acc = ph.psum("acc", [128, 512])
        ones = ph.psum("ones", [128, 512])
        s_st, s_mm, s_all = ph.sem("st"), ph.sem("mm"), ph.sem("all")
        block = ph.block()

        @block.gpsimd
        def _(gp):
            def take(t, b):
                if later(t):
                    gp.wait_ge(s_mm, t - 1)
                gp.tensor_copy(st[:, b, :], kv[:, bass.ds(t, 1), :].rearrange("p o c -> p (o c)"))
                gp.drain()
                gp.sem_inc(s_st, 1)
            each(gp, NT, take, peel=True)

        @block.tensor
        def _(pe):
            def product(t, b):
                pe.wait_ge(s_st, t + 1)
                first, end = isinstance(t, int) and t == 0, isinstance(t, int) and t == NT - 1
                for c in range(C):
                    mm = pe.matmul(acc[:, 128 * c:128 * c + 128], st[:, b, left + 128 * c:left + 128 * c + 128],
                                   st[:, b, right + 128 * c:right + 128 * c + 128], start=first and c == 0,
                                   stop=end and c == C - 1, skip_group_check=True)
                if sums is not None:
                    mm = pe.matmul(ones[:, 0:1], st[:, b, right:right + 128], core.ones[0:P, 0:1], start=first, stop=end)
                mm.then_inc(s_mm, 1)
            each(pe, NT, product, peel=True)

        @block.vector
        def _(v):
            v.wait_ge(s_mm, NT)
            v.tensor_copy(out[:, :, :].rearrange("p c e -> p (c e)"), acc[:, 0:K])
            if sums is not None:
                v.tensor_copy(sums[:, :], ones[:, 0:1])
            v.drain()


def head_mask(core, name, mask, W, scale):
    B = 128 // W
    with Phase(core, name) as ph:
        a = ph.sb("a", [128, 128])
        b = ph.sb("b", [128, 128])
        s = ph.sem("s")
        block = ph.block()

        @block.gpsimd
        def _(gp):
            gp.memset(a[:, :], scale).then_inc(s, 1)
            gp.wait_ge(s, 1)
            gp.affine_select(out=b[:, :].rearrange("p (b w) -> p b w", b=B), in_=a[:, :].rearrange("p (b w) -> p b w", b=B),
                             compare_op=ALU.is_ge, fill=0.0, base=0, pattern=[[-W, B], [0, W]], channel_multiplier=1).then_inc(s, 1)
            gp.wait_ge(s, 2)
            gp.affine_select(out=mask[:, :].rearrange("p (b w) -> p b w", b=B), in_=b[:, :].rearrange("p (b w) -> p b w", b=B),
                             compare_op=ALU.is_ge, fill=0.0, base=W - 1, pattern=[[W, B], [0, W]], channel_multiplier=-1)


def chain(core, name, steps):
    with Phase(core, name) as ph:
        acc = ph.psum("acc", [128, 512])
        mm_s, out_s = ph.sem("mm"), ph.sem("out")
        block = ph.block()

        @block.tensor
        def _(pe):
            for i, (to, col, terms, add) in enumerate(steps):
                if i:
                    pe.wait_ge(out_s, i)
                o = acc[0:to.shape[0], 0:to.shape[1]]
                for j, (lhs, rhs) in enumerate(terms):
                    mm = pe.matmul(o, lhs, rhs, start=(j == 0), stop=(j == len(terms) - 1))
                mm.then_inc(mm_s, 1)

        @block.vector
        def _(v):
            for i, (to, col, terms, add) in enumerate(steps):
                v.wait_ge(mm_s, i + 1)
                o = acc[0:to.shape[0], 0:to.shape[1]]
                if add is not None:
                    v.tensor_tensor(to, o, add, ALU.add)
                elif col is not None:
                    v.tensor_scalar(to, o, col, None, ALU.mult)
                else:
                    v.tensor_copy(to, o)
                v.drain()
                v.sem_inc(out_s, 1)


def column_softmax(core, name, kv, W):
    with Phase(core, name) as ph:
        top = ph.sb("top", [P, W])
        one = ph.sb("one", [W, 1])
        wide = ph.sb("wide", [W, P])
        low = ph.sb("low", [P, W])
        pa = ph.psum("pa", [128, 512])
        pb = ph.psum("pb", [128, 512])
        s_v, s_p = ph.sem("v"), ph.sem("p")
        block = ph.block()

        @block.tensor
        def _(pe):
            pe.wait_ge(s_v, 1)
            pe.transpose(pa[0:W, 0:P], top[:, :], core.ident[0:P, 0:P]).then_inc(s_p, 1)
            pe.wait_ge(s_v, 2)
            pe.transpose(pb[0:P, 0:W], wide[:, :], core.ident[0:W, 0:W]).then_inc(s_p, 1)

        @block.vector
        def _(v):
            v.tensor_reduce(top[:, :], kv[:, :, 0:W].rearrange("p t d -> p d t"), AX.X, ALU.max).then_inc(s_v, 1)
            v.wait_ge(s_p, 1)
            v.tensor_reduce(one[:, :], pa[0:W, 0:P], AX.X, ALU.max)
            v.drain()
            v.tensor_scalar(wide[:, :], core.ones[0:W, 0:P], one[:, :], None, ALU.mult).then_inc(s_v, 1)
            v.wait_ge(s_p, 2)
            v.tensor_copy(low[:, :], pb[0:P, 0:W])
            v.drain()
            v.tensor_tensor(kv[:, :, 0:W], kv[:, :, 0:W], low[:, :].unsqueeze(1).to_broadcast([P, NT, W]), ALU.subtract)
            v.drain()
    on_scalar(core, f"{name}_exp", lambda act: act.activation(kv[:, :, 0:W], kv[:, :, 0:W], ACT.Exp))


def linear_mix(core, name, src, dst, mode, K, W, scale, kv_w, q_t, out_w, kv_b=None, q_b=None, out_b=None, prepare=None, sums=False):
    C = K // 128
    with Phase(core, name) as ph:
        a = ph.sb("a", [128, 2, D])
        cvec = ph.sb("cvec", [1, D])
        with Phase(core, f"{name}_kvs") as pk:
            g = pk.sb("g", [128, C, 128])
            m2 = pk.sb("m2", [128, C, D])
            mask = pk.sb("mask", [128, 128])
            qt = pk.sb("qt", [128, C, D])
            sm = pk.sb("sm", [128, 1]) if sums else None
            rsm = pk.sb("rsm", [128, 1]) if sums else None
            head_mask(core, f"{name}_mask", mask, W, scale)
            pairs = [(qt[:, :, :], q_t.rearrange("(c p) i -> p c i", p=128))]
            if q_b is not None:
                bq = pk.sb("bq", [128, C])
                pairs.append((bq[:, :], q_b.rearrange("(c p) -> p c", p=128)))
            if out_b is not None:
                bo = pk.sb("bo", [1, D])
                pairs.append((bo[:, :], out_b.partition_broadcast(1)))
            if out_w is not None:
                wo = pk.sb("wo", [128, C, D])
                pairs.append((wo[:, :, :], out_w.rearrange("(c p) i -> p c i", p=128)))
            move(core, f"{name}_in", pairs)
            with Phase(core, f"{name}_kv") as pv:
                kv = pv.sb("kv", [P, NT, 2 * K])
                with Phase(core, f"{name}_w") as pw:
                    w = weights(core, pw, "w", 2 * K, kv_w)
                    b = rowvec(core, pw, "b", 2 * K, *kv_b) if kv_b is not None else None
                    project(core, f"{name}_project", src, w, 2 * K, ("copy", kv), bias=b)
                if prepare:
                    prepare(kv)
                if out_w is not None:
                    gram(core, f"{name}_gram", kv, K, K, 0, g, sums=sm)
                else:
                    gram(core, f"{name}_gram", kv, K, 0, K, g)

            def masked(v):
                v.tensor_tensor(g[:, :, :], g[:, :, :], mask[:, :].unsqueeze(1).to_broadcast([128, C, 128]), ALU.mult)
                if sums:
                    v.reciprocal(rsm[:, :], sm[:, :])
                if out_w is None:
                    v.memset(m2[:, :, :], 0.0)
                    v.drain()
                    for c in range(C):
                        v.tensor_copy(m2[:, c, 128 * c:128 * c + 128], g[:, c, :])
            on_vector(core, f"{name}_masked", masked)
            steps = []
            if out_w is not None:
                steps += [(m2[:, c, :], rsm[:, 0:1] if sums else None, [(g[:, c, :], wo[:, c, :])], None) for c in range(C)]
            steps += [(a[:, i, :], None, [(qt[:, c, 128 * i:128 * i + 128], m2[:, c, :]) for c in range(C)], None) for i in range(2)]
            if q_b is not None:
                steps.append((cvec[:, :], None, [(bq[:, c:c + 1], m2[:, c, :]) for c in range(C)], bo[:, :] if out_b is not None else None))
            elif out_b is not None:
                steps.append((cvec[:, :], None, [(core.ones[0:1, 0:1], bo[:, :])], None))
            chain(core, f"{name}_chain", steps)
        project(core, f"{name}_out", src, a, D, (mode, dst), bias=cvec if (q_b is not None or out_b is not None) else None)


def moe(core, name, x, out, TOP, NE, F, gate_w, gate_b, w1, b1, w2, b2, func, weigh, capacity=None):
    nc, ins = core.nc, core.ins
    TT = (TOP * N + 127 * NE) // 128
    FC = F // 128
    tx = core.dram(f"{name}_tx", (N, D))
    ty = core.dram(f"{name}_ty", (TT * 128, D))
    toks = core.dram(f"{name}_toks", (TT * 128, 1), I32)
    with Phase(core, name) as ph:
        w8 = ph.sb("w8", [P, NT, TOP])
        pos = ph.sb("pos", [P, NT, TOP], I32)
        te = ph.sb("te", [1, TT], I32)
        tok = ph.sb("tok", [128, TT], I32)
        move(core, f"{name}_tab", [(nodes(tx), x[:, :, :])])
        with Phase(core, f"{name}_route") as pr:
            lg = pr.sb("lg", [P, NT, NE])
            pw8 = pr.sb("pw8", [P, NT, 8])
            ix8 = pr.sb("ix8", [P, NT, 8], U32)
            ixf = pr.sb("ixf", [P, NT, TOP])
            oh = pr.sb("oh", [P, TOP, NT, NE])
            ohs = pr.sb("ohs", [P, NT, NE])
            before = pr.sb("before", [P, NT + 1, NE])
            rank = pr.sb("rank", [P, NT, NE])
            tmp = pr.sb("tmp", [P, NT, NE])
            col = pr.sb("col", [P, NT, 1])
            kept = pr.sb("kept", [P, NT, TOP])
            posf = pr.sb("posf", [P, NT, TOP])
            tl = pr.sb("tl", [P, 3, NE])
            tstart = pr.sb("tstart", [P, NE])
            ct = pr.sb("ct", [1, TT, NE])
            io = pr.sb("io", [1, TT])
            bf = pr.sb("bf", [1, TT])
            tid = pr.sb("tid", [P, NT], I32)
            zero = pr.sb("zero", [128, TT], I32)
            with Phase(core, f"{name}_gate") as pg:
                gw = weights(core, pg, "gw", NE, gate_w)
                gb = rowvec(core, pg, "gb", NE, gate_b) if gate_b is not None else None
                project(core, f"{name}_logits", x, gw, NE, ("copy", lg), bias=gb)
            if weigh != "top logits":
                def less_top(v):
                    v.tensor_reduce(col[:, :, :], lg[:, :, :], AX.X, ALU.max)
                    v.drain()
                    v.tensor_tensor(lg[:, :, :], lg[:, :, :], col[:, :, :].to_broadcast([P, NT, NE]), ALU.subtract)
                on_vector(core, f"{name}_less", less_top)
                on_scalar(core, f"{name}_exp", lambda act: act.activation(lg[:, :, :], lg[:, :, :], ACT.Exp))

                def over_sum(v):
                    v.tensor_reduce(col[:, :, :], lg[:, :, :], AX.X, ALU.add)
                    v.drain()
                    v.reciprocal(col[:, :, :], col[:, :, :])
                    v.drain()
                    v.tensor_tensor(lg[:, :, :], lg[:, :, :], col[:, :, :].to_broadcast([P, NT, NE]), ALU.mult)
                on_vector(core, f"{name}_probs", over_sum)

            def choose(v):
                for t in range(NT):
                    v.max(pw8[:, t, :], lg[:, t, :])
                v.drain()
                for t in range(NT):
                    v.max_index(ix8[:, t, :], pw8[:, t, :], lg[:, t, :])
                v.drain()
                v.tensor_copy(ixf[:, :, :], ix8[:, :, 0:TOP])
                v.tensor_copy(w8[:, :, :], pw8[:, :, 0:TOP])
                v.drain()
                for k in range(TOP):
                    v.tensor_tensor(oh[:, k, :, :], core.iota[0:P, 0:NE].unsqueeze(1).to_broadcast([P, NT, NE]),
                                    ixf[:, :, k:k + 1].to_broadcast([P, NT, NE]), ALU.is_equal)
                if weigh == "over their sum":
                    v.tensor_tensor(col[:, :, 0], w8[:, :, 0], w8[:, :, 1], ALU.add)
                    v.drain()
                    v.tensor_scalar(col[:, :, :], col[:, :, :], 1e-12, None, ALU.max)
                    v.drain()
                    v.reciprocal(col[:, :, :], col[:, :, :])
                    v.drain()
                    v.tensor_tensor(w8[:, :, :], w8[:, :, :], col[:, :, :].to_broadcast([P, NT, TOP]), ALU.mult)
                if weigh == "top logits":
                    v.tensor_tensor(w8[:, :, :], w8[:, :, :], pw8[:, :, 0:1].to_broadcast([P, NT, TOP]), ALU.subtract)
                v.drain()
                if TOP == 2:
                    v.tensor_tensor(ohs[:, :, :], oh[:, 0, :, :], oh[:, 1, :, :], ALU.add)
                else:
                    v.tensor_copy(ohs[:, :, :], oh[:, 0, :, :])
                v.memset(before[:, 0, :], 0.0)
                v.drain()
                for t in range(NT):
                    v.tensor_tensor(before[:, t + 1, :], before[:, t, :], ohs[:, t, :], ALU.add)
                    v.drain()
            on_vector(core, f"{name}_choose", choose)
            if weigh == "top logits":
                on_scalar(core, f"{name}_wexp", lambda act: act.activation(w8[:, :, :], w8[:, :, :], ACT.Exp))

                def norm(v):
                    v.tensor_reduce(col[:, :, :], w8[:, :, :], AX.X, ALU.add)
                    v.drain()
                    v.reciprocal(col[:, :, :], col[:, :, :])
                    v.drain()
                    v.tensor_tensor(w8[:, :, :], w8[:, :, :], col[:, :, :].to_broadcast([P, NT, TOP]), ALU.mult)
                on_vector(core, f"{name}_wnorm", norm)

            with Phase(core, f"{name}_rank") as pk:
                pa = pk.psum("pa", [P, 512])
                pb = pk.psum("pb", [P, 512])
                s_mm, s_io = pk.sem("mm"), pk.sem("io")
                block = pk.block()

                @block.gpsimd
                def _(gp):
                    gp.iota(io[:, :], [[1, TT]], 0, 0, allow_small_or_imprecise_dtypes=True)
                    gp.iota(tid[:, :], [[P, NT]], 0, 1)
                    gp.memset(zero[:, :], 0)
                    gp.drain()
                    gp.sem_inc(s_io, 1)

                @block.tensor
                def _(pe):
                    pe.matmul(pa[:, 0:NT * NE], core.tri[0:P, 0:P], ohs[:, :, :].rearrange("p t e -> p (t e)"), start=True, stop=False)
                    pe.matmul(pa[:, 0:NT * NE], core.ones[0:P, 0:P], before[:, 0:NT, :].rearrange("p t e -> p (t e)"), start=False, stop=True)
                    pe.matmul(pb[:, 0:NE], core.ones[0:P, 0:P], before[:, NT, :], start=True, stop=True).then_inc(s_mm, 1)

                @block.vector
                def _(v):
                    v.wait_ge(s_mm, 1)
                    v.tensor_copy(rank[:, :, :].rearrange("p t e -> p (t e)"), pa[:, 0:NT * NE])
                    v.tensor_scalar(tl[:, 0, :], pb[:, 0:NE], 1.0 / 128, 63.75 / 128, ALU.mult, ALU.add)
                    v.memset(tl[:, 2, :], 0.0)
                    v.memset(tstart[:, 0:1], 0.0)
                    v.drain()
                    v.tensor_scalar(tl[:, 1, :], tl[:, 0, :], ROUND, -ROUND, ALU.add, ALU.add)
                    v.drain()
                    v.tensor_tensor_scan(tstart[:, 1:NE], tl[:, 1, 0:NE - 1], tl[:, 2, 0:NE - 1], 0.0, ALU.add, ALU.add)
                    if capacity is not None:
                        v.tensor_tensor(tmp[:, :, :], rank[:, :, :], oh[:, 0, :, :], ALU.mult)
                        v.drain()
                        v.tensor_reduce(col[:, :, :], tmp[:, :, :], AX.X, ALU.add)
                        v.drain()
                        v.tensor_scalar(kept[:, :, :], col[:, :, :], float(capacity), None, ALU.is_lt)
                        v.drain()
                        v.tensor_tensor(w8[:, :, :], w8[:, :, :], kept[:, :, :], ALU.mult)
                    v.drain()
                    v.tensor_scalar(tl[:, 0, :], tstart[:, :], 128.0, None, ALU.mult)
                    v.drain()
                    v.tensor_tensor(rank[:, :, :], rank[:, :, :], tl[:, 0:1, :].to_broadcast([P, NT, NE]), ALU.add)
                    for k in range(TOP):
                        v.drain()
                        v.tensor_tensor(tmp[:, :, :], rank[:, :, :], oh[:, k, :, :], ALU.mult)
                        v.drain()
                        v.tensor_reduce(posf[:, :, k:k + 1], tmp[:, :, :], AX.X, ALU.add)
                    v.drain()
                    v.tensor_copy(pos[:, :, :], posf[:, :, :])
                    v.wait_ge(s_io, 1)
                    v.tensor_tensor(ct[:, :, :], io[:, :].unsqueeze(2).to_broadcast([1, TT, NE]),
                                    tstart[0:1, :].unsqueeze(1).to_broadcast([1, TT, NE]), ALU.is_ge)
                    v.drain()
                    v.tensor_reduce(bf[:, :], ct[:, :, :], AX.X, ALU.add)
                    v.drain()
                    v.tensor_scalar(te[:, :], bf[:, :], -1.0, None, ALU.add)
                    v.drain()

            move(core, f"{name}_clear", [(toks.rearrange("(p t) o -> p (t o)", p=128), zero[:, :])])
            with Phase(core, f"{name}_scatter") as pk:
                st = pk.sb("st", [P, 2, TOP + 1], I32)
                s_st, s_sc = pk.sem("st"), [pk.sem(f"sc{b}") for b in range(2)]
                block = pk.block()

                @block.gpsimd
                def _(gp):
                    def put(t, b):
                        if later(t):
                            gp.wait_ge(s_sc[b], 8 * TOP * (t - b) if not isinstance(t, int) else 16 * TOP * (t // 2))
                        gp.tensor_copy(st[:, b, 0:TOP], pos[:, bass.ds(t, 1), :].rearrange("p o c -> p (o c)"))
                        gp.tensor_copy(st[:, b, TOP:TOP + 1], tid[:, bass.ds(t, 1)])
                        gp.drain()
                        gp.sem_inc(s_st, 1)
                        gp.wait_ge(s_st, t + 1)
                        gp.nop(nofuse=True)
                        for k in range(TOP):
                            gp.indirect_dma_start(toks, bass.IndirectOffsetOnAxis(ap=st[:, b, k:k + 1].bitcast(U32), axis=0),
                                                  st[:, b, TOP:TOP + 1], None).then_inc(s_sc[b], 16)
                    each(gp, NT, put, peel=True)
                    gp.wait_ge(s_sc[0], 16 * TOP * (NT - NT // 2))
                    gp.wait_ge(s_sc[1], 16 * TOP * (NT // 2))
            move(core, f"{name}_tokin", [(tok[:, :], toks.rearrange("(t p) o -> p (t o)", p=128))])

        with Phase(core, f"{name}_experts") as pe_:
            ix = pe_.sb("ix", [128, 2, 1], I32)
            xg = pe_.sb("xg", [128, 2, D])
            xt = pe_.sb("xt", [128, 2, 2, 128])
            w1b = pe_.sb("w1b", [128, 2, 2, F])
            w2b = pe_.sb("w2b", [128, 2, FC, D])
            b1b = pe_.sb("b1b", [128, 2, FC])
            b2b = pe_.sb("b2b", [1, 2, D])
            ht = pe_.sb("ht", [128, 2, FC, 128])
            yb = pe_.sb("yb", [128, 2, D])
            px = pe_.psum("px", [128, 512])
            phid = pe_.psum("phid", [128, 2, max(FC * 128, 512)])
            py = pe_.psum("py", [128, 2, 512])
            s_ix, s_turn, s_xt, s_up, s_ht, s_down, s_y = (pe_.sem("ix"), pe_.sem("turn"), pe_.sem("xt"), pe_.sem("up"),
                                                           pe_.sem("ht"), pe_.sem("down"), pe_.sem("y"))
            s_x = [pe_.sem(f"x{b}") for b in range(2)]
            s_w = [pe_.sem(f"w{b}") for b in range(2)]
            s_o = [pe_.sem(f"o{b}") for b in range(2)]
            block = pe_.block()

            @block.sync
            def _(sp):
                def load(t, b):
                    if later(t):
                        sp.wait_ge(s_down, t - 1)
                    e = sp.value_load(te[0:1, bass.ds(t, 1)], min_val=0, max_val=NE - 1)
                    sp.dma_start(w1b[:, b, :, :], w1[bass.ds(e, 1), :, :, :].rearrange("o p k f -> p (o k) f")).then_inc(s_w[b], 16)
                    sp.dma_start(w2b[:, b, :, :], w2[bass.ds(e, 1), :, :, :].rearrange("o p k f -> p (o k) f")).then_inc(s_w[b], 16)
                    sp.dma_start(b1b[:, b, :], b1[bass.ds(e, 1), :, :].rearrange("o p f -> p (o f)")).then_inc(s_w[b], 16)
                    sp.dma_start(b2b[:, b, :], b2[bass.ds(e, 1), :]).then_inc(s_w[b], 16)
                each(sp, TT, load, peel=True)

            def w_in(eng, t, b):
                eng.wait_ge(s_w[b], 64 * (t // 2 + 1) if isinstance(t, int) else 32 * (t - b + 2))

            @block.gpsimd
            def _(gp):
                def gather(t, b):
                    if later(t):
                        gp.wait_ge(s_turn, t - 1)
                    gp.tensor_copy(ix[:, b, :], tok[:, bass.ds(t, 1)])
                    gp.drain()
                    gp.sem_inc(s_ix, 1)
                    gp.wait_ge(s_ix, t + 1)
                    gp.nop(nofuse=True)
                    gp.indirect_dma_start(xg[:, b, :], None, tx, bass.IndirectOffsetOnAxis(ap=ix[:, b, 0:1].bitcast(U32), axis=0)
                                          ).then_inc(s_x[b], 16)
                each(gp, TT, gather, peel=True)

            @block.tensor
            def _(pe):
                def turn(t, b):
                    pe.wait_ge(s_x[b], 16 * (t // 2 + 1) if isinstance(t, int) else 8 * (t - b + 2))
                    if later(t, 1):
                        pe.wait_ge(s_xt, t)
                    for k in range(2):
                        mm = pe.transpose(px[:, 128 * k:128 * k + 128], xg[:, b, 128 * k:128 * k + 128], core.ident[:, :])
                    mm.then_inc(s_turn, 1)

                def up(t, b):
                    w_in(pe, t, b)
                    pe.wait_ge(s_xt, t + 1)
                    if later(t):
                        pe.wait_ge(s_ht, t - 1)
                    for f in range(FC):
                        for k in range(2):
                            mm = pe.matmul(phid[:, b, 128 * f:128 * f + 128], w1b[:, b, k, 128 * f:128 * f + 128], xt[:, b, k, :],
                                           start=(k == 0), stop=(k == 1))
                    mm.then_inc(s_up, 1)

                def down(t, b):
                    pe.wait_ge(s_ht, t + 1)
                    if later(t):
                        pe.wait_ge(s_y, t - 1)
                    for f in range(FC):
                        pe.matmul(py[:, b, 0:D], ht[:, b, f, :], w2b[:, b, f, :], start=(f == 0), stop=False)
                    pe.matmul(py[:, b, 0:D], core.ones[0:1, :], b2b[:, b, :], start=False, stop=True).then_inc(s_down, 1)
                piped(pe, TT, [(0, turn), (1, up), (2, down)], 2)

            @block.vector
            def _(v):
                def lay(t, b):
                    v.wait_ge(s_turn, t + 1)
                    if later(t):
                        v.wait_ge(s_up, t - 1)
                    v.tensor_copy(xt[:, b, :, :].rearrange("p k c -> p (k c)"), px[:, 0:256]).then_inc(s_xt, 1)

                def result(t, b):
                    v.wait_ge(s_down, t + 1)
                    if later(t):
                        v.wait_ge(s_o[b], 8 * (t - b) if not isinstance(t, int) else 16 * (t // 2))
                    v.tensor_copy(yb[:, b, :], py[:, b, 0:D]).then_inc(s_y, 1)
                piped(v, TT, [(0, lay), (2, result)], 2)

            @block.scalar
            def _(act):
                def middle(t, b):
                    act.wait_ge(s_up, t + 1)
                    w_in(act, t, b)
                    if later(t):
                        act.wait_ge(s_down, t - 1)
                    for f in range(FC):
                        act.activation(ht[:, b, f, :], phid[:, b, 128 * f:128 * f + 128], func, bias=b1b[:, b, f:f + 1])
                    act.drain()
                    act.sem_inc(s_ht, 1)

                def put(t, b):
                    act.wait_ge(s_y, t + 1)
                    act.dma_start(ty[bass.ds(t * 128, 128), :], yb[:, b, :]).then_inc(s_o[b], 16)
                piped(act, TT, [(0, middle), (2, put)], 2)
                act.wait_ge(s_o[0], 16 * (TT - TT // 2))
                act.wait_ge(s_o[1], 16 * (TT // 2))

        with Phase(core, f"{name}_combine") as pc:
            ix = pc.sb("ix", [P, 2, TOP], I32)
            y = pc.sb("y", [P, 2, TOP, D])
            part = pc.sb("part", [P, 2, D])
            s_ix, s_used = pc.sem("ix"), pc.sem("used")
            s_in = [pc.sem(f"in{b}") for b in range(2)]
            block = pc.block()

            @block.gpsimd
            def _(gp):
                def gather(t, b):
                    if later(t):
                        gp.wait_ge(s_used, t - 1)
                    gp.tensor_copy(ix[:, b, :], pos[:, bass.ds(t, 1), :].rearrange("p o c -> p (o c)"))
                    gp.drain()
                    gp.sem_inc(s_ix, 1)
                    gp.wait_ge(s_ix, t + 1)
                    gp.nop(nofuse=True)
                    for k in range(TOP):
                        gp.indirect_dma_start(y[:, b, k, :], None, ty, bass.IndirectOffsetOnAxis(ap=ix[:, b, k:k + 1].bitcast(U32), axis=0)
                                              ).then_inc(s_in[b], 16)
                each(gp, NT, gather, peel=True)

            @block.vector
            def _(v):
                def add(t, b):
                    v.wait_ge(s_in[b], 16 * TOP * (t // 2 + 1) if isinstance(t, int) else 8 * TOP * (t - b + 2))
                    to = out[:, bass.ds(t, 1), :].rearrange("p o c -> p (o c)")
                    w = [w8[:, bass.ds(t, 1), k:k + 1].rearrange("p o c -> p (o c)") for k in range(TOP)]
                    if TOP == 1:
                        v.tensor_tensor(to, y[:, b, 0, :], w[0].to_broadcast([P, D]), ALU.mult)
                    else:
                        v.tensor_tensor(part[:, 0, :], y[:, b, 0, :], w[0].to_broadcast([P, D]), ALU.mult)
                        v.tensor_tensor(part[:, 1, :], y[:, b, 1, :], w[1].to_broadcast([P, D]), ALU.mult)
                        v.drain()
                        v.tensor_tensor(to, part[:, 0, :], part[:, 1, :], ALU.add)
                    v.drain()
                    v.sem_inc(s_used, 1)
                each(v, NT, add)


def add_to(core, name, x, *parts):
    def body(v):
        for p in parts:
            v.tensor_tensor(x[:, :, :], x[:, :, :], p[:, :, :], ALU.add)
            v.drain()
    on_vector(core, name, body)


def layer0(core, x, xn):
    ins = core.ins
    normalize(core, "l0_norm", x, xn)
    with Phase(core, "l0") as ph:
        g = ph.sb("g", [P, NT, D])
        gat(core, "l0_gat1", xn, g, "L0_gnn_W1", "L0_gnn_att_src1", "L0_gnn_att_dst1", "L0_gnn_b1")
        gat(core, "l0_gat2", g, g, "L0_gnn_W2", "L0_gnn_att_src2", "L0_gnn_att_dst2", "L0_gnn_b2")
        add_to(core, "l0_add", x, g)
    linear_mix(core, "l0_mix", xn, x, "add", D, 32, 1.0 / N, ins["L0_mix_kv"], ins["L0_mix_Wq"], ins["L0_mix_WfcT"],
               kv_b=(ins["L0_mix_bk"], ins["L0_mix_bv"]), q_b=ins["L0_mix_bq"], out_b=ins["L0_mix_bfc"])


def layer0_ffn(core, x, xn):
    ins = core.ins
    normalize(core, "f0_norm", x, xn)
    with Phase(core, "f0") as ph:
        g = ph.sb("g", [P, NT, D])
        moe(core, "f0_moe", xn, g, 2, 8, 512, ins["L0_ffn_gate_w"], ins["L0_ffn_gate_b"], ins["L0_ffn_W1"], ins["L0_ffn_b1"],
            ins["L0_ffn_W2"], ins["L0_ffn_b2"], ACT.Gelu, "probs")
        add_to(core, "f0_add", x, g)


def layer1(core, x, xn):
    ins = core.ins
    normalize(core, "l1_norm", x, xn)
    table = core.dram("l1_table", (N, D))
    with Phase(core, "l1") as ph:
        g = ph.sb("g", [P, NT, D])
        with Phase(core, "l1_w") as pw:
            w = weights(core, pw, "w", D, ins["L1_gnn_W2T"])
            project(core, "l1_rows", xn, w, D, ("copy", g))
        move(core, "l1_tab", [(nodes(table), g[:, :, :])])
        edge_sums(core, "l1_sum", 0, g, table, core.e_src)
        with Phase(core, "l1_v") as pw:
            w = weights(core, pw, "w", D, ins["L1_gnn_W1T"])
            project(core, "l1_self", xn, w, D, ("add", g))

        def relu_add(v):
            v.scalar_tensor_tensor(out=x[:, :, :], in0=g[:, :, :], scalar=0.0, in1=x[:, :, :], op0=ALU.max, op1=ALU.add)
        on_vector(core, "l1_relu", relu_add)
        with Phase(core, "l1_gain") as pg:
            gain = pg.sb("gain", [P, 2, 512])
            small = pg.sb("small", [P, 4, 32])
            move(core, "l1_gains", [(small[:, i, :], ins[f"L1_mix_{n}"].partition_broadcast(P))
                                    for i, n in enumerate(("kln_g", "vln_g", "kln_b", "vln_b"))])

            def spread(v):
                for i in range(4):
                    v.tensor_copy(gain[:, i // 2, 256 * (i % 2):256 * (i % 2) + 256].rearrange("p (h c) -> p h c", c=32),
                                  small[:, i:i + 1, :].to_broadcast([P, 8, 32]))
            on_vector(core, "l1_spread", spread)
            linear_mix(core, "l1_mix", xn, g, "copy", D, 32, 1.0 / N, ins["L1_mix_kv"], ins["L1_mix_WqT"], None,
                       kv_b=(ins["L1_mix_kv_b"],), q_b=ins["L1_mix_q_b"],
                       prepare=lambda kv: normalize(core, "l1_kvn", kv, kv, G=16, gain=gain))
        add_to(core, "l1_ret", g, xn)
        with Phase(core, "l1_h") as ph2:
            h = ph2.sb("h", [P, NT, D])
            w = weights(core, ph2, "w", D, ins["L1_mix_w1"])
            w2 = weights(core, ph2, "w2", D, ins["L1_mix_w2"])
            b1 = rowvec(core, ph2, "b1", D, ins["L1_mix_b1"])
            b2 = rowvec(core, ph2, "b2", D, ins["L1_mix_b2"])
            project(core, "l1_up", g, w, D, ("copy", h), bias=b1)
            on_scalar(core, "l1_gelu", lambda act: act.activation(h[:, :, :], h[:, :, :], ACT.Gelu))
            project(core, "l1_down", h, w2, D, ("add", x), bias=b2)
        add_to(core, "l1_bias", x, xn)


def layer1_ffn(core, x, xn):
    ins = core.ins
    normalize(core, "f1_norm", x, xn)
    with Phase(core, "f1") as ph:
        g = ph.sb("g", [P, NT, D])
        moe(core, "f1_moe", xn, g, 1, 8, 1024, ins["L1_ffn_gate_w"], ins["L1_ffn_gate_b"], ins["L1_ffn_w1"], ins["L1_ffn_b1"],
            ins["L1_ffn_w2"], ins["L1_ffn_b2"], ACT.Relu, "probs", capacity=-(-5 * N // 4 // 8) if (5 * N) % 32 == 0 else 5 * N // 32 + 1)
        with Phase(core, "f1_fix") as pf:
            m = pf.sb("m", [P, NT, D], I32)
            c = pf.sb("c", [P, 3])

            def finite(v):
                for i, val in enumerate((0.0, 1e4, -1e4)):
                    v.memset(c[:, i:i + 1], val)
                for i, (op, bound) in enumerate(((ALU.not_equal, None), (ALU.is_gt, 3.4028234663852886e38), (ALU.is_lt, -3.4028234663852886e38))):
                    if bound is None:
                        v.tensor_tensor(m[:, :, :], g[:, :, :], g[:, :, :], op)
                    else:
                        v.tensor_scalar(m[:, :, :], g[:, :, :], bound, None, op)
                    v.drain()
                    v.copy_predicated(g[:, :, :], m[:, :, :], c[:, i:i + 1].unsqueeze(1).to_broadcast([P, NT, D]))
                    v.drain()
            on_vector(core, "f1_finite", finite)
        add_to(core, "f1_add", x, g)


def layer2(core, x, xn):
    ins = core.ins
    normalize(core, "l2_norm", x, xn)
    table, score = core.dram("l2_table", (N, D)), core.dram("l2_score", (N, 1))
    with Phase(core, "l2") as ph:
        h = ph.sb("h", [P, NT, D])
        acc = ph.sb("acc", [P, NT, D + 1])
        sc = ph.sb("sc", [128, TE, 1])
        best = ph.sb("best", [P, NT, 2])
        hs = ph.sb("hs", [P, NT, 1])
        with Phase(core, "l2_w") as pw:
            w = weights(core, pw, "w", D, ins["L2_gnn_WnT"])
            b = rowvec(core, pw, "b", D, ins["L2_gnn_bn"])
            project(core, "l2_rows", xn, w, D, ("copy", h), bias=b)
        with Phase(core, "l2_x") as px:
            tmp = px.sb("tmp", [P, NT, D])
            arow = rowvec(core, px, "a", D, ins["L2_gnn_attn"].rearrange("a b c -> (a b c)"), parts=P)

            def term(v):
                v.tensor_tensor(tmp[:, :, :], h[:, :, :], arow[:, :].unsqueeze(1).to_broadcast([P, NT, D]), ALU.mult)
                v.drain()
                v.tensor_reduce(hs[:, :, :], tmp[:, :, :], AX.X, ALU.add)
            on_vector(core, "l2_term", term)
        move(core, "l2_tabs", [(nodes(table), h[:, :, :]), (nodes(score), hs[:, :, :])])
        edge_scores(core, "l2_sc", 1, sc, best, score, core.e_src, ee=True)
        on_vector(core, "l2_best", lambda v: v.tensor_copy(hs[:, :, :], best[:, :, 0:1]))
        edge_sums(core, "l2_sum", 1, acc, table, core.e_src, sc, hs)

        def finish(v):
            v.tensor_scalar(hs[:, :, :], acc[:, :, D:D + 1], 1e-16, None, ALU.add)
            v.drain()
            v.reciprocal(hs[:, :, :], hs[:, :, :])
            v.drain()
            v.tensor_tensor(h[:, :, :], acc[:, :, 0:D], hs[:, :, :].to_broadcast([P, NT, D]), ALU.mult)
            v.drain()
            v.scalar_tensor_tensor(out=x[:, :, :], in0=h[:, :, :], scalar=0.0, in1=x[:, :, :], op0=ALU.max, op1=ALU.add)
        on_vector(core, "l2_finish", finish)
    linear_mix(core, "l2_mix", xn, x, "add", 128, 32, 32.0 ** -0.5, ins["L2_mix_kv"], ins["L2_mix_WqT"], ins["L2_mix_W_out"],
               out_b=ins["L2_mix_b_out"], prepare=lambda kv: column_softmax(core, "l2_soft", kv, 128), sums=True)


def layer2_ffn(core, x, xn):
    ins = core.ins
    normalize(core, "f2_norm", x, xn)
    with Phase(core, "f2") as ph:
        g = ph.sb("g", [P, NT, D])
        moe(core, "f2_moe", xn, g, 2, 16, 512, ins["L2_ffn_gate_w"], ins["L2_ffn_gate_b"], ins["L2_ffn_w1"], ins["L2_ffn_b1"],
            ins["L2_ffn_w2"], ins["L2_ffn_b2"], ACT.Relu, "top logits")
        add_to(core, "f2_add", g, xn)
        gain = ph.sb("gain", [P, 2, D])
        move(core, "f2_gains", [(gain[:, 0, :], ins["L2_ffn_gamma"].partition_broadcast(P)), (gain[:, 1, :], ins["L2_ffn_beta"].partition_broadcast(P))])
        normalize(core, "f2_out", g, g, gain=gain)
        add_to(core, "f2_add2", x, g)


def hgt(core, name, l, src, dst):
    ins = core.ins
    H, L = 32, 2
    tk, tm = core.dram(f"{name}_tk", (N, 2 * D)), core.dram(f"{name}_tm", (N, 2 * D))
    with Phase(core, name) as ph:
        alpha = ph.sb("alpha", [128, 2])
        wk = ph.sb("wk", [128, 2, 2 * D])
        wm = ph.sb("wm", [128, 2, 2 * D])
        with Phase(core, f"{name}_mats") as pm:
            m8 = pm.sb("m8", [128, 2, 128])
            tt = pm.sb("tt", [128, 2, 2, 2, 8])
            wt = pm.sb("wt", [128, 2, 2, D])
            pri = pm.sb("pri", [16, 4])
            pcol = pm.sb("pcol", [128, 4])
            hot = pm.sb("hot", [16, 128])
            bd = pm.sb("bd", [128, 2, 2, 2, 128])
            head_mask(core, f"{name}_m8a", m8[:, 0, :], 8, 8.0 ** -0.5)
            head_mask(core, f"{name}_m8b", m8[:, 1, :], 8, 1.0)
            move(core, f"{name}_in", [(alpha[:, 0:1], ins["L3_gnn_skip"][l:l + 1].partition_broadcast(128))]
                 + [(pri[:, 2 * c:2 * c + 2], ins["L3_gnn_pri"][l, 16 * c:16 * c + 16, :]) for c in range(2)]
                 + [(tt[:, i, t, c, :], ins[n][l, t, 128 * c:128 * c + 128, :]) for i, n in enumerate(("L3_gnn_Watt", "L3_gnn_Wmsg"))
                    for t in range(2) for c in range(2)]
                 + [(wt[:, i, :, :], ins[n][l].rearrange("(c p) i -> p c i", p=128)) for i, n in enumerate(("L3_gnn_WkT", "L3_gnn_WvT"))])
            with Phase(core, f"{name}_hot") as p2:
                block = p2.block()

                @block.gpsimd
                def _(gp):
                    gp.affine_select(out=hot[:, :].rearrange("h (b w) -> h b w", w=8), in_=core.ones[0:16, :].rearrange("h (b w) -> h b w", w=8),
                                     compare_op=ALU.is_equal, fill=0.0, base=0, pattern=[[-1, 16], [0, 8]], channel_multiplier=1)
                    gp.drain()
            on_scalar(core, f"{name}_alpha", lambda act: act.activation(alpha[:, 0:1], alpha[:, 0:1], ACT.Sigmoid))
            chain(core, f"{name}_pcol", [(pcol[:, :], None, [(hot[:, :], pri[:, :])], None)])

            def spread(v):
                v.tensor_scalar(alpha[:, 1:2], alpha[:, 0:1], -1.0, 1.0, ALU.mult, ALU.add)
                for i in range(2):
                    for t in range(2):
                        for c in range(2):
                            v.tensor_tensor(bd[:, i, t, c, :].rearrange("p (b f) -> p b f", f=8), m8[:, i, :].rearrange("p (b f) -> p b f", f=8),
                                            tt[:, i, t, c, :].unsqueeze(1).to_broadcast([128, 16, 8]), ALU.mult)
                v.drain()
                for t in range(2):
                    for c in range(2):
                        v.tensor_scalar(bd[:, 0, t, c, :], bd[:, 0, t, c, :], pcol[:, 2 * c + t:2 * c + t + 1], None, ALU.mult)
            on_vector(core, f"{name}_spread", spread)
            chain(core, f"{name}_prod", [(w[:, r, D * t + 128 * c:D * t + 128 * c + 128], None, [(wt[:, i, c, 128 * r:128 * r + 128], bd[:, i, t, c, :])], None)
                                         for i, w in enumerate((wk, wm)) for t in range(2) for c in range(2) for r in range(2)])
        for n, w, tab in (("k", wk, tk), ("m", wm, tm)):
            with Phase(core, f"{name}_{n}") as pt:
                big = pt.sb("big", [P, NT, 2 * D])
                project(core, f"{name}_{n}p", src, w, 2 * D, ("copy", big))
                move(core, f"{name}_{n}t", [(nodes(tab), big[:, :, :])])
        typed = [t.rearrange("n (t c) -> (n t) c", t=2) for t in (tk, tm)]
        with Phase(core, f"{name}_edges") as pe:
            sc = pe.sb("sc", [128, TE, H])
            best = pe.sb("best", [P, NT, H + 1])
            with Phase(core, f"{name}_q") as pq:
                q = pq.sb("q", [P, NT, D])
                with Phase(core, f"{name}_qw") as pw:
                    w = weights(core, pw, "w", D, ins["L3_gnn_Wq"][l])
                    project(core, f"{name}_qp", src, w, D, ("copy", q))
                edge_scores(core, f"{name}_sc", H, sc, best, typed[0], core.e_srct, q=q)
            acc = pe.sb("acc", [P, NT, D + H])
            edge_sums(core, f"{name}_sum", H, acc, typed[1], core.e_srct, sc, best[:, :, 0:H])

            def finish(v):
                v.tensor_scalar(best[:, :, 0:H], acc[:, :, D:D + H], 1e-30, None, ALU.max)
                v.drain()
                v.reciprocal(best[:, :, 0:H], best[:, :, 0:H])
                v.drain()
                with v.Fori(0, NT) as t:
                    a = acc[:, bass.ds(t, 1), 0:D].rearrange("p o (h c) -> p (o h) c", h=H)
                    v.tensor_tensor(a, a, best[:, bass.ds(t, 1), 0:H].rearrange("p o h -> p (o h)").unsqueeze(2).to_broadcast([P, H, D // H]), ALU.mult)
                v.drain()
                v.tensor_scalar(src[:, :, :], src[:, :, :], alpha[0:P, 1:2], None, ALU.mult)
            on_vector(core, f"{name}_finish", finish)
            with Phase(core, f"{name}_wa") as pw:
                w = weights(core, pw, "w", D, ins["L3_gnn_Wa"][l])
                on_vector(core, f"{name}_scale", lambda v: v.tensor_scalar(w[:, :, :], w[:, :, :], alpha[:, 0:1], None, ALU.mult))
                project(core, f"{name}_out", acc, w, D, ("add", src))
            on_vector(core, f"{name}_to", lambda v: v.tensor_copy(dst[:, :, :], src[:, :, :]))


def layer3(core, x, xn):
    ins = core.ins
    normalize(core, "l3_norm", x, xn)
    with Phase(core, "l3") as ph:
        kept = core.dram("l3_x", (N, D))
        move(core, "l3_keep", [(nodes(kept), x[:, :, :])])
        on_vector(core, "l3_copy", lambda v: v.tensor_copy(x[:, :, :], xn[:, :, :]))
        for l in range(2):
            hgt(core, f"l3_hgt{l}", l, x, x)
        g = ph.sb("g", [P, NT, D])
        move(core, "l3_back", [(g[:, :, :], nodes(kept))])
        add_to(core, "l3_add", x, g)
    linear_mix(core, "l3_mix", xn, x, "add", 512, 64, 1.0 / N, ins["L3_mix_kv"], ins["L3_mix_Wq"], ins["L3_mix_WoutT"],
               out_b=ins["L3_mix_b_out"], prepare=lambda kv: normalize(core, "l3_kvn", kv, kv, G=16))


def layer3_ffn(core, x, xn):
    ins = core.ins
    normalize(core, "f3_norm", x, xn)
    with Phase(core, "f3") as ph:
        g = ph.sb("g", [P, NT, D])
        moe(core, "f3_moe", xn, g, 2, 8, 256, ins["L3_ffn_routerT"], None, ins["L3_ffn_w1"], ins["L3_ffn_b1"],
            ins["L3_ffn_w2"], ins["L3_ffn_b2"], ACT.Gelu, "over their sum")
        add_to(core, "f3_add", x, g, xn)


LAYERS = [layer0, layer0_ffn, layer1, layer1_ffn, layer2, layer2_ffn, layer3, layer3_ffn]


def build(nc, ins, out, layers=LAYERS, x_in=None):
    core = Core(nc, ins, out)
    with Phase(core, "keep") as keep:
        x = keep.sb("x", [P, NT, D])
        xn = keep.sb("xn", [P, NT, D])
        constants(core, keep)
        move(core, "x_in", [(x[:, :, :], nodes(ins["x"]))])
        sort_edges(core, keep)
        for layer in layers:
            layer(core, x, xn)
        move(core, "x_out", [(nodes(out), x[:, :, :])])


def lay_out(i):
    import numpy as np

    a = {k: np.asarray(v) for k, v in i.items()}
    t = lambda n: np.ascontiguousarray(a[n].T)
    put = {k: a[k] for k in (
        "x", "src", "dst", "edge_attr_128", "edge_type_2", "L0_gnn_W1", "L0_gnn_att_src1", "L0_gnn_att_dst1", "L0_gnn_b1",
        "L0_gnn_W2", "L0_gnn_att_src2", "L0_gnn_att_dst2", "L0_gnn_b2", "L0_mix_Wq", "L0_mix_bq", "L0_mix_bk", "L0_mix_bv", "L0_mix_bfc",
        "L0_ffn_gate_w", "L0_ffn_gate_b", "L0_ffn_b2", "L1_mix_kln_g", "L1_mix_kln_b", "L1_mix_vln_g", "L1_mix_vln_b",
        "L1_mix_w1", "L1_mix_b1", "L1_mix_w2", "L1_mix_b2", "L1_ffn_gate_w", "L1_ffn_gate_b", "L1_ffn_b2", "L2_gnn_bn", "L2_gnn_We",
        "L2_gnn_be", "L2_gnn_attn", "L2_mix_W_out", "L2_mix_b_out", "L2_ffn_gate_w", "L2_ffn_gate_b", "L2_ffn_b2", "L2_ffn_gamma",
        "L2_ffn_beta", "L3_gnn_Wq", "L3_gnn_Wa", "L3_gnn_pri", "L3_gnn_skip", "L3_mix_b_out", "L3_ffn_b2")}
    put["L0_mix_kv"] = np.concatenate([t("L0_mix_Wk"), t("L0_mix_Wv")], 1)
    put["L0_mix_WfcT"] = t("L0_mix_Wfc")
    put["L1_gnn_W1T"], put["L1_gnn_W2T"] = t("L1_gnn_W1"), t("L1_gnn_W2")
    w = a["L1_mix_w_qkv"].reshape(256, 8, 3, 32).transpose(0, 2, 1, 3).reshape(256, 768)
    b = a["L1_mix_b_qkv"].reshape(8, 3, 32).transpose(1, 0, 2).reshape(768)
    put["L1_mix_kv"], put["L1_mix_WqT"] = np.ascontiguousarray(w[:, 256:]), np.ascontiguousarray(w[:, :256].T)
    put["L1_mix_kv_b"], put["L1_mix_q_b"] = b[256:].copy(), b[:256].copy()
    put["L2_gnn_WnT"] = t("L2_gnn_Wn")
    put["L2_mix_kv"] = np.ascontiguousarray(a["L2_mix_W_qkv"][:, 128:])
    put["L2_mix_WqT"] = np.ascontiguousarray(a["L2_mix_W_qkv"][:, :128].T)
    for n in ("Wk", "Wv"):
        put[f"L3_gnn_{n}T"] = np.ascontiguousarray(a[f"L3_gnn_{n}"].transpose(0, 2, 1))
    for n in ("Watt", "Wmsg"):
        put[f"L3_gnn_{n}"] = np.ascontiguousarray(a[f"L3_gnn_{n}"].transpose(0, 2, 1, 3, 4).reshape(2, 2, 256, 8))
    put["L3_mix_Wq"] = np.ascontiguousarray(a["L3_mix_w_qkv"][:512])
    put["L3_mix_kv"] = np.ascontiguousarray(a["L3_mix_w_qkv"][512:].T)
    put["L3_mix_WoutT"] = t("L3_mix_w_out")
    put["L3_ffn_routerT"] = t("L3_ffn_router_w")
    for n, u, d in (("L0_ffn", "W1", "W2"), ("L1_ffn", "w1", "w2"), ("L2_ffn", "w1", "w2"), ("L3_ffn", "w1", "w2")):
        for k, w in ((u, a[f"{n}_{u}"]), (d, a[f"{n}_{d}"])):
            e, r, c = w.shape
            put[f"{n}_{k}"] = np.ascontiguousarray(w.reshape(e, r // 128, 128, c).transpose(0, 2, 1, 3))
        b = a[f"{n}_b1"]
        put[f"{n}_b1"] = np.ascontiguousarray(b.reshape(b.shape[0], -1, 128).transpose(0, 2, 1))
    return put


def kernel(**inputs):
    import concourse.bacc as _bacc
    from concourse.bass_utils import run_bass_kernel_spmd as _run

    nc = _bacc.Bacc("TRN2", target_bir_lowering=False, num_devices=1)
    arrays, ins = {}, {}
    for name, a in lay_out(inputs).items():
        arrays[f"in_{name}"] = a
        ins[name] = nc.dram_tensor(f"in_{name}", a.shape, mybir.dt.from_np(a.dtype), kind="ExternalInput").ap()
    out = nc.dram_tensor("out", (N, D), F32, kind="ExternalOutput").ap()
    build(nc, ins, out)
    return _run(nc, [arrays], core_ids=[0]).results[0]["out"]
```

```python
from contextlib import ExitStack

import concourse.bass as bass
from concourse import mybir

F32 = mybir.dt.float32
BF16 = mybir.dt.bfloat16
I32 = mybir.dt.int32
U32 = mybir.dt.uint32
ALU = mybir.AluOpType
ACT = mybir.ActivationFunctionType
AX = mybir.AxisListType

N, D, E = 3125, 256, 50000
P = 125
NT = N // P
ER = E // P
EG = 4
TE = 416
assert E // 128 + NT <= TE and TE % EG == 0
NG = TE // EG
GE = EG * 128
BIG = 1.0e30
ROUND = 12582912.0


def each(eng, count, body, unroll=2, peel=False):
    for i in range(unroll if peel else 0):
        body(i, i)
    with eng.Fori(int(peel), count // unroll) as k:
        for u in range(unroll):
            body(unroll * k + u, u)
    for i in range(count - count % unroll, count):
        body(i, i % unroll)


def later(i, n=2):
    return not isinstance(i, int) or i >= n


def piped(eng, count, stages, unroll=4):
    first = -(-(max(lag for lag, _ in stages) + unroll) // unroll) * unroll

    def step(i, u):
        for lag, body in stages:
            if not isinstance(i, int) or 0 <= i - lag < count:
                body(i - lag, (u - lag) % unroll)
    for i in range(first):
        step(i, i % unroll)
    last = count // unroll * unroll
    with eng.Fori(first // unroll, last // unroll) as k:
        for u in range(unroll):
            step(unroll * k + u, u)
    for i in range(last, count + max(lag for lag, _ in stages)):
        step(i, i % unroll)


class Core:

    def __init__(self, nc, ins, out):
        self.nc, self.ins, self.out = nc, ins, out
        self.spent = []

    def dram(self, name, shape, dt=F32):
        return self.nc.dram_tensor(name, shape, dt, kind="Internal").ap()


class Phase:

    def __init__(self, core, name):
        self.core, self.nc, self.name = core, core.nc, name

    def __enter__(self):
        self.ctx = ExitStack()
        self.sems = []
        if len(self.core.spent) > 90:
            self.nc.all_engine_barrier()
            self.nc.clear_and_free_semaphores(self.core.spent)
            self.nc.all_engine_barrier()
            self.core.spent = []
        return self

    def __exit__(self, *a):
        self.ctx.close()
        self.core.spent += self.sems

    def sb(self, name, shape, dt=F32):
        return self.ctx.enter_context(self.nc.sbuf_tensor(f"{self.name}_{name}", shape, dt))

    def psum(self, name, shape, dt=F32):
        return self.ctx.enter_context(self.nc.psum_tensor(f"{self.name}_{name}", shape, dt))

    def sem(self, name):
        self.sems.append(self.nc.alloc_semaphore(f"{self.name}_{name}"))
        return self.sems[-1]

    def block(self):
        return self.ctx.enter_context(self.nc.Block())


def constants(core, keep):
    core.ident = keep.sb("ident", [128, 128])
    core.ones = keep.sb("ones", [128, 128])
    core.tri = keep.sb("tri", [128, 128])
    core.low = keep.sb("low", [128, 128])
    core.iota = keep.sb("iota", [128, 128])
    core.iotap = keep.sb("iotap", [128, 1])
    with Phase(core, "const") as ph:
        made = ph.sem("made")
        block = ph.block()

        @block.gpsimd
        def _(gp):
            gp.memset(core.ones[:, :], 1.0).then_inc(made, 1)
            gp.iota(core.iota[:, :], [[1, 128]], 0, 0, allow_small_or_imprecise_dtypes=True).then_inc(made, 1)
            gp.iota(core.iotap[:, :], [[0, 1]], 0, 1, allow_small_or_imprecise_dtypes=True).then_inc(made, 1)
            gp.wait_ge(made, 3)
            gp.affine_select(out=core.ident[:, :], in_=core.ones[:, :], compare_op=ALU.is_equal, fill=0.0,
                             base=0, pattern=[[1, 128]], channel_multiplier=-1)
            gp.affine_select(out=core.tri[:, :], in_=core.ones[:, :], compare_op=ALU.is_gt, fill=0.0,
                             base=0, pattern=[[1, 128]], channel_multiplier=-1)
            gp.affine_select(out=core.low[:, :], in_=core.ones[:, :], compare_op=ALU.is_gt, fill=0.0,
                             base=0, pattern=[[-1, 128]], channel_multiplier=1)


def sort_edges(core, keep):
    ins = core.ins
    core.e_src = keep.sb("e_src", [128, TE], I32)
    core.e_srct = keep.sb("e_srct", [128, TE], I32)
    core.e_loc = keep.sb("e_loc", [128, TE])
    core.e_last = keep.sb("e_last", [128, TE])
    core.e_ee = keep.sb("e_ee", [128, TE])
    core.e_blk = keep.sb("e_blk", [1, TE], I32)
    core.locrow = core.dram("locrow", (TE * 128,))
    core.rstrow = core.dram("rstrow", (TE * 128,))
    dstrows = core.dram("dstrows", (ER, P))
    lorows = core.dram("lorows", (ER, P))
    recs = core.dram("recs", (TE * 128, 4), I32)
    dsts = core.dram("dsts", (TE * 128 + 2,))
    G = 8
    NGU = ER // G

    with Phase(core, "prep") as keep2:
        dstc = keep2.sb("dst", [P, ER])
        hic = keep2.sb("hi", [P, ER])
        loc = keep2.sb("lo", [P, ER])
        rec = keep2.sb("rec", [P, ER, 4], I32)
        start = keep2.sb("start", [P, NT])

        with Phase(core, "digits") as ph:
            si = ph.sb("si", [P, ER], I32)
            di = ph.sb("di", [P, ER], I32)
            ti = ph.sb("ti", [P, ER], I32)
            tmp = ph.sb("tmp", [P, ER])
            sf = ph.sb("sf", [P, ER])
            tf = ph.sb("tf", [P, ER])
            att = ph.sb("att", [128, 2])
            attb = ph.sb("attb", [128, 2, P])
            web = ph.sb("web", [128, 2, 129])
            wea = ph.sb("wea", [P, 129])
            ea = ph.sb("ea", [P, 2, G, 128])
            prod = ph.sb("prod", [P, G, 128])
            ee = ph.sb("ee", [P, ER])
            rowsb = ph.sb("rowsb", [100, 2, 4, P])
            pad = ph.sb("pad", [128, TE, 4], I32)
            pw = ph.psum("pw", [P, 129])
            pt = ph.psum("pt", [100, 4, P])
            loaded, attr_in = ph.sem("loaded"), [ph.sem(f"attr_in{b}") for b in range(2)]
            attr_used = ph.sem("attr_used")
            bc, wea_ready, wea_here = ph.sem("bc"), ph.sem("wea_ready"), ph.sem("wea_here")
            digits, turned, rows_out, stored, padded = (ph.sem("digits"), ph.sem("turned"), ph.sem("rows_out"),
                                                        ph.sem("stored"), ph.sem("padded"))
            block = ph.block()
            attr = ins["edge_attr_128"].rearrange("(p t) c -> p t c", p=P)

            @block.sync
            def _(sp):
                for dst, src in ((si, "src"), (di, "dst"), (ti, "edge_type_2")):
                    sp.dma_start(dst[:, :], ins[src].rearrange("(p t) -> p t", p=P)).then_inc(loaded, 16)
                sp.dma_start(web[:, :, 0:128], ins["L2_gnn_We"].rearrange("(k p) c -> p k c", p=128)).then_inc(loaded, 16)
                with core.nc.allow_non_contiguous_dma(reason="two short columns"):
                    sp.dma_start(web[:, :, 128:129], ins["L2_gnn_be"].rearrange("(k p o) -> p k o", p=128, o=1)).then_inc(loaded, 16)
                    sp.dma_start(att[:, :], ins["L2_gnn_attn"].rearrange("a b (k p) -> p (a b k)", p=128)).then_inc(loaded, 16)

                def load(g, b):
                    sp.wait_ge(attr_used, g + 1)
                    sp.dma_start(ea[:, b, :, :], attr[:, bass.ds(g * G, G), :]).then_inc(attr_in[b], 16)
                each(sp, NGU, load)
                sp.wait_ge(rows_out, 2)
                for i, rows in enumerate((dstrows, lorows)):
                    sp.dma_start(rows.rearrange("(j r) p -> r j p", r=100), rowsb[:, i, :, :]).then_inc(stored, 16)
                sp.wait_ge(padded, 1)
                sp.dma_start(recs.rearrange("(p t) w -> p t w", p=128), pad[:, :, :]).then_inc(stored, 16)
                sp.wait_ge(stored, 48)

            @block.gpsimd
            def _(gp):
                gp.memset(pad[:, :, :], 0)
                gp.drain()
                gp.memset(pad[:, :, 1:2], -1).then_inc(padded, 1)

            @block.tensor
            def _(pe):
                pe.wait_ge(bc, 2)
                for k in range(2):
                    mm = pe.matmul(pw[:, :], attb[:, k, :], web[:, k, :], start=(k == 0), stop=(k == 1))
                mm.then_inc(wea_ready, 1)
                pe.wait_ge(digits, 1)
                for i, m in enumerate((dstc, loc)):
                    if i:
                        pe.wait_ge(rows_out, i)
                    for j in range(4):
                        mm = pe.transpose(pt[:, j, :], m[:, 100 * j:100 * j + 100], core.ident[0:P, 0:P])
                    mm.then_inc(turned, 1)

            @block.scalar
            def _(act):
                for i in range(2):
                    act.wait_ge(turned, i + 1)
                    act.copy(rowsb[:, i, :, :], pt[:, :, :]).then_inc(rows_out, 1)

            @block.vector
            def _(v):
                v.sem_inc(attr_used, 2)
                v.wait_ge(loaded, 96)
                for k in range(2):
                    v.tensor_scalar(attb[:, k, :], core.ones[:, 0:P], att[:, k:k + 1], None, ALU.mult).then_inc(bc, 1)
                v.tensor_copy(dstc[:, :], di[:, :])
                v.tensor_copy(sf[:, :], si[:, :])
                v.tensor_copy(tf[:, :], ti[:, :])
                v.drain()
                v.tensor_scalar(tmp[:, :], dstc[:, :], -62.0, 1.0 / P, ALU.add, ALU.mult)
                v.drain()
                v.tensor_scalar(hic[:, :], tmp[:, :], ROUND, -ROUND, ALU.add, ALU.add)
                v.drain()
                v.scalar_tensor_tensor(out=loc[:, :], in0=hic[:, :], scalar=-float(P), in1=dstc[:, :],
                                       op0=ALU.mult, op1=ALU.add).then_inc(digits, 1)
                v.tensor_copy(rec[:, :, 0], si[:, :])
                v.tensor_copy(rec[:, :, 1], di[:, :])
                v.scalar_tensor_tensor(out=rec[:, :, 2], in0=sf[:, :], scalar=2.0, in1=tf[:, :],
                                       op0=ALU.mult, op1=ALU.add)
                v.wait_ge(wea_ready, 1)
                v.tensor_copy(wea[:, :], pw[:, :])
                v.drain()

                def score(g, b):
                    v.wait_ge(attr_in[b], 16 * (g // 2 + 1) if isinstance(g, int) else 8 * (g - b) + 16)
                    v.tensor_tensor(prod[:, :, :], ea[:, b, :, :], wea[:, 0:128].unsqueeze(1).to_broadcast([P, G, 128]),
                                    ALU.mult).then_inc(attr_used, 1)
                    v.drain()
                    v.tensor_reduce(ee[:, bass.ds(g * G, G)], prod[:, :, :], AX.X, ALU.add)
                    v.drain()
                each(v, NGU, score)
                v.tensor_scalar(rec[:, :, 3].bitcast(F32), ee[:, :], wea[:, 128:129], None, ALU.add)

        with Phase(core, "count") as ph:
            ohl = ph.sb("ohl", [P, 2, G, P], BF16)
            ohh = ph.sb("ohh", [P, 2, G, NT], BF16)
            zero = ph.sb("zero", [P, P], BF16)
            total = ph.sb("total", [P, NT])
            tiles = ph.sb("tiles", [P, 3, NT])
            tstart = ph.sb("tstart", [P, NT])
            ct = ph.sb("ct", [1, TE, NT])
            io = ph.sb("io", [1, TE])
            bf = ph.sb("bf", [1, TE])
            ph_t = ph.psum("t", [P, NT])
            ph_c = ph.psum("c", [P, NT])
            ph_b = ph.psum("b", [P, NT])
            zeroed, hot, used, summed, copied, ranked = (ph.sem("zeroed"), ph.sem("hot"), ph.sem("used"),
                                                         ph.sem("summed"), ph.sem("copied"), ph.sem("ranked"))
            counted = ph.sem("counted")
            block = ph.block()

            @block.gpsimd
            def _(gp):
                gp.iota(io[:, :], [[1, TE]], 0, 0, allow_small_or_imprecise_dtypes=True).then_inc(counted, 1)

            @block.tensor
            def _(pe):
                pe.sem_inc(used, 2)
                pe.wait_ge(zeroed, 1)
                pe.matmul(ph_t[:, :], zero[:, :], zero[:, 0:NT], start=True, stop=False)

                def count(g, b):
                    pe.wait_ge(hot, g + 1)
                    for j in range(G):
                        mm = pe.matmul(ph_t[:, :], ohl[:, b, j, :], ohh[:, b, j, :], start=False, stop=False)
                    mm.then_inc(used, 1)
                each(pe, NGU, count)
                pe.matmul(ph_t[:, :], zero[:, :], zero[:, 0:NT], start=False, stop=True).then_inc(summed, 1)
                pe.wait_ge(copied, 1)
                pe.matmul(ph_b[:, :], core.tri[0:P, 0:P], total[:, :], start=True, stop=True)
                pe.matmul(ph_c[:, :], core.ones[0:P, 0:P], total[:, :], start=True, stop=True).then_inc(ranked, 1)

            @block.vector
            def _(v):
                v.memset(zero[:, :], 0.0).then_inc(zeroed, 1)

                def hots(g, b):
                    v.wait_ge(used, g + 1)
                    v.tensor_tensor(ohl[:, b, :, :], core.iota[0:P, 0:P].unsqueeze(1).to_broadcast([P, G, P]),
                                    loc[:, bass.ds(g * G, G)].unsqueeze(2).to_broadcast([P, G, P]), ALU.is_equal)
                    v.tensor_tensor(ohh[:, b, :, :], core.iota[0:P, 0:NT].unsqueeze(1).to_broadcast([P, G, NT]),
                                    hic[:, bass.ds(g * G, G)].unsqueeze(2).to_broadcast([P, G, NT]), ALU.is_equal)
                    v.drain()
                    v.sem_inc(hot, 1)
                each(v, NGU, hots)
                v.wait_ge(summed, 1)
                v.tensor_copy(total[:, :], ph_t[:, :]).then_inc(copied, 1)
                v.wait_ge(ranked, 1)
                v.tensor_scalar(tiles[:, 0, :], ph_c[:, :], 1.0 / 128, 63.75 / 128, ALU.mult, ALU.add)
                v.drain()
                v.tensor_scalar(tiles[:, 1, :], tiles[:, 0, :], ROUND, -ROUND, ALU.add, ALU.add)
                v.memset(tiles[:, 2, :], 0.0)
                v.drain()
                v.memset(tstart[:, 0:1], 0.0)
                v.tensor_tensor_scan(tstart[:, 1:NT], tiles[:, 1, 0:NT - 1], tiles[:, 2, 0:NT - 1], 0.0, ALU.add, ALU.add)
                v.drain()
                v.scalar_tensor_tensor(out=start[:, :], in0=tstart[:, :], scalar=128.0, in1=ph_b[:, :],
                                       op0=ALU.mult, op1=ALU.add)
                v.wait_ge(counted, 1)
                v.tensor_tensor(ct[:, :, :], io[:, :].unsqueeze(2).to_broadcast([1, TE, NT]),
                                tstart[0:1, :].unsqueeze(1).to_broadcast([1, TE, NT]), ALU.is_ge)
                v.drain()
                v.tensor_reduce(bf[:, :], ct[:, :, :], AX.X, ALU.add)
                v.drain()
                v.tensor_scalar(core.e_blk[:, :], bf[:, :], -1.0, None, ALU.add)

        with Phase(core, "place") as ph:
            ohl = ph.sb("ohl", [P, 4, G, P])
            ohh = ph.sb("ohh", [P, 4, G, NT])
            oht = ph.sb("oht", [P, 4, G, P])
            eq = ph.sb("eq", [P, 2, G, P])
            rank = ph.sb("rank", [P, 4, G])
            lk = ph.sb("lk", [P, G, NT])
            posf = ph.sb("posf", [P, G])
            posf2 = ph.sb("posf2", [P, G])
            pos = ph.sb("pos", [P, 4, G], I32)
            stage = ph.sb("stage", [P, 4, G, 4], I32)
            run = ph.sb("run", [P, 2, G + 1, NT])
            drow = ph.sb("drow", [P, 2, G * P])
            lrow = ph.sb("lrow", [P, 2, G * P])
            p_delta = ph.psum("delta", [P, 2, 512])
            p_look = ph.psum("look", [P, 2, 512])
            rows_in, rows_used = [ph.sem(f"rows_in{b}") for b in range(2)], ph.sem("rows_used")
            hot, delta, runs, looked, placed = ph.sem("hot"), ph.sem("delta"), ph.sem("runs"), ph.sem("looked"), ph.sem("placed")
            scat = [ph.sem(f"scat{b}") for b in range(4)]
            block = ph.block()

            @block.sync
            def _(sp):
                def load(g, b):
                    sp.wait_ge(rows_used, g + 1)
                    for sbt, rows in ((drow, dstrows), (lrow, lorows)):
                        sp.dma_start(sbt[:, b, :], rows[bass.ds(g * G, G), :].rearrange("t p -> (t p)").partition_broadcast(P)
                                     ).then_inc(rows_in[b], 16)
                each(sp, NGU, load)

            @block.tensor
            def _(pe):
                def count(g, b):
                    pe.wait_ge(hot, g + 1)
                    for j in range(G):
                        mm = pe.matmul(p_delta[:, b % 2, j * NT:(j + 1) * NT], ohl[:, b, j, :], ohh[:, b, j, :], start=True, stop=True)
                    mm.then_inc(delta, 1)

                def look(g, b):
                    pe.wait_ge(runs, G * (g + 1))
                    for j in range(G):
                        mm = pe.matmul(p_look[:, b % 2, j * NT:(j + 1) * NT], oht[:, b, j, :], run[:, b % 2, j, :],
                                       start=True, stop=True)
                    mm.then_inc(looked, 1)
                piped(pe, NGU, [(0, count), (1, look)])

            @block.vector
            def _(v):
                v.sem_inc(rows_used, 2)
                v.tensor_copy(run[:, 1, G, :], start[:, :])
                v.drain()

                def hots(g, b):
                    v.wait_ge(rows_in[b % 2], 32 * (g // 2 + 1) if isinstance(g, int) else 16 * (g - b % 2 + 2))
                    if later(g, 4):
                        v.wait_ge(looked, g - 3)
                    v.tensor_tensor(ohl[:, b, :, :], core.iota[0:P, 0:P].unsqueeze(1).to_broadcast([P, G, P]),
                                    loc[:, bass.ds(g * G, G)].unsqueeze(2).to_broadcast([P, G, P]), ALU.is_equal)
                    v.tensor_tensor(ohh[:, b, :, :], core.iota[0:P, 0:NT].unsqueeze(1).to_broadcast([P, G, NT]),
                                    hic[:, bass.ds(g * G, G)].unsqueeze(2).to_broadcast([P, G, NT]), ALU.is_equal)
                    v.tensor_scalar(oht[:, b, :, :].rearrange("p g e -> p (g e)"), lrow[:, b % 2, :], core.iotap[0:P, :], None, ALU.is_equal
                                    ).then_inc(hot, 1)

                def same(j):
                    def body(g, b):
                        ins = v.scalar_tensor_tensor(out=eq[:, b % 2, j, :], in0=drow[:, b % 2, j * P:(j + 1) * P],
                                                     scalar=dstc[:, bass.ds(g * G + j, 1)], in1=core.low[0:P, 0:P],
                                                     op0=ALU.is_equal, op1=ALU.mult)
                        if j == G - 1:
                            ins.then_inc(rows_used, 1)
                    return 0, body

                def run_on(j):
                    def body(g, b):
                        c = b % 2
                        last = run[:, c, j, :] if j else run[:, 1 - c, G, :]
                        if j == 0:
                            v.wait_ge(delta, g + 1)
                        if j or later(g, 1):
                            v.wait_ge(runs, g * G + j)
                        if j == 0:
                            v.tensor_copy(run[:, c, 0, :], last)
                        v.tensor_tensor(run[:, c, j + 1, :], last, p_delta[:, c, j * NT:(j + 1) * NT], ALU.add).then_inc(runs, 1)
                    return 1, body

                def ranks(g, b):
                    v.drain()
                    v.tensor_reduce(rank[:, b, :], eq[:, b % 2, :, :], AX.X, ALU.add)

                def place(g, b):
                    v.wait_ge(looked, g + 1)
                    v.tensor_tensor(lk[:, :, :], p_look[:, b % 2, 0:G * NT].rearrange("p (g h) -> p g h", g=G), ohh[:, b, :, :], ALU.mult)
                    v.drain()
                    v.tensor_reduce(posf[:, :], lk[:, :, :], AX.X, ALU.add)
                    v.drain()
                    v.tensor_tensor(posf2[:, :], posf[:, :], rank[:, b, :], ALU.add)
                    v.drain()
                    if later(g, 4):
                        v.wait_ge(scat[b], G * 16 * (g // 4) if isinstance(g, int) else G * 4 * (g - b))
                    v.tensor_copy(pos[:, b, :], posf2[:, :])
                    v.tensor_copy(stage[:, b, :, :], rec[:, bass.ds(g * G, G), :])
                    v.drain()
                    v.sem_inc(placed, 1)
                piped(v, NGU, [(0, hots)] + [s for j in range(G) for s in (same(j), run_on(j))] + [(0, ranks), (2, place)])

            @block.gpsimd
            def _(gp):
                def scatter(g, b):
                    gp.wait_ge(placed, g + 1)
                    gp.nop(nofuse=True)
                    for j in range(G):
                        gp.indirect_dma_start(recs, bass.IndirectOffsetOnAxis(ap=pos[:, b, j:j + 1].bitcast(U32), axis=0),
                                              stage[:, b, j, :], None).then_inc(scat[b], 16)
                each(gp, NGU, scatter, 4)
                for b in range(4):
                    gp.wait_ge(scat[b], G * 16 * ((NGU - b + 3) // 4))

    with Phase(core, "cols") as ph:
        R, J = 104, 4
        rc = ph.sb("rc", [128, TE, 4], I32)
        dcol = ph.sb("dcol", [128, TE])
        drow = ph.sb("drow", [R, J, 128])
        win = ph.sb("win", [R, 3, J, 128])
        tmp = ph.sb("tmp", [R, 4, J * 128])
        ends = ph.sb("ends", [1, 2])
        pt = ph.psum("pt", [R, J, 128])
        pc = ph.psum("pc", [128, 2, 512])
        loaded, cols, turned, rows, stored, windows = (ph.sem("loaded"), ph.sem("cols"), ph.sem("turned"), ph.sem("rows"),
                                                       ph.sem("stored"), ph.sem("windows"))
        made, back = ph.sem("made"), ph.sem("back")
        block = ph.block()

        @block.sync
        def _(sp):
            sp.dma_start(rc[:, :, :], recs.rearrange("(t p) w -> p t w", p=128)).then_inc(loaded, 16)
            sp.wait_ge(rows, 1)
            sp.dma_start(dsts[1:1 + TE * 128].rearrange("(j r e) -> r j e", r=R, e=128), drow[:, :, :]).then_inc(stored, 16)
            sp.dma_start(dsts[0:1].rearrange("(a b) -> a b", a=1), ends[:, 0:1]).then_inc(stored, 16)
            sp.dma_start(dsts[TE * 128 + 1:TE * 128 + 2].rearrange("(a b) -> a b", a=1), ends[:, 1:2]).then_inc(stored, 16)
            sp.wait_ge(stored, 48)
            for i, o in enumerate((1, 0, 2)):
                sp.dma_start(win[:, i, :, :], dsts[o:o + TE * 128].rearrange("(j r e) -> r j e", r=R, e=128)).then_inc(windows, 16)
            sp.wait_ge(made, 1)
            sp.dma_start(core.locrow.rearrange("(j r e) -> r j e", r=R, e=128), tmp[:, 1, :].rearrange("r (j e) -> r j e", j=J)).then_inc(stored, 16)
            sp.dma_start(core.rstrow.rearrange("(j r e) -> r j e", r=R, e=128), tmp[:, 2, :].rearrange("r (j e) -> r j e", j=J)).then_inc(stored, 16)
            sp.wait_ge(stored, 80)

        @block.tensor
        def _(pe):
            pe.wait_ge(cols, 1)
            for j in range(J):
                mm = pe.transpose(pt[:, j, :], dcol[:, R * j:R * j + R], core.ident[:, :])
            mm.then_inc(turned, 1)
            pe.wait_ge(made, 1)
            for i, k in enumerate((1, 3)):
                for j in range(J):
                    mm = pe.transpose(pc[:, i, R * j:R * j + R], tmp[:, k, 128 * j:128 * j + 128], core.ident[0:R, 0:R])
            mm.then_inc(back, 1)

        @block.vector
        def _(v):
            v.memset(ends[:, :], -2.0)
            v.wait_ge(loaded, 16)
            v.tensor_copy(dcol[:, :], rc[:, :, 1]).then_inc(cols, 1)
            v.tensor_copy(core.e_src[:, :], rc[:, :, 0])
            v.tensor_copy(core.e_srct[:, :], rc[:, :, 2])
            v.tensor_copy(core.e_ee[:, :], rc[:, :, 3].bitcast(F32))
            v.wait_ge(turned, 1)
            v.tensor_copy(drow[:, :, :], pt[:, :, :])
            v.drain()
            v.sem_inc(rows, 1)
            v.wait_ge(windows, 48)
            here, before, after = (win[:, i, :, :].rearrange("r j e -> r (j e)") for i in range(3))
            t = [tmp[:, i, :] for i in range(4)]
            v.tensor_scalar(t[0], here, -62.0, 1.0 / P, ALU.add, ALU.mult)
            v.drain()
            v.tensor_scalar(t[1], t[0], ROUND, -ROUND, ALU.add, ALU.add)
            v.drain()
            v.scalar_tensor_tensor(out=t[0], in0=t[1], scalar=-float(P), in1=here, op0=ALU.mult, op1=ALU.add)
            v.tensor_scalar(t[2], here, 0.0, None, ALU.is_ge)
            v.drain()
            v.scalar_tensor_tensor(out=t[3], in0=t[0], scalar=1.0, in1=t[2], op0=ALU.add, op1=ALU.mult)
            v.drain()
            v.tensor_scalar(t[1], t[3], -1.0, None, ALU.add)
            v.tensor_tensor(t[0], here, after, ALU.not_equal)
            v.tensor_tensor(t[2], here, before, ALU.not_equal)
            v.drain()
            v.tensor_tensor(here, t[0], t[3], ALU.mult)
            v.tensor_scalar(before, t[2], -BIG, None, ALU.mult)
            v.drain()
            v.tensor_scalar(t[3], here, -1.0, None, ALU.add)
            v.tensor_copy(t[2], before)
            v.drain()
            v.sem_inc(made, 1)
            v.wait_ge(back, 1)
            v.tensor_copy(core.e_loc[:, :], pc[:, 0, 0:TE])
            v.tensor_copy(core.e_last[:, :], pc[:, 1, 0:TE])


def blocks_of(core, engine, i):
    _, blks = core.nc.values_load_multi_w_load_instructions(
        core.e_blk[0:1, bass.ds(i * EG, EG)], engines=[engine], min_val=0, max_val=NT - 1,
        skip_runtime_bounds_check_because="sort_edges counts the blocks up, from 0 to at most NT - 1")
    return blks


def edge_scores(core, name, H, sc, best, table, idx, q=None, ee=False):
    nc = core.nc
    W = table.shape[1]
    with Phase(core, name) as ph:
        ix = ph.sb("ix", [128, 8, EG], I32)
        g = ph.sb("g", [128, 4, EG, W])
        rst = ph.sb("rst", [H, 4, GE])
        run = ph.sb("run", [H, 2, GE])
        raw = ph.sb("raw", [128, 4, EG, H])
        last = ph.sb("last", [128, 4, EG, P])
        bk = ph.sb("bk", [128, 2, EG, H + 1])
        back = ph.psum("back", [128, 512])[:, 0:EG * H].rearrange("p (g h) -> p g h", h=H)
        rows = ph.psum("rows", [H, GE])
        tops = ph.psum("tops", [P, 2, 512])
        if q is not None:
            lrow = ph.sb("lrow", [P, 4, GE])
            hot = ph.sb("hot", [P, 2, GE])
            prod = ph.sb("prod", [128, EG, D])
            qe = ph.psum("qe", [128, 2, EG, D])
        s_ix, s_used = ph.sem("ix_ready"), ph.sem("g_used")
        s_g = [ph.sem(f"g_in{b}") for b in range(4)]
        s_rst = [ph.sem(f"rst_in{b}") for b in range(4)]
        s_lrow = [ph.sem(f"lrow_in{b}") for b in range(4)] if q is not None else None
        s_run, s_raw, s_kept, s_rows, s_back, s_bk = (ph.sem("run"), ph.sem("raw"), ph.sem("kept"), ph.sem("rows"),
                                                      ph.sem("back"), ph.sem("bk"))
        s_last, s_tops, s_added, s_hot, s_qe = ph.sem("last"), ph.sem("tops"), ph.sem("added"), ph.sem("hot"), ph.sem("qe")
        s_zero = ph.sem("zero")
        block = ph.block()

        @block.sync
        def _(sp):
            def load(i, b):
                sp.wait_ge(s_run, i + 1)
                sp.dma_start(rst[:, b, :], core.rstrow[bass.ds(i * GE, GE)].partition_broadcast(H)).then_inc(s_rst[b], 16)

            def load_dst(i, b):
                sp.wait_ge(s_hot, i + 1)
                sp.dma_start(lrow[:, b, :], core.locrow[bass.ds(i * GE, GE)].partition_broadcast(P)).then_inc(s_lrow[b], 16)
            piped(sp, NG, ([(0, load_dst)] if q is not None else []) + [(2, load)])

        def rows_in(eng, sem, i, b):
            eng.wait_ge(sem[b], 16 * (i // 4 + 1) if isinstance(i, int) else 4 * (i - b + 4))

        @block.gpsimd
        def _(gp):
            def indices(i, b):
                gp.tensor_copy(ix[:, b, :], idx[:, bass.ds(i * EG, EG)]).then_inc(s_ix, 1)

            def gather(i, b):
                if later(i, 4):
                    gp.wait_ge(s_used, i - 3)
                gp.wait_ge(s_ix, i + 1)
                gp.nop(nofuse=True)
                for j in range(EG):
                    gp.indirect_dma_start(g[:, b % 4, j, :], None, table,
                                          bass.IndirectOffsetOnAxis(ap=ix[:, b, j:j + 1].bitcast(U32), axis=0)).then_inc(s_g[b % 4], 16)
            piped(gp, NG, [(0, indices), (1, gather)], 8)

        @block.tensor
        def _(pe):
            def queries(i, b):
                pe.wait_ge(s_hot, i + 5)
                if later(i):
                    pe.wait_ge(s_used, i - 1)
                blks = blocks_of(core, mybir.EngineType.PE, i)
                for j in range(EG):
                    mm = pe.matmul(qe[:, b % 2, j, :], hot[:, b % 2, 128 * j:128 * j + 128], q[:, bass.ds(blks[j], 1), :].rearrange("p o c -> p (o c)"),
                                   start=True, stop=True)
                mm.then_inc(s_qe, 1)

            def turn(i, b):
                pe.wait_ge(s_raw, i + 1)
                if later(i, 1):
                    pe.wait_ge(s_run, i + 4)
                for j in range(EG):
                    mm = pe.transpose(rows[:, 128 * j:128 * j + 128], raw[:, b, j, :], core.ident[:, :])
                mm.then_inc(s_rows, 1)

            def turn_back(i, b):
                pe.wait_ge(s_run, i + 5)
                if later(i, 1):
                    pe.wait_ge(s_bk, i)
                pe.nop(nofuse=True)
                for j in range(EG):
                    mm = pe.transpose(back[:, j, :], run[:, b % 2, 128 * j:128 * j + 128], core.ident[0:H, 0:H])
                mm.then_inc(s_back, 1)

            def pick(i, b):
                pe.wait_ge(s_bk, i + 1)
                pe.wait_ge(s_last, i + 1)
                if later(i):
                    pe.wait_ge(s_added, EG * (i - 1))
                for j in range(EG):
                    mm = pe.matmul(tops[:, b % 2, j * (H + 1):(j + 1) * (H + 1)], last[:, b, j, :], bk[:, b % 2, j, :],
                                   start=True, stop=True)
                mm.then_inc(s_tops, 1)
            piped(pe, NG, ([(1, queries)] if q is not None else []) + [(3, turn), (5, turn_back), (6, pick)])

        @block.scalar
        def _(act):
            act.wait_ge(s_zero, 1)

            def keep(i, b):
                act.wait_ge(s_raw, i + 1)
                act.copy(sc[:, bass.ds(i * EG, EG), :], raw[:, b, :, :]).then_inc(s_kept, 1)

            def copy_back(i, b):
                act.wait_ge(s_back, i + 1)
                if later(i):
                    act.wait_ge(s_tops, i - 1)
                act.copy(bk[:, b % 2, :, 0:H], back[:, :, :]).then_inc(s_bk, 1)
            piped(act, NG, [(2, keep), (5, copy_back)])

        @block.vector
        def _(v):
            v.memset(best[:, :, :], 0.0)
            v.memset(bk[:, :, :, H:H + 1], 1.0)
            v.memset(run[:, 1, GE - 1:GE], -BIG)
            v.drain()
            v.sem_inc(s_run, 4)
            if q is not None:
                v.sem_inc(s_hot, 4)
            v.sem_inc(s_zero, 1)

            def one_hot(i, b):
                rows_in(v, s_lrow, i, b)
                if later(i):
                    v.wait_ge(s_qe, i - 1)
                v.tensor_scalar(hot[:, b % 2, :], lrow[:, b, :], core.iotap[0:P, :], None, ALU.is_equal).then_inc(s_hot, 1)

            def score(i, b):
                v.wait_ge(s_g[b], 16 * EG * (i // 4 + 1) if isinstance(i, int) else 4 * EG * (i - b + 4))
                if later(i, 4):
                    v.wait_ge(s_kept, i - 3)
                    v.wait_ge(s_rows, i - 3)
                if q is not None:
                    v.wait_ge(s_qe, i + 1)
                    if later(i, 1):
                        v.wait_ge(s_raw, i)
                    v.tensor_tensor(prod[:, :, :], g[:, b, :, :], qe[:, b % 2, :, :], ALU.mult).then_inc(s_used, 1)
                elif ee:
                    ex = core.e_ee[:, bass.ds(i * EG, EG)].unsqueeze(2)
                    v.tensor_tensor(g[:, b, :, :], g[:, b, :, :], ex, ALU.add)
                    v.drain()
                    v.scalar_tensor_tensor(out=raw[:, b, :, :], in0=g[:, b, :, :], scalar=0.01, in1=g[:, b, :, :],
                                           op0=ALU.mult, op1=ALU.max)
                    v.drain()
                    v.sem_inc(s_raw, 1)
                    v.sem_inc(s_used, 1)
                else:
                    v.tensor_copy(raw[:, b, :, :], g[:, b, :, :])
                    v.drain()
                    v.sem_inc(s_raw, 1)
                    v.sem_inc(s_used, 1)

            def sum_up(i, b):
                v.wait_ge(s_used, i + 1)
                v.tensor_reduce(raw[:, b, :, :], prod[:, :, :].rearrange("p g (h d) -> p g h d", h=H), AX.X, ALU.add).then_inc(s_raw, 1)

            def scan(i, b):
                rows_in(v, s_rst, i, b)
                v.wait_ge(s_rows, i + 1)
                if later(i):
                    v.wait_ge(s_back, i - 1)
                if later(i, 1):
                    v.wait_ge(s_run, i + 4)
                v.tensor_tensor_scan(run[:, b % 2, :], rst[:, b, :], rows[:, :], run[:, 1 - b % 2, GE - 1:GE], ALU.add, ALU.max
                                     ).then_inc(s_run, 1)

            def last_edges(i, b):
                if later(i, 4):
                    v.wait_ge(s_tops, i - 3)
                v.tensor_tensor(last[:, b, :, :], core.iota[:, 0:P].unsqueeze(1).to_broadcast([128, EG, P]),
                                core.e_last[:, bass.ds(i * EG, EG)].unsqueeze(2).to_broadcast([128, EG, P]), ALU.is_equal
                                ).then_inc(s_last, 1)

            blks = [None] * EG

            def add_tile(j):
                def add(i, b):
                    if j == 0:
                        v.wait_ge(s_tops, i + 1)
                        blks[:] = blocks_of(core, mybir.EngineType.DVE, i)
                    slot = best[:, bass.ds(blks[j], 1), :].rearrange("p o c -> p (o c)")
                    if j or later(i, 1):
                        v.wait_ge(s_added, EG * i + j)
                    v.tensor_tensor(slot, slot, tops[:, b % 2, j * (H + 1):(j + 1) * (H + 1)], ALU.add).then_inc(s_added, 1)
                return 8, add
            piped(v, NG, [(4, scan), add_tile(0)] + ([(0, one_hot)] if q is not None else [])
                  + [add_tile(1), (2, score), add_tile(2), (4, last_edges), add_tile(3)]
                  + ([(2, sum_up)] if q is not None else []))


def edge_sums(core, name, H, acc, table, idx, sc=None, dtab=None, leaky=False):
    nc = core.nc
    WO = D + H
    with Phase(core, name) as ph:
        ix = ph.sb("ix", [128, 8, EG], I32)
        g = ph.sb("g", [128, 4, EG, D])
        here = ph.sb("here", [128, 4, EG, P])
        out = ph.psum("out", [P, EG, 512])
        if H:
            WD = dtab.shape[2]
            lrow = ph.sb("lrow", [P, 2, GE])
            hot = ph.sb("hot", [P, 2, GE])
            x = ph.sb("x", [128, 3, EG, H])
            msg = ph.sb("msg", [128, 4, EG, WO])
            de = ph.psum("de", [128, 2, 512])
        s_ix, s_used = ph.sem("ix_ready"), ph.sem("g_used")
        s_g = [ph.sem(f"g_in{b}") for b in range(4)]
        s_row = [ph.sem(f"row_in{b}") for b in range(2)]
        s_hot, s_de, s_x, s_ex, s_msg, s_here, s_out, s_added = (
            ph.sem("hot"), ph.sem("de"), ph.sem("x"), ph.sem("ex"), ph.sem("msg"), ph.sem("here"), ph.sem("out"), ph.sem("added"))
        block = ph.block()

        @block.sync
        def _(sp):
            def load(i, b):
                sp.wait_ge(s_hot, i + 1)
                sp.dma_start(lrow[:, b, :], core.locrow[bass.ds(i * GE, GE)].partition_broadcast(P)).then_inc(s_row[b], 16)
            if H:
                each(sp, NG, load)

        @block.gpsimd
        def _(gp):
            def indices(i, b):
                gp.tensor_copy(ix[:, b, :], idx[:, bass.ds(i * EG, EG)]).then_inc(s_ix, 1)

            def gather(i, b):
                if later(i, 4):
                    gp.wait_ge(s_msg if H else s_out, i - 3 if H else EG * (i - 3))
                gp.wait_ge(s_ix, i + 1)
                gp.nop(nofuse=True)
                for j in range(EG):
                    gp.indirect_dma_start(g[:, b % 4, j, :], None, table,
                                          bass.IndirectOffsetOnAxis(ap=ix[:, b, j:j + 1].bitcast(U32), axis=0)).then_inc(s_g[b % 4], 16)
            piped(gp, NG, [(0, indices), (1, gather)], 8)

        def g_in(eng, i, b):
            eng.wait_ge(s_g[b], 16 * EG * (i // 4 + 1) if isinstance(i, int) else 4 * EG * (i - b + 4))

        @block.tensor
        def _(pe):
            def of_dst(i, b):
                pe.wait_ge(s_hot, i + 3)
                if later(i):
                    pe.wait_ge(s_x, i - 1)
                blks = blocks_of(core, mybir.EngineType.PE, i)
                for j in range(EG):
                    mm = pe.matmul(de[:, b % 2, j * WD:(j + 1) * WD], hot[:, b % 2, 128 * j:128 * j + 128],
                                   dtab[:, bass.ds(blks[j], 1), :].rearrange("p o c -> p (o c)"), start=True, stop=True)
                mm.then_inc(s_de, 1)

            def total(i, b):
                pe.wait_ge(s_here, i + 1)
                if H:
                    pe.wait_ge(s_msg, i + 1)
                else:
                    g_in(pe, i, b)
                for j in range(EG):
                    if later(i, 1):
                        pe.wait_ge(s_added, EG * (i - 1) + j + 1)
                    pe.matmul(out[:, j, 0:WO], here[:, b, j, :], msg[:, b, j, :] if H else g[:, b, j, :], start=True, stop=True
                              ).then_inc(s_out, 1)
            piped(pe, NG, [(1, of_dst), (4, total)] if H else [(1, total)])

        if H:
            @block.scalar
            def _(act):
                def weigh(i, b):
                    act.wait_ge(s_x, i + 1)
                    if later(i, 4):
                        act.wait_ge(s_out, EG * (i - 3))
                    act.activation(msg[:, b, :, D:WO], x[:, 2, :, :], ACT.Exp).then_inc(s_ex, 1)
                piped(act, NG, [(2, weigh)])

        @block.vector
        def _(v):
            v.memset(acc[:, :, :], 0.0)
            v.drain()
            if H:
                v.sem_inc(s_hot, 2)

            def one_hot(i, b):
                v.wait_ge(s_row[b % 2], 16 * (i // 2 + 1) if isinstance(i, int) else 8 * (i - b % 2 + 2))
                if later(i):
                    v.wait_ge(s_de, i - 1)
                v.tensor_scalar(hot[:, b % 2, :], lrow[:, b % 2, :], core.iotap[0:P, :], None, ALU.is_equal).then_inc(s_hot, 1)

            def score(i, b):
                v.wait_ge(s_de, i + 1)
                if later(i, 1):
                    v.wait_ge(s_ex, i)
                d = de[:, b % 2, 0:EG * WD].rearrange("p (g w) -> p g w", g=EG)
                e = sc[:, bass.ds(i * EG, EG), :]
                if leaky:
                    v.tensor_tensor(x[:, 0, :, :], e, d[:, :, H:2 * H], ALU.add)
                    v.drain()
                    v.scalar_tensor_tensor(out=x[:, 1, :, :], in0=x[:, 0, :, :], scalar=0.2, in1=x[:, 0, :, :], op0=ALU.mult, op1=ALU.max)
                    v.drain()
                    v.tensor_tensor(x[:, 0, :, :], x[:, 1, :, :], d[:, :, 0:H], ALU.subtract)
                else:
                    v.tensor_tensor(x[:, 0, :, :], e, d[:, :, 0:H], ALU.subtract)
                v.drain()
                v.tensor_scalar(x[:, 2, :, :], x[:, 0, :, :], 0.0, None, ALU.min).then_inc(s_x, 1)

            def weigh(i, b):
                g_in(v, i, b)
                v.wait_ge(s_ex, i + 1)
                if later(i, 4):
                    v.wait_ge(s_out, EG * (i - 3))
                v.tensor_tensor(msg[:, b, :, 0:D].rearrange("p g (h d) -> p g h d", h=H),
                                g[:, b, :, :].rearrange("p g (h d) -> p g h d", h=H),
                                msg[:, b, :, D:WO].unsqueeze(3).to_broadcast([128, EG, H, D // H]), ALU.mult
                                ).then_inc(s_msg, 1)

            def edges_here(i, b):
                if later(i, 4):
                    v.wait_ge(s_out, EG * (i - 3))
                v.tensor_tensor(here[:, b, :, :], core.iota[:, 0:P].unsqueeze(1).to_broadcast([128, EG, P]),
                                core.e_loc[:, bass.ds(i * EG, EG)].unsqueeze(2).to_broadcast([128, EG, P]), ALU.is_equal
                                ).then_inc(s_here, 1)

            blks = [None] * EG

            def add_tile(lag, j):
                def add(i, b):
                    if j == 0:
                        blks[:] = blocks_of(core, mybir.EngineType.DVE, i)
                    slot = acc[:, bass.ds(blks[j], 1), :].rearrange("p o c -> p (o c)")
                    v.wait_ge(s_out, EG * i + j + 1)
                    if j or later(i, 1):
                        v.wait_ge(s_added, EG * i + j)
                    v.tensor_tensor(slot, slot, out[:, j, 0:WO], ALU.add).then_inc(s_added, 1)
                return lag, add
            if H:
                piped(v, NG, [add_tile(5, 0), (0, one_hot), add_tile(5, 1), (2, score), add_tile(5, 2), (3, edges_here),
                              add_tile(5, 3), (3, weigh)])
            else:
                piped(v, NG, [(1, edges_here)] + [add_tile(2, j) for j in range(EG)])


def move(core, name, pairs):
    with Phase(core, name) as ph:
        moved = ph.sem("moved")
        block = ph.block()

        @block.sync
        def _(sp):
            with core.nc.allow_non_contiguous_dma(reason="short rows"):
                for dst, src in pairs:
                    sp.dma_start(dst, src).then_inc(moved, 16)
            sp.wait_ge(moved, 16 * len(pairs))


def on_vector(core, name, body):
    with Phase(core, name) as ph:
        block = ph.block()

        @block.vector
        def _(v):
            body(v)
            v.drain()


def on_scalar(core, name, body):
    with Phase(core, name) as ph:
        block = ph.block()

        @block.scalar
        def _(act):
            body(act)
            act.drain()


def nodes(a):
    return a.rearrange("(t p) c -> p t c", p=P)


def flat(a):
    return a.rearrange("p t c -> p (t c)")


def normalize(core, name, src, dst, G=1, gain=None):
    C = src.shape[2]
    W = C // G
    with Phase(core, name) as ph:
        st = ph.sb("st", [P, NT * G, 6])
        mv = ph.sb("mv", [P, NT * G, 2])
        ve = ph.sb("ve", [P, NT * G])
        sd = ph.sb("sd", [P, NT * G])
        rs = ph.sb("rs", [P, NT * G])
        TQ = 5 if C <= 512 else 1
        sq = ph.sb("sq", [P, 2, TQ, C])
        less, squared, taken = ph.sem("less"), ph.sem("squared"), ph.sem("taken")
        var, root = ph.sem("var"), ph.sem("root")
        s3 = src[:, :, :].rearrange("p t (g c) -> p (t g) c", g=G)
        d3 = dst[:, :, :].rearrange("p t (g c) -> p (t g) c", g=G)
        block = ph.block()

        @block.vector
        def _(v):
            if G == 1:
                with v.Fori(0, NT) as t:
                    v.bn_stats(st[:, bass.ds(t, 1), :].rearrange("p o c -> p (o c)"), s3[:, bass.ds(t, 1), :].rearrange("p o c -> p (o c)"))
                v.drain()
                for t in range(NT):
                    v.bn_aggr(mv[:, t, :], st[:, t, :])
                v.drain()
                v.tensor_tensor(d3, s3, mv[:, :, 0:1].to_broadcast([P, NT * G, W]), ALU.subtract)
            else:
                v.tensor_reduce(ve[:, :], s3, AX.X, ALU.add)
                v.drain()
                v.tensor_scalar(mv[:, :, 0], ve[:, :], 1.0 / W, None, ALU.mult)
                v.drain()
                for t in range(0, NT, TQ):
                    v.tensor_tensor(d3[:, t * G:(t + TQ) * G, :], s3[:, t * G:(t + TQ) * G, :],
                                    mv[:, t * G:(t + TQ) * G, 0:1].to_broadcast([P, TQ * G, W]), ALU.subtract).then_inc(less, 1)
                for i in range(NT // TQ):
                    v.wait_ge(squared, i + 1)
                    v.tensor_reduce(ve[:, i * TQ * G:(i + 1) * TQ * G], sq[:, i % 2, :, :].rearrange("p t (g c) -> p (t g) c", g=G),
                                    AX.X, ALU.add).then_inc(taken, 1)
                v.drain()
                v.tensor_scalar(mv[:, :, 1], ve[:, :], 1.0 / W, None, ALU.mult)
            v.drain()
            v.tensor_scalar(ve[:, :], mv[:, :, 1], 1e-5, None, ALU.add)
            v.drain()
            v.sem_inc(var, 1)
            v.wait_ge(root, 1)
            v.reciprocal(rs[:, :], sd[:, :])
            v.drain()
            v.tensor_tensor(d3, d3, rs[:, :].unsqueeze(2).to_broadcast([P, NT * G, W]), ALU.mult)
            v.drain()
            if gain is not None:
                v.tensor_tensor(dst[:, :, :], dst[:, :, :], gain[:, 0:1, :].to_broadcast([P, NT, C]), ALU.mult)
                v.drain()
                v.tensor_tensor(dst[:, :, :], dst[:, :, :], gain[:, 1:2, :].to_broadcast([P, NT, C]), ALU.add)
                v.drain()

        @block.scalar
        def _(act):
            for i in range(NT // TQ if G > 1 else 0):
                act.wait_ge(less, i + 1)
                if i >= 2:
                    act.wait_ge(taken, i - 1)
                act.activation(sq[:, i % 2, :, :], dst[:, i * TQ:(i + 1) * TQ, :], ACT.Square).then_inc(squared, 1)
            act.wait_ge(var, 1)
            act.activation(sd[:, :], ve[:, :], ACT.Sqrt).then_inc(root, 1)


def project(core, name, src, w, M, use, bias=None, table=None):
    mode, dst = use
    cuts = [(c, min(c + 512, M)) for c in range(0, M, 512)]
    with Phase(core, name) as ph:
        rows = ph.sb("rows", [P, 4, D])
        xt = ph.sb("xt", [128, 4, 2, P])
        pt = ph.psum("pt", [128, 2, 512])
        out = ph.psum("out", [P, 2, len(cuts), 512])
        if mode == "pass":
            dst = ph.sb("passing", [P, 4, M])
        s_stored = [ph.sem(f"stored{b}") for b in range(4)]
        s_rows, s_turn, s_xt, s_mm, s_used = ph.sem("rows"), ph.sem("turned"), ph.sem("xt"), ph.sem("mm"), ph.sem("used")
        ptv = pt[:, :, 0:2 * P].rearrange("c b (k p) -> c b k p", k=2)
        block = ph.block()

        @block.tensor
        def _(pe):
            def turn(t, b):
                pe.wait_ge(s_rows, t + 1)
                if later(t):
                    pe.wait_ge(s_xt, t - 1)
                for k in range(2):
                    mm = pe.transpose(ptv[:, b % 2, k, :], rows[:, b, 128 * k:128 * k + 128], core.ident[0:P, 0:P])
                mm.then_inc(s_turn, 1)

            def multiply(t, b):
                pe.wait_ge(s_xt, t + 1)
                if later(t):
                    pe.wait_ge(s_used, t - 1)
                for i, (c, d) in enumerate(cuts):
                    for k in range(2):
                        mm = pe.matmul(out[:, b % 2, i, 0:d - c], xt[:, b, k, :], w[:, k, c:d], start=(k == 0), stop=(k == 1))
                mm.then_inc(s_mm, 1)
            piped(pe, NT, [(0, turn), (2, multiply)])

        @block.scalar
        def _(act):
            def lay(t, b):
                act.wait_ge(s_turn, t + 1)
                if later(t, 4):
                    act.wait_ge(s_mm, t - 3)
                act.copy(xt[:, b, :, :], ptv[:, b % 2, :, :]).then_inc(s_xt, 1)
            each(act, NT, lay, 4, peel=True)

        @block.vector
        def _(v):
            def stage(t, b):
                if later(t, 4):
                    v.wait_ge(s_turn, t - 3)
                v.tensor_copy(rows[:, b, :], src[:, bass.ds(t, 1), 0:D].rearrange("p o c -> p (o c)")).then_inc(s_rows, 1)
                if mode == "add" and bias is not None:
                    to = dst[:, bass.ds(t, 1), :].rearrange("p o c -> p (o c)")
                    v.tensor_tensor(to, to, bias[:, :], ALU.add)

            def take(t, b):
                v.wait_ge(s_mm, t + 1)
                if mode == "pass" and later(t, 4):
                    v.wait_ge(s_stored[b], 4 * (t - b) if not isinstance(t, int) else 16 * (t // 4))
                for i, (c, d) in enumerate(cuts):
                    to = dst[:, b, c:d] if mode == "pass" else dst[:, bass.ds(t, 1), c:d].rearrange("p o c -> p (o c)")
                    o = out[:, b % 2, i, 0:d - c]
                    if mode == "add":
                        ins = v.tensor_tensor(to, to, o, ALU.add)
                    elif bias is not None:
                        ins = v.tensor_tensor(to, o, bias[:, c:d], ALU.add)
                    else:
                        ins = v.tensor_copy(to, o)
                if len(cuts) > 1:
                    v.drain()
                    v.sem_inc(s_used, 1)
                else:
                    ins.then_inc(s_used, 1)
            piped(v, NT, [(0, stage), (3, take)])

        if table is not None:
            @block.sync
            def _(sp):
                def store(t, b):
                    sp.wait_ge(s_used, t + 1)
                    rows_out = dst[:, b, :] if mode == "pass" else dst[:, bass.ds(t, 1), :].rearrange("p o c -> p (o c)")
                    sp.dma_start(table[bass.ds(t * P, P), :], rows_out).then_inc(s_stored[b], 16)
                each(sp, NT, store, 4)
                for b in range(4):
                    sp.wait_ge(s_stored[b], 16 * ((NT - b + 3) // 4))


def weights(core, ph, name, M, *srcs):
    w = ph.sb(name, [128, 2, M])
    pairs, c = [], 0
    for src in srcs:
        m = src.shape[1]
        pairs.append((w[:, :, c:c + m], src.rearrange("(k p) m -> p k m", p=128)))
        c += m
    move(core, f"{ph.name}_{name}_in", pairs)
    return w


def rowvec(core, ph, name, M, *srcs, parts=1):
    r = ph.sb(name, [parts, M])
    pairs, c = [], 0
    for src in srcs:
        m = src.shape[0]
        pairs.append((r[:, c:c + m], src.partition_broadcast(parts)))
        c += m
    move(core, f"{ph.name}_{name}_in", pairs)
    return r


def elu(core, name, a, tmp):
    on_vector(core, f"{name}_lo", lambda v: v.tensor_scalar(flat(tmp[:, :, :]), flat(a[:, :, :]), 0.0, None, ALU.min))
    on_scalar(core, f"{name}_ex", lambda act: act.activation(flat(tmp[:, :, :]), flat(tmp[:, :, :]), ACT.Exp))

    def hi(v):
        v.tensor_scalar(flat(a[:, :, :]), flat(a[:, :, :]), 0.0, -1.0, ALU.max, ALU.add)
        v.drain()
        v.tensor_tensor(a[:, :, :], a[:, :, :], tmp[:, :, :], ALU.add)
    on_vector(core, f"{name}_hi", hi)


def gat(core, name, src, dst, W, att_src, att_dst, b):
    H = 4
    ins = core.ins
    th, tas = core.dram(f"{name}_th", (N, D)), core.dram(f"{name}_tas", (N, H))
    with Phase(core, name) as ph:
        h = ph.sb("h", [P, NT, D])
        a_s = ph.sb("a_s", [P, NT, H])
        dtab = ph.sb("dtab", [P, NT, 2 * H])
        sc = ph.sb("sc", [128, TE, H])
        best = ph.sb("best", [P, NT, H + 1])
        acc = ph.sb("acc", [P, NT, D + H])
        sw = ph.sb("sw", [P, NT, H])
        den = ph.sb("den", [P, NT, H])
        t = ph.sb("t", [P, NT, H])
        brow = rowvec(core, ph, "b", D, ins[b], parts=P)
        arow = rowvec(core, ph, "a", 2 * D, ins[att_src].rearrange("h c -> (h c)"), ins[att_dst].rearrange("h c -> (h c)"), parts=P)
        with Phase(core, f"{name}_w") as pw:
            w = weights(core, pw, "w", D, ins[W])
            project(core, f"{name}_h", src, w, D, ("copy", h), table=th)
        with Phase(core, f"{name}_x") as px:
            tmp = px.sb("tmp", [P, NT, D])

            def terms(v):
                for k, to in ((0, a_s[:, :, :]), (1, dtab[:, :, H:2 * H])):
                    v.tensor_tensor(tmp[:, :, :], h[:, :, :], arow[:, D * k:D * k + D].unsqueeze(1).to_broadcast([P, NT, D]), ALU.mult)
                    v.drain()
                    v.tensor_reduce(to, tmp[:, :, :].rearrange("p t (h c) -> p t h c", h=H), AX.X, ALU.add)
                    v.drain()
            on_vector(core, f"{name}_terms", terms)
        move(core, f"{name}_tabs", [(nodes(tas), a_s[:, :, :])])
        edge_scores(core, f"{name}_sc", H, sc, best, tas, core.e_src)

        def greatest(v):
            v.tensor_scalar(t[:, :, 0:1], best[:, :, H:H + 1], -1.0, BIG, ALU.add, ALU.mult)
            v.drain()
            v.tensor_tensor(den[:, :, :], best[:, :, 0:H], t[:, :, 0:1].to_broadcast([P, NT, H]), ALU.add)
            v.drain()
            v.tensor_tensor(sw[:, :, :], den[:, :, :], a_s[:, :, :], ALU.max)
            v.drain()
            v.tensor_tensor(t[:, :, :], sw[:, :, :], dtab[:, :, H:2 * H], ALU.add)
            v.tensor_tensor(den[:, :, :], a_s[:, :, :], dtab[:, :, H:2 * H], ALU.add)
            v.drain()
            v.scalar_tensor_tensor(out=dtab[:, :, 0:H], in0=t[:, :, :], scalar=0.2, in1=t[:, :, :], op0=ALU.mult, op1=ALU.max)
            v.scalar_tensor_tensor(out=sw[:, :, :], in0=den[:, :, :], scalar=0.2, in1=den[:, :, :], op0=ALU.mult, op1=ALU.max)
            v.drain()
            v.tensor_tensor(t[:, :, :], sw[:, :, :], dtab[:, :, 0:H], ALU.subtract)
        on_vector(core, f"{name}_greatest", greatest)
        on_scalar(core, f"{name}_self", lambda act: act.activation(sw[:, :, :], t[:, :, :], ACT.Exp))
        edge_sums(core, f"{name}_sum", H, acc, th, core.e_src, sc, dtab, leaky=True)

        def finish(v):
            v.tensor_tensor(den[:, :, :], acc[:, :, D:D + H], sw[:, :, :], ALU.add)
            for hh in range(H):
                c = slice(64 * hh, 64 * hh + 64)
                v.tensor_tensor(h[:, :, c], h[:, :, c], sw[:, :, hh:hh + 1].to_broadcast([P, NT, 64]), ALU.mult)
            v.drain()
            v.tensor_tensor(h[:, :, :], h[:, :, :], acc[:, :, 0:D], ALU.add)
            v.reciprocal(t[:, :, :], den[:, :, :])
            v.drain()
            for hh in range(H):
                c = slice(64 * hh, 64 * hh + 64)
                v.tensor_tensor(h[:, :, c], h[:, :, c], t[:, :, hh:hh + 1].to_broadcast([P, NT, 64]), ALU.mult)
            v.drain()
            v.tensor_tensor(dst[:, :, :], h[:, :, :], brow[:, :].unsqueeze(1).to_broadcast([P, NT, D]), ALU.add)
        on_vector(core, f"{name}_finish", finish)
        elu(core, f"{name}_elu", dst, h)


def gram(core, name, kv, K, left, right, out, sums=None):
    C = K // 128
    W = kv.shape[2]
    with Phase(core, name) as ph:
        st = ph.sb("st", [P, 4, W])
        acc = ph.psum("acc", [128, 512])
        ones = ph.psum("ones", [128, 512])
        s_st, s_mm, s_all = ph.sem("st"), ph.sem("mm"), ph.sem("all")
        block = ph.block()

        @block.tensor
        def _(pe):
            def product(t, b):
                pe.wait_ge(s_st, t + 1)
                first, end = isinstance(t, int) and t == 0, isinstance(t, int) and t == NT - 1
                for c in range(C):
                    mm = pe.matmul(acc[:, 128 * c:128 * c + 128], st[:, b, left + 128 * c:left + 128 * c + 128],
                                   st[:, b, right + 128 * c:right + 128 * c + 128], start=first and c == 0,
                                   stop=end and c == C - 1, skip_group_check=True)
                if sums is not None:
                    mm = pe.matmul(ones[:, 0:1], st[:, b, right:right + 128], core.ones[0:P, 0:1], start=first, stop=end)
                mm.then_inc(s_mm, 1)
            each(pe, NT, product, 4, peel=True)

        @block.vector
        def _(v):
            def take(t, b):
                if later(t, 4):
                    v.wait_ge(s_mm, t - 3)
                v.tensor_copy(st[:, b, :], kv[:, bass.ds(t, 1), :].rearrange("p o c -> p (o c)")).then_inc(s_st, 1)
            each(v, NT, take, 4, peel=True)
            v.wait_ge(s_mm, NT)
            v.tensor_copy(out[:, :, :].rearrange("p c e -> p (c e)"), acc[:, 0:K])
            if sums is not None:
                v.tensor_copy(sums[:, :], ones[:, 0:1])
            v.drain()


def head_mask(core, name, mask, W, scale):
    B = 128 // W
    with Phase(core, name) as ph:
        a = ph.sb("a", [128, 128])
        b = ph.sb("b", [128, 128])
        s = ph.sem("s")
        block = ph.block()

        @block.gpsimd
        def _(gp):
            gp.memset(a[:, :], scale).then_inc(s, 1)
            gp.wait_ge(s, 1)
            gp.affine_select(out=b[:, :].rearrange("p (b w) -> p b w", b=B), in_=a[:, :].rearrange("p (b w) -> p b w", b=B),
                             compare_op=ALU.is_ge, fill=0.0, base=0, pattern=[[-W, B], [0, W]], channel_multiplier=1).then_inc(s, 1)
            gp.wait_ge(s, 2)
            gp.affine_select(out=mask[:, :].rearrange("p (b w) -> p b w", b=B), in_=b[:, :].rearrange("p (b w) -> p b w", b=B),
                             compare_op=ALU.is_ge, fill=0.0, base=W - 1, pattern=[[W, B], [0, W]], channel_multiplier=-1)


def chain(core, name, steps):
    with Phase(core, name) as ph:
        acc = ph.psum("acc", [128, 512])
        mm_s, out_s = ph.sem("mm"), ph.sem("out")
        block = ph.block()

        @block.tensor
        def _(pe):
            for i, (to, col, terms, add) in enumerate(steps):
                if i:
                    pe.wait_ge(out_s, i)
                o = acc[0:to.shape[0], 0:to.shape[1]]
                for j, (lhs, rhs) in enumerate(terms):
                    mm = pe.matmul(o, lhs, rhs, start=(j == 0), stop=(j == len(terms) - 1))
                mm.then_inc(mm_s, 1)

        @block.vector
        def _(v):
            for i, (to, col, terms, add) in enumerate(steps):
                v.wait_ge(mm_s, i + 1)
                o = acc[0:to.shape[0], 0:to.shape[1]]
                if add is not None:
                    v.tensor_tensor(to, o, add, ALU.add)
                elif col is not None:
                    v.tensor_scalar(to, o, col, None, ALU.mult)
                else:
                    v.tensor_copy(to, o)
                v.drain()
                v.sem_inc(out_s, 1)


def column_softmax(core, name, kv, W):
    with Phase(core, name) as ph:
        top = ph.sb("top", [P, W])
        one = ph.sb("one", [W, 1])
        wide = ph.sb("wide", [W, P])
        low = ph.sb("low", [P, W])
        pa = ph.psum("pa", [128, 512])
        pb = ph.psum("pb", [128, 512])
        s_v, s_p = ph.sem("v"), ph.sem("p")
        block = ph.block()

        @block.tensor
        def _(pe):
            pe.wait_ge(s_v, 1)
            pe.transpose(pa[0:W, 0:P], top[:, :], core.ident[0:P, 0:P]).then_inc(s_p, 1)
            pe.wait_ge(s_v, 2)
            pe.transpose(pb[0:P, 0:W], wide[:, :], core.ident[0:W, 0:W]).then_inc(s_p, 1)

        @block.vector
        def _(v):
            v.tensor_reduce(top[:, :], kv[:, :, 0:W].rearrange("p t d -> p d t"), AX.X, ALU.max).then_inc(s_v, 1)
            v.wait_ge(s_p, 1)
            v.tensor_reduce(one[:, :], pa[0:W, 0:P], AX.X, ALU.max)
            v.drain()
            v.tensor_scalar(wide[:, :], core.ones[0:W, 0:P], one[:, :], None, ALU.mult).then_inc(s_v, 1)
            v.wait_ge(s_p, 2)
            v.tensor_copy(low[:, :], pb[0:P, 0:W])
            v.drain()
            v.tensor_tensor(kv[:, :, 0:W], kv[:, :, 0:W], low[:, :].unsqueeze(1).to_broadcast([P, NT, W]), ALU.subtract)
            v.drain()
    on_scalar(core, f"{name}_exp", lambda act: act.activation(kv[:, :, 0:W], kv[:, :, 0:W], ACT.Exp))


def linear_mix(core, name, src, dst, mode, K, W, scale, kv_w, q_t, out_w, kv_b=None, q_b=None, out_b=None, prepare=None, sums=False):
    C = K // 128
    with Phase(core, name) as ph:
        a = ph.sb("a", [128, 2, D])
        cvec = ph.sb("cvec", [P, D])
        with Phase(core, f"{name}_kvs") as pk:
            g = pk.sb("g", [128, C, 128])
            m2 = pk.sb("m2", [128, C, D])
            mask = pk.sb("mask", [128, 128])
            qt = pk.sb("qt", [128, C, D])
            sm = pk.sb("sm", [128, 1]) if sums else None
            rsm = pk.sb("rsm", [128, 1]) if sums else None
            head_mask(core, f"{name}_mask", mask, W, scale)
            pairs = [(qt[:, :, :], q_t.rearrange("(c p) i -> p c i", p=128))]
            if q_b is not None:
                bq = pk.sb("bq", [128, C])
                bqs = pk.sb("bqs", [128, C, P])
                pairs.append((bq[:, :], q_b.rearrange("(c p) -> p c", p=128)))
            if out_b is not None:
                bo = pk.sb("bo", [P, D]) if q_b is not None else cvec
                pairs.append((bo[:, :], out_b.partition_broadcast(P)))
            if out_w is not None:
                wo = pk.sb("wo", [128, C, D])
                pairs.append((wo[:, :, :], out_w.rearrange("(c p) i -> p c i", p=128)))
            move(core, f"{name}_in", pairs)
            with Phase(core, f"{name}_kv") as pv:
                kv = pv.sb("kv", [P, NT, 2 * K])
                with Phase(core, f"{name}_w") as pw:
                    w = weights(core, pw, "w", 2 * K, kv_w)
                    b = rowvec(core, pw, "b", 2 * K, *kv_b, parts=P) if kv_b is not None else None
                    project(core, f"{name}_project", src, w, 2 * K, ("copy", kv), bias=b)
                if prepare:
                    prepare(kv)
                if out_w is not None:
                    gram(core, f"{name}_gram", kv, K, K, 0, g, sums=sm)
                else:
                    gram(core, f"{name}_gram", kv, K, 0, K, g)

            def masked(v):
                v.tensor_tensor(g[:, :, :], g[:, :, :], mask[:, :].unsqueeze(1).to_broadcast([128, C, 128]), ALU.mult)
                if sums:
                    v.reciprocal(rsm[:, :], sm[:, :])
                if q_b is not None:
                    v.tensor_copy(bqs[:, :, :], bq[:, :].unsqueeze(2).to_broadcast([128, C, P]))
                if out_w is None:
                    v.memset(m2[:, :, :], 0.0)
                    v.drain()
                    for c in range(C):
                        v.tensor_copy(m2[:, c, 128 * c:128 * c + 128], g[:, c, :])
            on_vector(core, f"{name}_masked", masked)
            steps = []
            if out_w is not None:
                steps += [(m2[:, c, :], rsm[:, 0:1] if sums else None, [(g[:, c, :], wo[:, c, :])], None) for c in range(C)]
            steps += [(a[:, i, :], None, [(qt[:, c, 128 * i:128 * i + 128], m2[:, c, :]) for c in range(C)], None) for i in range(2)]
            if q_b is not None:
                steps.append((cvec[:, :], None, [(bqs[:, c, :], m2[:, c, :]) for c in range(C)], bo[:, :] if out_b is not None else None))
            chain(core, f"{name}_chain", steps)
        project(core, f"{name}_out", src, a, D, (mode, dst), bias=cvec if (q_b is not None or out_b is not None) else None)


def moe(core, name, x, out, TOP, NE, F, gate_w, gate_b, w1, b1, w2, b2, func, weigh, capacity=None):
    nc, ins = core.nc, core.ins
    TT = (TOP * N + 127 * NE) // 128
    FC = F // 128
    tx = core.dram(f"{name}_tx", (N, D))
    ty = core.dram(f"{name}_ty", (TT * 128, D))
    toks = core.dram(f"{name}_toks", (TT * 128, 1), I32)
    with Phase(core, name) as ph:
        w8 = ph.sb("w8", [P, NT, TOP])
        pos = ph.sb("pos", [P, NT, TOP], I32)
        te = ph.sb("te", [1, TT], I32)
        tok = ph.sb("tok", [128, TT], I32)
        with Phase(core, f"{name}_route") as pr:
            lg = pr.sb("lg", [P, NT, NE])
            pw8 = pr.sb("pw8", [P, NT, 8])
            ix8 = pr.sb("ix8", [P, NT, 8], U32)
            ixf = pr.sb("ixf", [P, NT, TOP])
            oh = pr.sb("oh", [P, TOP, NT, NE])
            ohs = pr.sb("ohs", [P, NT, NE])
            before = pr.sb("before", [P, NT + 1, NE])
            rank = pr.sb("rank", [P, NT, NE])
            tmp = pr.sb("tmp", [P, NT, NE])
            col = pr.sb("col", [P, NT, 1])
            kept = pr.sb("kept", [P, NT, TOP])
            posf = pr.sb("posf", [P, NT, TOP])
            tl = pr.sb("tl", [P, 3, NE])
            tstart = pr.sb("tstart", [P, NE])
            ct = pr.sb("ct", [1, TT, NE])
            io = pr.sb("io", [1, TT])
            bf = pr.sb("bf", [1, TT])
            tid = pr.sb("tid", [P, NT], I32)
            zero = pr.sb("zero", [128, TT], I32)
            with Phase(core, f"{name}_gate") as pg:
                gw = weights(core, pg, "gw", NE, gate_w)
                gb = rowvec(core, pg, "gb", NE, gate_b, parts=P) if gate_b is not None else None
                project(core, f"{name}_logits", x, gw, NE, ("copy", lg), bias=gb)
            if weigh != "top logits":
                def less_top(v):
                    v.tensor_reduce(col[:, :, :], lg[:, :, :], AX.X, ALU.max)
                    v.drain()
                    v.tensor_tensor(lg[:, :, :], lg[:, :, :], col[:, :, :].to_broadcast([P, NT, NE]), ALU.subtract)
                on_vector(core, f"{name}_less", less_top)
                on_scalar(core, f"{name}_exp", lambda act: act.activation(lg[:, :, :], lg[:, :, :], ACT.Exp))

                def over_sum(v):
                    v.tensor_reduce(col[:, :, :], lg[:, :, :], AX.X, ALU.add)
                    v.drain()
                    v.reciprocal(col[:, :, :], col[:, :, :])
                    v.drain()
                    v.tensor_tensor(lg[:, :, :], lg[:, :, :], col[:, :, :].to_broadcast([P, NT, NE]), ALU.mult)
                on_vector(core, f"{name}_probs", over_sum)

            def choose(v):
                for t in range(NT):
                    v.max(pw8[:, t, :], lg[:, t, :])
                v.drain()
                for t in range(NT):
                    v.max_index(ix8[:, t, :], pw8[:, t, :], lg[:, t, :])
                v.drain()
                v.tensor_copy(ixf[:, :, :], ix8[:, :, 0:TOP])
                v.tensor_copy(w8[:, :, :], pw8[:, :, 0:TOP])
                v.drain()
                for k in range(TOP):
                    v.tensor_tensor(oh[:, k, :, :], core.iota[0:P, 0:NE].unsqueeze(1).to_broadcast([P, NT, NE]),
                                    ixf[:, :, k:k + 1].to_broadcast([P, NT, NE]), ALU.is_equal)
                if weigh == "over their sum":
                    v.tensor_tensor(col[:, :, 0], w8[:, :, 0], w8[:, :, 1], ALU.add)
                    v.drain()
                    v.tensor_scalar(col[:, :, :], col[:, :, :], 1e-12, None, ALU.max)
                    v.drain()
                    v.reciprocal(col[:, :, :], col[:, :, :])
                    v.drain()
                    v.tensor_tensor(w8[:, :, :], w8[:, :, :], col[:, :, :].to_broadcast([P, NT, TOP]), ALU.mult)
                if weigh == "top logits":
                    v.tensor_tensor(w8[:, :, :], w8[:, :, :], pw8[:, :, 0:1].to_broadcast([P, NT, TOP]), ALU.subtract)
                v.drain()
                if TOP == 2:
                    v.tensor_tensor(ohs[:, :, :], oh[:, 0, :, :], oh[:, 1, :, :], ALU.add)
                else:
                    v.tensor_copy(ohs[:, :, :], oh[:, 0, :, :])
                v.memset(before[:, 0, :], 0.0)
                v.drain()
                for t in range(NT):
                    v.tensor_tensor(before[:, t + 1, :], before[:, t, :], ohs[:, t, :], ALU.add)
                    v.drain()
            on_vector(core, f"{name}_choose", choose)
            if weigh == "top logits":
                on_scalar(core, f"{name}_wexp", lambda act: act.activation(w8[:, :, :], w8[:, :, :], ACT.Exp))

                def norm(v):
                    v.tensor_reduce(col[:, :, :], w8[:, :, :], AX.X, ALU.add)
                    v.drain()
                    v.reciprocal(col[:, :, :], col[:, :, :])
                    v.drain()
                    v.tensor_tensor(w8[:, :, :], w8[:, :, :], col[:, :, :].to_broadcast([P, NT, TOP]), ALU.mult)
                on_vector(core, f"{name}_wnorm", norm)

            with Phase(core, f"{name}_rank") as pk:
                pa = pk.psum("pa", [P, 512])
                pb = pk.psum("pb", [P, 512])
                s_mm, s_io = pk.sem("mm"), pk.sem("io")
                block = pk.block()

                @block.gpsimd
                def _(gp):
                    gp.iota(io[:, :], [[1, TT]], 0, 0, allow_small_or_imprecise_dtypes=True)
                    gp.iota(tid[:, :], [[P, NT]], 0, 1)
                    gp.memset(zero[:, :], 0)
                    gp.drain()
                    gp.sem_inc(s_io, 1)

                @block.tensor
                def _(pe):
                    pe.matmul(pa[:, 0:NT * NE], core.tri[0:P, 0:P], ohs[:, :, :].rearrange("p t e -> p (t e)"), start=True, stop=False)
                    pe.matmul(pa[:, 0:NT * NE], core.ones[0:P, 0:P], before[:, 0:NT, :].rearrange("p t e -> p (t e)"), start=False, stop=True)
                    pe.matmul(pb[:, 0:NE], core.ones[0:P, 0:P], before[:, NT, :], start=True, stop=True).then_inc(s_mm, 1)

                @block.vector
                def _(v):
                    v.wait_ge(s_mm, 1)
                    v.tensor_copy(rank[:, :, :].rearrange("p t e -> p (t e)"), pa[:, 0:NT * NE])
                    v.tensor_scalar(tl[:, 0, :], pb[:, 0:NE], 1.0 / 128, 63.75 / 128, ALU.mult, ALU.add)
                    v.memset(tl[:, 2, :], 0.0)
                    v.memset(tstart[:, 0:1], 0.0)
                    v.drain()
                    v.tensor_scalar(tl[:, 1, :], tl[:, 0, :], ROUND, -ROUND, ALU.add, ALU.add)
                    v.drain()
                    v.tensor_tensor_scan(tstart[:, 1:NE], tl[:, 1, 0:NE - 1], tl[:, 2, 0:NE - 1], 0.0, ALU.add, ALU.add)
                    if capacity is not None:
                        v.tensor_tensor(tmp[:, :, :], rank[:, :, :], oh[:, 0, :, :], ALU.mult)
                        v.drain()
                        v.tensor_reduce(col[:, :, :], tmp[:, :, :], AX.X, ALU.add)
                        v.drain()
                        v.tensor_scalar(kept[:, :, :], col[:, :, :], float(capacity), None, ALU.is_lt)
                        v.drain()
                        v.tensor_tensor(w8[:, :, :], w8[:, :, :], kept[:, :, :], ALU.mult)
                    v.drain()
                    v.tensor_scalar(tl[:, 0, :], tstart[:, :], 128.0, None, ALU.mult)
                    v.drain()
                    v.tensor_tensor(rank[:, :, :], rank[:, :, :], tl[:, 0:1, :].to_broadcast([P, NT, NE]), ALU.add)
                    for k in range(TOP):
                        v.drain()
                        v.tensor_tensor(tmp[:, :, :], rank[:, :, :], oh[:, k, :, :], ALU.mult)
                        v.drain()
                        v.tensor_reduce(posf[:, :, k:k + 1], tmp[:, :, :], AX.X, ALU.add)
                    v.drain()
                    v.tensor_copy(pos[:, :, :], posf[:, :, :])
                    v.wait_ge(s_io, 1)
                    v.tensor_tensor(ct[:, :, :], io[:, :].unsqueeze(2).to_broadcast([1, TT, NE]),
                                    tstart[0:1, :].unsqueeze(1).to_broadcast([1, TT, NE]), ALU.is_ge)
                    v.drain()
                    v.tensor_reduce(bf[:, :], ct[:, :, :], AX.X, ALU.add)
                    v.drain()
                    v.tensor_scalar(te[:, :], bf[:, :], -1.0, None, ALU.add)
                    v.drain()

            move(core, f"{name}_clear", [(nodes(tx), x[:, :, :]), (toks.rearrange("(p t) o -> p (t o)", p=128), zero[:, :])])
            with Phase(core, f"{name}_scatter") as pk:
                st = pk.sb("st", [P, 4, TOP + 1], I32)
                s_st, s_sc = pk.sem("st"), [pk.sem(f"sc{b}") for b in range(4)]
                block = pk.block()

                @block.gpsimd
                def _(gp):
                    def put(t, b):
                        if later(t, 4):
                            gp.wait_ge(s_sc[b], 4 * TOP * (t - b) if not isinstance(t, int) else 16 * TOP * (t // 4))
                        gp.tensor_copy(st[:, b, 0:TOP], pos[:, bass.ds(t, 1), :].rearrange("p o c -> p (o c)")).then_inc(s_st, 1)
                        gp.tensor_copy(st[:, b, TOP:TOP + 1], tid[:, bass.ds(t, 1)]).then_inc(s_st, 1)
                        gp.wait_ge(s_st, 2 * t + 2)
                        gp.nop(nofuse=True)
                        for k in range(TOP):
                            gp.indirect_dma_start(toks, bass.IndirectOffsetOnAxis(ap=st[:, b, k:k + 1].bitcast(U32), axis=0),
                                                  st[:, b, TOP:TOP + 1], None).then_inc(s_sc[b], 16)
                    each(gp, NT, put, 4, peel=True)
                    for b in range(4):
                        gp.wait_ge(s_sc[b], 16 * TOP * ((NT - b + 3) // 4))
            move(core, f"{name}_tokin", [(tok[:, :], toks.rearrange("(t p) o -> p (t o)", p=128))])

        with Phase(core, f"{name}_experts") as pe_:
            ix = pe_.sb("ix", [128, 4, 1], I32)
            xg = pe_.sb("xg", [128, 4, D])
            xt = pe_.sb("xt", [128, 2, 2, 128])
            w1b = pe_.sb("w1b", [128, 4, 2, F])
            w2b = pe_.sb("w2b", [128, 4, FC, D])
            b1b = pe_.sb("b1b", [128, 4, FC])
            b2s = pe_.sb("b2s", [128, NE, D])
            ht = pe_.sb("ht", [128, 2, FC, 128])
            yb = pe_.sb("yb", [128, 4, D])
            px = pe_.psum("px", [128, 2, 512])
            phid = pe_.psum("phid", [128, 2, max(FC * 128, 512)])
            py = pe_.psum("py", [128, 2, 512])
            s_ix, s_turn, s_xt, s_up, s_ht, s_down, s_y = (pe_.sem("ix"), pe_.sem("turn"), pe_.sem("xt"), pe_.sem("up"),
                                                           pe_.sem("ht"), pe_.sem("down"), pe_.sem("y"))
            s_b2 = pe_.sem("b2")
            s_x = [pe_.sem(f"x{b}") for b in range(4)]
            s_w = [pe_.sem(f"w{b}") for b in range(4)]
            s_o = [pe_.sem(f"o{b}") for b in range(4)]
            block = pe_.block()

            @block.sync
            def _(sp):
                def load(t, b):
                    if later(t, 4):
                        sp.wait_ge(s_down, t - 3)
                    e = sp.value_load(te[0:1, bass.ds(t, 1)], min_val=0, max_val=NE - 1)
                    sp.dma_start(w1b[:, b, :, :], w1[bass.ds(e, 1), :, :, :].rearrange("o p k f -> p (o k) f")).then_inc(s_w[b], 16)
                    sp.dma_start(w2b[:, b, :, :], w2[bass.ds(e, 1), :, :, :].rearrange("o p k f -> p (o k) f")).then_inc(s_w[b], 16)
                    sp.dma_start(b1b[:, b, :], b1[bass.ds(e, 1), :, :].rearrange("o p f -> p (o f)")).then_inc(s_w[b], 16)
                each(sp, TT, load, 4, peel=True)

            def w_in(eng, t, b):
                eng.wait_ge(s_w[b], 48 * (t // 4 + 1) if isinstance(t, int) else 12 * (t - b + 4))

            @block.gpsimd
            def _(gp):
                def gather(t, b):
                    if later(t, 4):
                        gp.wait_ge(s_turn, t - 3)
                    gp.tensor_copy(ix[:, b, :], tok[:, bass.ds(t, 1)]).then_inc(s_ix, 1)
                    gp.wait_ge(s_ix, t + 1)
                    gp.nop(nofuse=True)
                    gp.indirect_dma_start(xg[:, b, :], None, tx, bass.IndirectOffsetOnAxis(ap=ix[:, b, 0:1].bitcast(U32), axis=0)
                                          ).then_inc(s_x[b], 16)
                each(gp, TT, gather, 4, peel=True)

            @block.tensor
            def _(pe):
                def turn(t, b):
                    pe.wait_ge(s_x[b], 16 * (t // 4 + 1) if isinstance(t, int) else 4 * (t - b + 4))
                    if later(t):
                        pe.wait_ge(s_xt, t - 1)
                    for k in range(2):
                        mm = pe.transpose(px[:, b % 2, 128 * k:128 * k + 128], xg[:, b, 128 * k:128 * k + 128], core.ident[:, :])
                    mm.then_inc(s_turn, 1)

                def up(t, b):
                    w_in(pe, t, b)
                    pe.wait_ge(s_xt, t + 1)
                    if later(t):
                        pe.wait_ge(s_ht, t - 1)
                    for f in range(FC):
                        for k in range(2):
                            mm = pe.matmul(phid[:, b % 2, 128 * f:128 * f + 128], w1b[:, b, k, 128 * f:128 * f + 128], xt[:, b % 2, k, :],
                                           start=(k == 0), stop=(k == 1))
                    mm.then_inc(s_up, 1)

                def down(t, b):
                    pe.wait_ge(s_ht, t + 1)
                    if later(t):
                        pe.wait_ge(s_y, t - 1)
                    for f in range(FC):
                        mm = pe.matmul(py[:, b % 2, 0:D], ht[:, b % 2, f, :], w2b[:, b, f, :], start=(f == 0), stop=(f == FC - 1))
                    mm.then_inc(s_down, 1)
                piped(pe, TT, [(0, turn), (1, up), (2, down)])

            @block.vector
            def _(v):
                def lay(t, b):
                    v.wait_ge(s_turn, t + 1)
                    if later(t):
                        v.wait_ge(s_up, t - 1)
                    v.tensor_copy(xt[:, b % 2, :, :].rearrange("p k c -> p (k c)"), px[:, b % 2, 0:256]).then_inc(s_xt, 1)

                def result(t, b):
                    v.wait_ge(s_down, t + 1)
                    if later(t, 4):
                        v.wait_ge(s_o[b], 4 * (t - b) if not isinstance(t, int) else 16 * (t // 4))
                    e = v.value_load(te[0:1, bass.ds(t, 1)], min_val=0, max_val=NE - 1)
                    v.tensor_tensor(yb[:, b, :], py[:, b % 2, 0:D], b2s[:, bass.ds(e, 1), :].rearrange("p o c -> p (o c)"), ALU.add
                                    ).then_inc(s_y, 1)
                v.wait_ge(s_b2, 16)
                piped(v, TT, [(0, lay), (2, result)])

            @block.scalar
            def _(act):
                act.dma_start(b2s[:, :, :].rearrange("p e c -> p (e c)"), b2.rearrange("e c -> (e c)").partition_broadcast(128)).then_inc(s_b2, 16)

                def middle(t, b):
                    act.wait_ge(s_up, t + 1)
                    w_in(act, t, b)
                    if later(t):
                        act.wait_ge(s_down, t - 1)
                    for f in range(FC):
                        act.activation(ht[:, b % 2, f, :], phid[:, b % 2, 128 * f:128 * f + 128], func, bias=b1b[:, b, f:f + 1])
                    act.drain()
                    act.sem_inc(s_ht, 1)

                def put(t, b):
                    act.wait_ge(s_y, t + 1)
                    act.dma_start(ty[bass.ds(t * 128, 128), :], yb[:, b, :]).then_inc(s_o[b], 16)
                piped(act, TT, [(0, middle), (2, put)])
                for b in range(4):
                    act.wait_ge(s_o[b], 16 * ((TT - b + 3) // 4))

        with Phase(core, f"{name}_combine") as pc:
            ix = pc.sb("ix", [P, 4, TOP], I32)
            y = pc.sb("y", [P, 4, TOP, D])
            part = pc.sb("part", [P, 4, 2, D])
            s_ix, s_used = pc.sem("ix"), pc.sem("used")
            s_in = [pc.sem(f"in{b}") for b in range(4)]
            block = pc.block()

            @block.gpsimd
            def _(gp):
                def gather(t, b):
                    if later(t, 4):
                        gp.wait_ge(s_used, t - 3)
                    gp.tensor_copy(ix[:, b, :], pos[:, bass.ds(t, 1), :].rearrange("p o c -> p (o c)")).then_inc(s_ix, 1)
                    gp.wait_ge(s_ix, t + 1)
                    gp.nop(nofuse=True)
                    for k in range(TOP):
                        gp.indirect_dma_start(y[:, b, k, :], None, ty, bass.IndirectOffsetOnAxis(ap=ix[:, b, k:k + 1].bitcast(U32), axis=0)
                                              ).then_inc(s_in[b], 16)
                each(gp, NT, gather, 4, peel=True)

            @block.vector
            def _(v):
                def add(t, b):
                    v.wait_ge(s_in[b], 16 * TOP * (t // 4 + 1) if isinstance(t, int) else 4 * TOP * (t - b + 4))
                    to = out[:, bass.ds(t, 1), :].rearrange("p o c -> p (o c)")
                    w = [w8[:, bass.ds(t, 1), k:k + 1].rearrange("p o c -> p (o c)") for k in range(TOP)]
                    if TOP == 1:
                        v.tensor_tensor(to, y[:, b, 0, :], w[0].to_broadcast([P, D]), ALU.mult).then_inc(s_used, 1)
                    else:
                        v.tensor_tensor(part[:, b, 0, :], y[:, b, 0, :], w[0].to_broadcast([P, D]), ALU.mult)
                        v.tensor_tensor(part[:, b, 1, :], y[:, b, 1, :], w[1].to_broadcast([P, D]), ALU.mult)
                        v.drain()
                        v.tensor_tensor(to, part[:, b, 0, :], part[:, b, 1, :], ALU.add).then_inc(s_used, 1)
                each(v, NT, add, 4)


def add_to(core, name, x, *parts):
    def body(v):
        for p in parts:
            v.tensor_tensor(x[:, :, :], x[:, :, :], p[:, :, :], ALU.add)
            v.drain()
    on_vector(core, name, body)


def layer0(core, x, xn):
    ins = core.ins
    normalize(core, "l0_norm", x, xn)
    with Phase(core, "l0") as ph:
        g = ph.sb("g", [P, NT, D])
        gat(core, "l0_gat1", xn, g, "L0_gnn_W1", "L0_gnn_att_src1", "L0_gnn_att_dst1", "L0_gnn_b1")
        gat(core, "l0_gat2", g, g, "L0_gnn_W2", "L0_gnn_att_src2", "L0_gnn_att_dst2", "L0_gnn_b2")
        add_to(core, "l0_add", x, g)
    linear_mix(core, "l0_mix", xn, x, "add", D, 32, 1.0 / N, ins["L0_mix_kv"], ins["L0_mix_Wq"], ins["L0_mix_WfcT"],
               kv_b=(ins["L0_mix_bk"], ins["L0_mix_bv"]), q_b=ins["L0_mix_bq"], out_b=ins["L0_mix_bfc"])


def layer0_ffn(core, x, xn):
    ins = core.ins
    normalize(core, "f0_norm", x, xn)
    with Phase(core, "f0") as ph:
        g = ph.sb("g", [P, NT, D])
        moe(core, "f0_moe", xn, g, 2, 8, 512, ins["L0_ffn_gate_w"], ins["L0_ffn_gate_b"], ins["L0_ffn_W1"], ins["L0_ffn_b1"],
            ins["L0_ffn_W2"], ins["L0_ffn_b2"], ACT.Gelu, "probs")
        add_to(core, "f0_add", x, g)


def layer1(core, x, xn):
    ins = core.ins
    normalize(core, "l1_norm", x, xn)
    table = core.dram("l1_table", (N, D))
    with Phase(core, "l1") as ph:
        g = ph.sb("g", [P, NT, D])
        with Phase(core, "l1_w") as pw:
            w = weights(core, pw, "w", D, ins["L1_gnn_W2T"])
            project(core, "l1_rows", xn, w, D, ("copy", g), table=table)
        edge_sums(core, "l1_sum", 0, g, table, core.e_src)
        with Phase(core, "l1_v") as pw:
            w = weights(core, pw, "w", D, ins["L1_gnn_W1T"])
            project(core, "l1_self", xn, w, D, ("add", g))

        def relu_add(v):
            v.scalar_tensor_tensor(out=x[:, :, :], in0=g[:, :, :], scalar=0.0, in1=x[:, :, :], op0=ALU.max, op1=ALU.add)
        on_vector(core, "l1_relu", relu_add)
        with Phase(core, "l1_gain") as pg:
            gain = pg.sb("gain", [P, 2, 512])
            small = pg.sb("small", [P, 4, 32])
            move(core, "l1_gains", [(small[:, i, :], ins[f"L1_mix_{n}"].partition_broadcast(P))
                                    for i, n in enumerate(("kln_g", "vln_g", "kln_b", "vln_b"))])

            def spread(v):
                for i in range(4):
                    v.tensor_copy(gain[:, i // 2, 256 * (i % 2):256 * (i % 2) + 256].rearrange("p (h c) -> p h c", c=32),
                                  small[:, i:i + 1, :].to_broadcast([P, 8, 32]))
            on_vector(core, "l1_spread", spread)
            linear_mix(core, "l1_mix", xn, g, "copy", D, 32, 1.0 / N, ins["L1_mix_kv"], ins["L1_mix_WqT"], None,
                       kv_b=(ins["L1_mix_kv_b"],), q_b=ins["L1_mix_q_b"],
                       prepare=lambda kv: normalize(core, "l1_kvn", kv, kv, G=16, gain=gain))
        add_to(core, "l1_ret", g, xn)
        with Phase(core, "l1_h") as ph2:
            h = ph2.sb("h", [P, NT, D])
            w = weights(core, ph2, "w", D, ins["L1_mix_w1"])
            w2 = weights(core, ph2, "w2", D, ins["L1_mix_w2"])
            b1 = rowvec(core, ph2, "b1", D, ins["L1_mix_b1"], parts=P)
            b2 = rowvec(core, ph2, "b2", D, ins["L1_mix_b2"], parts=P)
            project(core, "l1_up", g, w, D, ("copy", h), bias=b1)
            on_scalar(core, "l1_gelu", lambda act: act.activation(h[:, :, :], h[:, :, :], ACT.Gelu))
            project(core, "l1_down", h, w2, D, ("add", x), bias=b2)
        add_to(core, "l1_bias", x, xn)


def layer1_ffn(core, x, xn):
    ins = core.ins
    normalize(core, "f1_norm", x, xn)
    with Phase(core, "f1") as ph:
        g = ph.sb("g", [P, NT, D])
        moe(core, "f1_moe", xn, g, 1, 8, 1024, ins["L1_ffn_gate_w"], ins["L1_ffn_gate_b"], ins["L1_ffn_w1"], ins["L1_ffn_b1"],
            ins["L1_ffn_w2"], ins["L1_ffn_b2"], ACT.Relu, "probs", capacity=-(-5 * N // 4 // 8) if (5 * N) % 32 == 0 else 5 * N // 32 + 1)
        with Phase(core, "f1_fix") as pf:
            m = pf.sb("m", [P, NT, D], I32)
            c = pf.sb("c", [P, 3])

            def finite(v):
                for i, val in enumerate((0.0, 1e4, -1e4)):
                    v.memset(c[:, i:i + 1], val)
                for i, (op, bound) in enumerate(((ALU.not_equal, None), (ALU.is_gt, 3.4028234663852886e38), (ALU.is_lt, -3.4028234663852886e38))):
                    if bound is None:
                        v.tensor_tensor(m[:, :, :], g[:, :, :], g[:, :, :], op)
                    else:
                        v.tensor_scalar(m[:, :, :], g[:, :, :], bound, None, op)
                    v.drain()
                    v.copy_predicated(g[:, :, :], m[:, :, :], c[:, i:i + 1].unsqueeze(1).to_broadcast([P, NT, D]))
                    v.drain()
            on_vector(core, "f1_finite", finite)
        add_to(core, "f1_add", x, g)


def layer2(core, x, xn):
    ins = core.ins
    normalize(core, "l2_norm", x, xn)
    table, score = core.dram("l2_table", (N, D)), core.dram("l2_score", (N, 1))
    with Phase(core, "l2") as ph:
        h = ph.sb("h", [P, NT, D])
        acc = ph.sb("acc", [P, NT, D + 1])
        sc = ph.sb("sc", [128, TE, 1])
        best = ph.sb("best", [P, NT, 2])
        hs = ph.sb("hs", [P, NT, 1])
        with Phase(core, "l2_w") as pw:
            w = weights(core, pw, "w", D, ins["L2_gnn_WnT"])
            b = rowvec(core, pw, "b", D, ins["L2_gnn_bn"], parts=P)
            project(core, "l2_rows", xn, w, D, ("copy", h), bias=b, table=table)
        with Phase(core, "l2_x") as px:
            tmp = px.sb("tmp", [P, NT, D])
            arow = rowvec(core, px, "a", D, ins["L2_gnn_attn"].rearrange("a b c -> (a b c)"), parts=P)

            def term(v):
                v.tensor_tensor(tmp[:, :, :], h[:, :, :], arow[:, :].unsqueeze(1).to_broadcast([P, NT, D]), ALU.mult)
                v.drain()
                v.tensor_reduce(hs[:, :, :], tmp[:, :, :], AX.X, ALU.add)
            on_vector(core, "l2_term", term)
        move(core, "l2_tabs", [(nodes(score), hs[:, :, :])])
        edge_scores(core, "l2_sc", 1, sc, best, score, core.e_src, ee=True)
        on_vector(core, "l2_best", lambda v: v.tensor_copy(hs[:, :, :], best[:, :, 0:1]))
        edge_sums(core, "l2_sum", 1, acc, table, core.e_src, sc, hs)

        def finish(v):
            v.tensor_scalar(hs[:, :, :], acc[:, :, D:D + 1], 1e-16, None, ALU.add)
            v.drain()
            v.reciprocal(hs[:, :, :], hs[:, :, :])
            v.drain()
            v.tensor_tensor(h[:, :, :], acc[:, :, 0:D], hs[:, :, :].to_broadcast([P, NT, D]), ALU.mult)
            v.drain()
            v.scalar_tensor_tensor(out=x[:, :, :], in0=h[:, :, :], scalar=0.0, in1=x[:, :, :], op0=ALU.max, op1=ALU.add)
        on_vector(core, "l2_finish", finish)
    linear_mix(core, "l2_mix", xn, x, "add", 128, 32, 32.0 ** -0.5, ins["L2_mix_kv"], ins["L2_mix_WqT"], ins["L2_mix_W_out"],
               out_b=ins["L2_mix_b_out"], prepare=lambda kv: column_softmax(core, "l2_soft", kv, 128), sums=True)


def layer2_ffn(core, x, xn):
    ins = core.ins
    normalize(core, "f2_norm", x, xn)
    with Phase(core, "f2") as ph:
        g = ph.sb("g", [P, NT, D])
        moe(core, "f2_moe", xn, g, 2, 16, 512, ins["L2_ffn_gate_w"], ins["L2_ffn_gate_b"], ins["L2_ffn_w1"], ins["L2_ffn_b1"],
            ins["L2_ffn_w2"], ins["L2_ffn_b2"], ACT.Relu, "top logits")
        add_to(core, "f2_add", g, xn)
        gain = ph.sb("gain", [P, 2, D])
        move(core, "f2_gains", [(gain[:, 0, :], ins["L2_ffn_gamma"].partition_broadcast(P)), (gain[:, 1, :], ins["L2_ffn_beta"].partition_broadcast(P))])
        normalize(core, "f2_out", g, g, gain=gain)
        add_to(core, "f2_add2", x, g)


def hgt(core, name, l, src, dst):
    ins = core.ins
    H, L = 32, 2
    tk, tm = core.dram(f"{name}_tk", (N, 2 * D)), core.dram(f"{name}_tm", (N, 2 * D))
    with Phase(core, name) as ph:
        alpha = ph.sb("alpha", [128, 2])
        wk = ph.sb("wk", [128, 2, 2 * D])
        wm = ph.sb("wm", [128, 2, 2 * D])
        with Phase(core, f"{name}_mats") as pm:
            m8 = pm.sb("m8", [128, 2, 128])
            tt = pm.sb("tt", [128, 2, 2, 2, 8])
            wt = pm.sb("wt", [128, 2, 2, D])
            pri = pm.sb("pri", [16, 4])
            pcol = pm.sb("pcol", [128, 4])
            hot = pm.sb("hot", [16, 128])
            bd = pm.sb("bd", [128, 2, 2, 2, 128])
            head_mask(core, f"{name}_m8a", m8[:, 0, :], 8, 8.0 ** -0.5)
            head_mask(core, f"{name}_m8b", m8[:, 1, :], 8, 1.0)
            move(core, f"{name}_in", [(alpha[:, 0:1], ins["L3_gnn_skip"][l:l + 1].partition_broadcast(128))]
                 + [(pri[:, 2 * c:2 * c + 2], ins["L3_gnn_pri"][l, 16 * c:16 * c + 16, :]) for c in range(2)]
                 + [(tt[:, i, t, c, :], ins[n][l, t, 128 * c:128 * c + 128, :]) for i, n in enumerate(("L3_gnn_Watt", "L3_gnn_Wmsg"))
                    for t in range(2) for c in range(2)]
                 + [(wt[:, i, :, :], ins[n][l].rearrange("(c p) i -> p c i", p=128)) for i, n in enumerate(("L3_gnn_WkT", "L3_gnn_WvT"))])
            with Phase(core, f"{name}_hot") as p2:
                block = p2.block()

                @block.gpsimd
                def _(gp):
                    gp.affine_select(out=hot[:, :].rearrange("h (b w) -> h b w", w=8), in_=core.ones[0:16, :].rearrange("h (b w) -> h b w", w=8),
                                     compare_op=ALU.is_equal, fill=0.0, base=0, pattern=[[-1, 16], [0, 8]], channel_multiplier=1)
                    gp.drain()
            on_scalar(core, f"{name}_alpha", lambda act: act.activation(alpha[:, 0:1], alpha[:, 0:1], ACT.Sigmoid))
            chain(core, f"{name}_pcol", [(pcol[:, :], None, [(hot[:, :], pri[:, :])], None)])

            def spread(v):
                v.tensor_scalar(alpha[:, 1:2], alpha[:, 0:1], -1.0, 1.0, ALU.mult, ALU.add)
                for i in range(2):
                    for t in range(2):
                        for c in range(2):
                            v.tensor_tensor(bd[:, i, t, c, :].rearrange("p (b f) -> p b f", f=8), m8[:, i, :].rearrange("p (b f) -> p b f", f=8),
                                            tt[:, i, t, c, :].unsqueeze(1).to_broadcast([128, 16, 8]), ALU.mult)
                v.drain()
                for t in range(2):
                    for c in range(2):
                        v.tensor_scalar(bd[:, 0, t, c, :], bd[:, 0, t, c, :], pcol[:, 2 * c + t:2 * c + t + 1], None, ALU.mult)
            on_vector(core, f"{name}_spread", spread)
            chain(core, f"{name}_prod", [(w[:, r, D * t + 128 * c:D * t + 128 * c + 128], None, [(wt[:, i, c, 128 * r:128 * r + 128], bd[:, i, t, c, :])], None)
                                         for i, w in enumerate((wk, wm)) for t in range(2) for c in range(2) for r in range(2)])
        for n, w, tab in (("k", wk, tk), ("m", wm, tm)):
            project(core, f"{name}_{n}p", src, w, 2 * D, ("pass", None), table=tab)
        typed = [t.rearrange("n (t c) -> (n t) c", t=2) for t in (tk, tm)]
        with Phase(core, f"{name}_edges") as pe:
            sc = pe.sb("sc", [128, TE, H])
            best = pe.sb("best", [P, NT, H + 1])
            with Phase(core, f"{name}_q") as pq:
                q = pq.sb("q", [P, NT, D])
                with Phase(core, f"{name}_qw") as pw:
                    w = weights(core, pw, "w", D, ins["L3_gnn_Wq"][l])
                    project(core, f"{name}_qp", src, w, D, ("copy", q))
                edge_scores(core, f"{name}_sc", H, sc, best, typed[0], core.e_srct, q=q)
            acc = pe.sb("acc", [P, NT, D + H])
            edge_sums(core, f"{name}_sum", H, acc, typed[1], core.e_srct, sc, best[:, :, 0:H])

            def finish(v):
                v.tensor_scalar(best[:, :, 0:H], acc[:, :, D:D + H], 1e-30, None, ALU.max)
                v.drain()
                v.reciprocal(best[:, :, 0:H], best[:, :, 0:H])
                v.drain()
                with v.Fori(0, NT) as t:
                    a = acc[:, bass.ds(t, 1), 0:D].rearrange("p o (h c) -> p (o h) c", h=H)
                    v.tensor_tensor(a, a, best[:, bass.ds(t, 1), 0:H].rearrange("p o h -> p (o h)").unsqueeze(2).to_broadcast([P, H, D // H]), ALU.mult)
                v.drain()
                v.tensor_scalar(src[:, :, :], src[:, :, :], alpha[0:P, 1:2], None, ALU.mult)
            on_vector(core, f"{name}_finish", finish)
            with Phase(core, f"{name}_wa") as pw:
                w = weights(core, pw, "w", D, ins["L3_gnn_Wa"][l])
                on_vector(core, f"{name}_scale", lambda v: v.tensor_scalar(w[:, :, :], w[:, :, :], alpha[:, 0:1], None, ALU.mult))
                project(core, f"{name}_out", acc, w, D, ("add", src))
            on_vector(core, f"{name}_to", lambda v: v.tensor_copy(dst[:, :, :], src[:, :, :]))


def layer3(core, x, xn):
    ins = core.ins
    normalize(core, "l3_norm", x, xn)
    with Phase(core, "l3") as ph:
        kept = core.dram("l3_x", (N, D))
        move(core, "l3_keep", [(nodes(kept), x[:, :, :])])
        on_vector(core, "l3_copy", lambda v: v.tensor_copy(x[:, :, :], xn[:, :, :]))
        for l in range(2):
            hgt(core, f"l3_hgt{l}", l, x, x)
        g = ph.sb("g", [P, NT, D])
        move(core, "l3_back", [(g[:, :, :], nodes(kept))])
        add_to(core, "l3_add", x, g)
    linear_mix(core, "l3_mix", xn, x, "add", 512, 64, 1.0 / N, ins["L3_mix_kv"], ins["L3_mix_Wq"], ins["L3_mix_WoutT"],
               out_b=ins["L3_mix_b_out"], prepare=lambda kv: normalize(core, "l3_kvn", kv, kv, G=16))


def layer3_ffn(core, x, xn):
    ins = core.ins
    normalize(core, "f3_norm", x, xn)
    with Phase(core, "f3") as ph:
        g = ph.sb("g", [P, NT, D])
        moe(core, "f3_moe", xn, g, 2, 8, 256, ins["L3_ffn_routerT"], None, ins["L3_ffn_w1"], ins["L3_ffn_b1"],
            ins["L3_ffn_w2"], ins["L3_ffn_b2"], ACT.Gelu, "over their sum")
        add_to(core, "f3_add", x, g, xn)


LAYERS = [layer0, layer0_ffn, layer1, layer1_ffn, layer2, layer2_ffn, layer3, layer3_ffn]


def build(nc, ins, out, layers=LAYERS, x_in=None):
    core = Core(nc, ins, out)
    with Phase(core, "keep") as keep:
        x = keep.sb("x", [P, NT, D])
        xn = keep.sb("xn", [P, NT, D])
        constants(core, keep)
        move(core, "x_in", [(x[:, :, :], nodes(ins["x"]))])
        sort_edges(core, keep)
        for layer in layers:
            layer(core, x, xn)
        move(core, "x_out", [(nodes(out), x[:, :, :])])


def lay_out(i):
    import numpy as np

    a = {k: np.asarray(v) for k, v in i.items()}
    t = lambda n: np.ascontiguousarray(a[n].T)
    put = {k: a[k] for k in (
        "x", "src", "dst", "edge_attr_128", "edge_type_2", "L0_gnn_W1", "L0_gnn_att_src1", "L0_gnn_att_dst1", "L0_gnn_b1",
        "L0_gnn_W2", "L0_gnn_att_src2", "L0_gnn_att_dst2", "L0_gnn_b2", "L0_mix_Wq", "L0_mix_bq", "L0_mix_bk", "L0_mix_bv", "L0_mix_bfc",
        "L0_ffn_gate_w", "L0_ffn_gate_b", "L0_ffn_b2", "L1_mix_kln_g", "L1_mix_kln_b", "L1_mix_vln_g", "L1_mix_vln_b",
        "L1_mix_w1", "L1_mix_b1", "L1_mix_w2", "L1_mix_b2", "L1_ffn_gate_w", "L1_ffn_gate_b", "L1_ffn_b2", "L2_gnn_bn", "L2_gnn_We",
        "L2_gnn_be", "L2_gnn_attn", "L2_mix_W_out", "L2_mix_b_out", "L2_ffn_gate_w", "L2_ffn_gate_b", "L2_ffn_b2", "L2_ffn_gamma",
        "L2_ffn_beta", "L3_gnn_Wq", "L3_gnn_Wa", "L3_gnn_pri", "L3_gnn_skip", "L3_mix_b_out", "L3_ffn_b2")}
    put["L0_mix_kv"] = np.concatenate([t("L0_mix_Wk"), t("L0_mix_Wv")], 1)
    put["L0_mix_WfcT"] = t("L0_mix_Wfc")
    put["L1_gnn_W1T"], put["L1_gnn_W2T"] = t("L1_gnn_W1"), t("L1_gnn_W2")
    w = a["L1_mix_w_qkv"].reshape(256, 8, 3, 32).transpose(0, 2, 1, 3).reshape(256, 768)
    b = a["L1_mix_b_qkv"].reshape(8, 3, 32).transpose(1, 0, 2).reshape(768)
    put["L1_mix_kv"], put["L1_mix_WqT"] = np.ascontiguousarray(w[:, 256:]), np.ascontiguousarray(w[:, :256].T)
    put["L1_mix_kv_b"], put["L1_mix_q_b"] = b[256:].copy(), b[:256].copy()
    put["L2_gnn_WnT"] = t("L2_gnn_Wn")
    put["L2_mix_kv"] = np.ascontiguousarray(a["L2_mix_W_qkv"][:, 128:])
    put["L2_mix_WqT"] = np.ascontiguousarray(a["L2_mix_W_qkv"][:, :128].T)
    for n in ("Wk", "Wv"):
        put[f"L3_gnn_{n}T"] = np.ascontiguousarray(a[f"L3_gnn_{n}"].transpose(0, 2, 1))
    for n in ("Watt", "Wmsg"):
        put[f"L3_gnn_{n}"] = np.ascontiguousarray(a[f"L3_gnn_{n}"].transpose(0, 2, 1, 3, 4).reshape(2, 2, 256, 8))
    put["L3_mix_Wq"] = np.ascontiguousarray(a["L3_mix_w_qkv"][:512])
    put["L3_mix_kv"] = np.ascontiguousarray(a["L3_mix_w_qkv"][512:].T)
    put["L3_mix_WoutT"] = t("L3_mix_w_out")
    put["L3_ffn_routerT"] = t("L3_ffn_router_w")
    for n, u, d in (("L0_ffn", "W1", "W2"), ("L1_ffn", "w1", "w2"), ("L2_ffn", "w1", "w2"), ("L3_ffn", "w1", "w2")):
        for k, w in ((u, a[f"{n}_{u}"]), (d, a[f"{n}_{d}"])):
            e, r, c = w.shape
            put[f"{n}_{k}"] = np.ascontiguousarray(w.reshape(e, r // 128, 128, c).transpose(0, 2, 1, 3))
        b = a[f"{n}_b1"]
        put[f"{n}_b1"] = np.ascontiguousarray(b.reshape(b.shape[0], -1, 128).transpose(0, 2, 1))
    return put


def kernel(**inputs):
    import concourse.bacc as _bacc
    from concourse.bass_utils import run_bass_kernel_spmd as _run

    nc = _bacc.Bacc("TRN2", target_bir_lowering=False, num_devices=1)
    arrays, ins = {}, {}
    for name, a in lay_out(inputs).items():
        arrays[f"in_{name}"] = a
        ins[name] = nc.dram_tensor(f"in_{name}", a.shape, mybir.dt.from_np(a.dtype), kind="ExternalInput").ap()
    out = nc.dram_tensor("out", (N, D), F32, kind="ExternalOutput").ap()
    build(nc, ins, out)
    return _run(nc, [arrays], core_ids=[0]).results[0]["out"]
```
